# Optimizing a Trainium2 kernel written in Bass

```python
import numpy as np
import jax
import jax.numpy as jnp

def _softmax(x, axis=-1):
    return jax.nn.softmax(x, axis=axis)

def _gelu(x):
    return jax.nn.gelu(x, approximate=True)

def _silu(x):
    return jax.nn.silu(x)

def _sigmoid(x):
    return jax.nn.sigmoid(x)

def _layernorm(x, axis=-1, eps=1e-05):
    m = jnp.mean(x, axis=axis, keepdims=True)
    v = jnp.var(x, axis=axis, keepdims=True)
    return (x - m) / jnp.sqrt(v + eps)

def _scatter_add(tgt, idx, src, axis=0):
    return tgt.at[idx].add(src)

def _segment_sum(src, seg, n):
    return jax.ops.segment_sum(src, seg, n)
kernel_name = 'mk_decoder_postln_d1_seqx_r4_ae8dbb'

def setup_inputs(seed: int=0):
    np.random.seed(seed)
    _w = jnp.asarray

    def _rec_inputs():
        import jax
        import jax.numpy as jnp
        _rk = jax.random.key(seed)
        x = -0.0002928 + 1 * jax.random.normal(jax.random.fold_in(_rk, 1), (32, 128, 256), jnp.float32)
        _lenS = 128 - jax.random.randint(jax.random.fold_in(_rk, 7), (32,), 0, max(1, 128 // 4) + 1, jnp.int32)
        _lenS2 = 128 - jax.random.randint(jax.random.fold_in(_rk, 8), (32,), 0, max(1, 128 // 4) + 1, jnp.int32)
        _ctx_1024P = jax.random.normal(jax.random.fold_in(_rk, 11), (32, 16, 256), jnp.float32)
        _ctx_1024c = jax.random.dirichlet(jax.random.fold_in(_rk, 511), 0.3 * jnp.ones((16,), jnp.float32), (32, 128))
        _ctx_1024t = jnp.einsum('bsk,bkd->bsd', _ctx_1024c, _ctx_1024P)
        _ctx_1024t = _ctx_1024t * jax.lax.rsqrt(jnp.mean(jnp.square(_ctx_1024t)) + 1e-12) * 0.953939
        ctx_1024 = -1.39393e-06 + 0.999914 * (_ctx_1024t + 0.3 * jax.random.normal(jax.random.fold_in(_rk, 611), (32, 128, 256), jnp.float32))
        return (x, ctx_1024)
    x, ctx_1024 = _rec_inputs()

    def _L0_attn_setup():
        import jax, jax.numpy as jnp
        import numpy as np
        B, N, DIM = (4, 2048, 256)
        H, DH, W = (16, 64, 128)
        INNER = H * DH
        key = jax.random.key(seed)
        k0, k1, k2, k3 = jax.random.split(key, 4)
        s = 0.02
        return {'x': jax.random.normal(k0, (B, N, DIM), jnp.float32), 'wq': jax.random.normal(k1, (DIM, INNER), jnp.float32) * s, 'wkv': jax.random.normal(k2, (DIM, 2 * INNER), jnp.float32) * s, 'wo': jax.random.normal(k3, (INNER, DIM), jnp.float32) * s, 'bo': jnp.zeros((DIM,), jnp.float32)}
    _L0_attn_all = _L0_attn_setup()
    _L0_attn_in = {k: v for k, v in _L0_attn_all.items() if k in ('wq', 'wkv', 'wo', 'bo')}
    del _L0_attn_all

    def _L0_xattn_setup():
        import math
        import jax, jax.numpy as jnp
        import numpy as np
        B, S, H, NH = (2, 512, 256, 4)
        DH = H // NH

        def _mlstm_parallel(qh, kh, vh, ig, fg, eps=1e-06):
            b, nh, s, dh = qh.shape
            log_f = jax.nn.log_sigmoid(fg)
            pcs = jnp.pad(jnp.cumsum(log_f, axis=-1), ((0, 0), (0, 0), (1, 0)))
            mat = pcs[..., :, None] - pcs[..., None, :]
            ltr = jnp.tril(jnp.ones((s, s), dtype=bool))
            log_fg_matrix = jnp.where(ltr, mat[..., 1:, 1:], -jnp.inf)
            log_D = log_fg_matrix + ig[..., None, :]
            max_log_D = jnp.max(log_D, axis=-1, keepdims=True)
            D = jnp.exp(log_D - max_log_D)
            qk = jnp.einsum('bhsd,bhtd->bhst', qh, kh) / math.sqrt(dh)
            C = qk * D
            normalizer = jnp.maximum(jnp.abs(C.sum(axis=-1, keepdims=True)), jnp.exp(-max_log_D))
            Cn = C / (normalizer + eps)
            return jnp.einsum('bhst,bhtd->bhsd', Cn, vh)
        key = jax.random.key(seed)
        ks = jax.random.split(key, 8)
        gate_std = 1.0 / math.sqrt(3 * H)
        return {'q': jax.random.normal(ks[0], (B, S, H), jnp.float32), 'k': jax.random.normal(ks[1], (B, S, H), jnp.float32), 'v': jax.random.normal(ks[2], (B, S, H), jnp.float32), 'w_igate': jax.random.normal(ks[3], (NH, 3 * H), jnp.float32) * gate_std, 'b_igate': jax.random.normal(ks[4], (NH,), jnp.float32) * 0.1, 'w_fgate': jax.random.normal(ks[5], (NH, 3 * H), jnp.float32) * gate_std, 'b_fgate': jnp.linspace(3.4, 6.0, NH, dtype=jnp.float32), 'ln_weight': jnp.zeros((H,), jnp.float32)}
    _L0_xattn_all = _L0_xattn_setup()
    _L0_xattn_in = {k: v for k, v in _L0_xattn_all.items() if k in ('w_igate', 'b_igate', 'w_fgate', 'b_fgate', 'ln_weight')}
    del _L0_xattn_all

    def _L0_ffn_setup():
        import jax, jax.numpy as jnp
        import numpy as np
        ALPHA = 1.702
        LIMIT = 7.0
        K = 2
        key = jax.random.key(seed)
        ks = jax.random.split(key, 4)
        B, S, H, E, I = (1, 256, 256, 8, 256)
        return {'hidden_states': jax.random.normal(ks[0], (B, S, H), jnp.float32), 'router_weight': jax.random.normal(ks[1], (E, H), jnp.float32), 'router_bias': jnp.zeros((E,), jnp.float32), 'gate_up_proj': jax.random.normal(ks[2], (E, H, 2 * I), jnp.float32) * 0.02, 'gate_up_bias': jnp.zeros((E, 2 * I), jnp.float32), 'down_proj': jax.random.normal(ks[3], (E, I, H), jnp.float32) * 0.02, 'down_bias': jnp.zeros((E, H), jnp.float32)}
    _L0_ffn_all = _L0_ffn_setup()
    _L0_ffn_in = {k: v for k, v in _L0_ffn_all.items() if k in ('router_weight', 'router_bias', 'gate_up_proj', 'gate_up_bias', 'down_proj', 'down_bias')}
    del _L0_ffn_all
    return {'x': x, 'ctx_1024': ctx_1024, 'L0_attn_wq': _L0_attn_in['wq'], 'L0_attn_wkv': _L0_attn_in['wkv'], 'L0_attn_wo': _L0_attn_in['wo'], 'L0_attn_bo': _L0_attn_in['bo'], 'L0_xattn_w_igate': _L0_xattn_in['w_igate'], 'L0_xattn_b_igate': _L0_xattn_in['b_igate'], 'L0_xattn_w_fgate': _L0_xattn_in['w_fgate'], 'L0_xattn_b_fgate': _L0_xattn_in['b_fgate'], 'L0_xattn_ln_weight': _L0_xattn_in['ln_weight'], 'L0_ffn_router_weight': _L0_ffn_in['router_weight'], 'L0_ffn_router_bias': _L0_ffn_in['router_bias'], 'L0_ffn_gate_up_proj': _L0_ffn_in['gate_up_proj'], 'L0_ffn_gate_up_bias': _L0_ffn_in['gate_up_bias'], 'L0_ffn_down_proj': _L0_ffn_in['down_proj'], 'L0_ffn_down_bias': _L0_ffn_in['down_bias']}

def reference(x, ctx_1024, L0_attn_wq, L0_attn_wkv, L0_attn_wo, L0_attn_bo, L0_xattn_w_igate, L0_xattn_b_igate, L0_xattn_w_fgate, L0_xattn_b_fgate, L0_xattn_ln_weight, L0_ffn_router_weight, L0_ffn_router_bias, L0_ffn_gate_up_proj, L0_ffn_gate_up_bias, L0_ffn_down_proj, L0_ffn_down_bias):
    import jax
    import jax.numpy as jnp

    def _L0_attn_ref(x, wq, wkv, wo, bo):
        import jax, jax.numpy as jnp
        import numpy as np
        B, N, DIM = (4, 2048, 256)
        H, DH, W = (16, 64, 128)
        INNER = H * DH
        b, n, _ = x.shape
        h, dh, w = (H, DH, W)
        scale = dh ** (-0.5)
        q = x @ wq
        k, v = jnp.split(x @ wkv, 2, axis=-1)

        def to_windows(t):
            t = t.reshape(b, n, h, dh).transpose(0, 2, 1, 3)
            return t.reshape(b * h, n // w, w, dh)
        qw, kw, vw = map(to_windows, (q, k, v))

        def add_prev_window(t):
            tp = jnp.pad(t, ((0, 0), (1, 0), (0, 0), (0, 0)))
            return jnp.concatenate([tp[:, :-1], tp[:, 1:]], axis=2)
        kw, vw = (add_prev_window(kw), add_prev_window(vw))
        sim = jnp.einsum('bwid,bwjd->bwij', qw, kw) * scale
        i, j = (w, 2 * w)
        causal = jnp.triu(jnp.ones((i, j), bool), j - i + 1)
        neg = -jnp.finfo(sim.dtype).max
        sim = jnp.where(causal, neg, sim)
        attn = jax.nn.softmax(sim, axis=-1)
        out = jnp.einsum('bwij,bwjd->bwid', attn, vw)
        out = out.reshape(b, h, n, dh).transpose(0, 2, 1, 3).reshape(b, n, h * dh)
        return out @ wo + bo

    def _L0_xattn_ref(q, k, v, w_igate, b_igate, w_fgate, b_fgate, ln_weight):
        import math
        import jax, jax.numpy as jnp
        import numpy as np
        B, S, H, NH = (2, 512, 256, 4)
        DH = H // NH

        def _mlstm_parallel(qh, kh, vh, ig, fg, eps=1e-06):
            b, nh, s, dh = qh.shape
            log_f = jax.nn.log_sigmoid(fg)
            pcs = jnp.pad(jnp.cumsum(log_f, axis=-1), ((0, 0), (0, 0), (1, 0)))
            mat = pcs[..., :, None] - pcs[..., None, :]
            ltr = jnp.tril(jnp.ones((s, s), dtype=bool))
            log_fg_matrix = jnp.where(ltr, mat[..., 1:, 1:], -jnp.inf)
            log_D = log_fg_matrix + ig[..., None, :]
            max_log_D = jnp.max(log_D, axis=-1, keepdims=True)
            D = jnp.exp(log_D - max_log_D)
            qk = jnp.einsum('bhsd,bhtd->bhst', qh, kh) / math.sqrt(dh)
            C = qk * D
            normalizer = jnp.maximum(jnp.abs(C.sum(axis=-1, keepdims=True)), jnp.exp(-max_log_D))
            Cn = C / (normalizer + eps)
            return jnp.einsum('bhst,bhtd->bhsd', Cn, vh)
        b, s, h = q.shape
        nh = b_igate.shape[0]
        dh = h // nh
        gin = jnp.concatenate([q, k, v], axis=-1)
        ig = jnp.einsum('bsd,hd->bhs', gin, w_igate) + b_igate[None, :, None]
        fg = jnp.einsum('bsd,hd->bhs', gin, w_fgate) + b_fgate[None, :, None]
        qh = q.reshape(b, s, nh, dh).transpose(0, 2, 1, 3)
        kh = k.reshape(b, s, nh, dh).transpose(0, 2, 1, 3)
        vh = v.reshape(b, s, nh, dh).transpose(0, 2, 1, 3)
        hst = _mlstm_parallel(qh, kh, vh, ig, fg)
        mean = hst.mean(axis=-1, keepdims=True)
        var = hst.var(axis=-1, keepdims=True)
        hn = (hst - mean) / jnp.sqrt(var + 1e-05)
        scale = (1.0 + ln_weight).reshape(nh, dh)
        hn = hn * scale[None, :, None, :]
        return hn.transpose(0, 2, 1, 3).reshape(b, s, h)

    def _L0_ffn_ref(hidden_states, router_weight, router_bias, gate_up_proj, gate_up_bias, down_proj, down_bias):
        import jax, jax.numpy as jnp
        import numpy as np
        ALPHA = 1.702
        LIMIT = 7.0
        K = 2
        B, S, H = hidden_states.shape
        E = router_weight.shape[0]
        I = down_proj.shape[1]
        T = B * S
        flat = hidden_states.reshape(T, H)
        logits = flat @ router_weight.T + router_bias
        scores = jax.nn.softmax(logits, axis=-1)
        topk_vals, topk_idx = jax.lax.top_k(scores, K)
        w = jnp.zeros((T, E), scores.dtype).at[jnp.arange(T)[:, None], topk_idx].set(topk_vals)
        gu = jnp.einsum('th,ehf->tef', flat, gate_up_proj) + gate_up_bias
        gate = jnp.minimum(gu[..., :I], LIMIT)
        up = jnp.clip(gu[..., I:], -LIMIT, LIMIT)
        glu = gate * jax.nn.sigmoid(gate * ALPHA)
        act = (up + 1.0) * glu
        down = jnp.einsum('tei,eih->teh', act, down_proj) + down_bias
        out = jnp.einsum('teh,te->th', down, w)
        return out.reshape(B, S, H)
    x = _layernorm(x + _L0_attn_ref(x, L0_attn_wq, L0_attn_wkv, L0_attn_wo, L0_attn_bo), axis=-1)
    x = _layernorm(x + _L0_xattn_ref(x, ctx_1024, ctx_1024, L0_xattn_w_igate, L0_xattn_b_igate, L0_xattn_w_fgate, L0_xattn_b_fgate, L0_xattn_ln_weight), axis=-1)
    x = _layernorm(x + _L0_ffn_ref(x, L0_ffn_router_weight, L0_ffn_router_bias, L0_ffn_gate_up_proj, L0_ffn_gate_up_bias, L0_ffn_down_proj, L0_ffn_down_bias), axis=-1)
    return x

_drawn_inputs = setup_inputs


def setup_inputs(seed=0):
    import zlib

    import numpy as np

    out = dict(_drawn_inputs(seed))
    spreads = {'L0_attn_bo': (0.0, 0.363),
     'L0_xattn_ln_weight': (0.0, 0.1),
     'L0_ffn_router_bias': (0.0, 2.0),
     'L0_ffn_gate_up_bias': (0.0, 0.438),
     'L0_ffn_down_bias': (0.0, 0.1)}
    factors = {'L0_attn_wq': 8.0, 'L0_attn_wkv': 5.974, 'L0_attn_wo': 6.368, 'L0_xattn_b_igate': 64.0}
    for name, (base, spread) in spreads.items():
        noise = np.random.default_rng([zlib.crc32(name.encode()), seed]).standard_normal(out[name].shape)
        drawn = base * np.exp(spread * noise) if base else spread * noise
        out[name] = jnp.asarray(drawn.astype(out[name].dtype))
    for name, factor in factors.items():
        out[name] = (out[name] * factor).astype(out[name].dtype)
    return out
```

```python
from contextlib import ExitStack

import concourse.bass as bass
from concourse import mybir

F32 = mybir.dt.float32
F32R = mybir.dt.float32r
BF16 = mybir.dt.bfloat16
I32 = mybir.dt.int32
ALU = mybir.AluOpType
ACT = mybir.ActivationFunctionType
AX = mybir.AxisListType

P = 128
NSEQ = 32
DM = 256
KC = DM // P
GS = 4
GROUPS = NSEQ // GS
GT = GS * P

HEADS = 16
DH = 64
INNER = HEADS * DH
QH = 4
QUADS = HEADS // QH
UNITS = QUADS * GS
QF = QH * DH
OC = QF // P
BLOCKS = 2 * OC
AHEAD = BLOCKS + 1
SWITCH = UNITS - AHEAD
ATT_SCALE = DH**-0.5
MASKED = -3.0e38
LN_EPS = 1e-5
RSQRT_SEED = 0x5F3759DF
NEWTON = 3
NEWTON_OPS = 4 * NEWTON

MH = 4
MD = DM // MH
QK_SCALE = MD**-0.5
NORM_EPS = 1e-6
PAIRS = GS * MH
CHOICES = GS * 8

E = 8
FI = 256
FB = FI // P
LIMIT = 7.0
ALPHA = 1.702


def stand_apart(eng, passed):
    eng.sem_inc(passed, 1)


def newton_rsqrt(pool, done, base, y, half_v, tmp, three_halves):
    k = 0

    def step(ins):
        nonlocal k
        k += 1
        ins.then_inc(done, 1)
        pool.wait_ge(done, base + k)

    for _ in range(NEWTON):
        step(pool.tensor_tensor(tmp, y, y, ALU.mult))
        step(pool.tensor_tensor(tmp, tmp, half_v, ALU.mult))
        step(pool.tensor_tensor(tmp, three_halves, tmp, ALU.subtract))
        step(pool.tensor_tensor(y, y, tmp, ALU.mult))


def attention(nc, y1, x, wq, wkv, wo, bo):
    with ExitStack() as ctx:
        def sb(name, shape, dt=F32):
            return ctx.enter_context(nc.sbuf_tensor(name, shape, dt))

        def bank(name):
            return ctx.enter_context(nc.psum_tensor(name, [P, 512], F32))

        def sem(name):
            return ctx.enter_context(nc.semaphore(name))

        w_raw = sb("w_raw", [P, KC, 3 * INNER])
        w_hi = sb("w_hi", [P, KC, 3 * INNER], F32R)
        w_lo = sb("w_lo", [P, KC, 3 * INNER], F32R)
        wo_raw = w_raw[:, 0, 0:8 * DM].rearrange("p (c n) -> p c n", c=8)
        wo_hi = sb("wo_hi", [P, INNER // P, DM], F32R)
        wo_lo = sb("wo_lo", [P, INNER // P, DM], F32R)
        bo_row = sb("bo_row", [1, DM])
        bo_all = sb("bo_all", [P, DM])
        ident = sb("ident", [P, P])
        mask = sb("mask", [P, P])
        x_in = sb("x_in", [P, GS, DM])
        x_res = sb("x_res", [P, GS, DM])
        xT_hi = sb("xT_hi", [P, KC, GT], F32R)
        xT_lo = sb("xT_lo", [P, KC, GT], F32R)
        qkT = sb("qkT", [P, 2, BLOCKS, GT])
        v_one = sb("v_one", [P, 2, GS, QH, DH + 1])
        probs = sb("probs", [P, 2, QH, P])
        probsT = sb("probsT", [P, QH, P])
        row_max = sb("row_max", [P, 2, QH])
        neg_max = sb("neg_max", [P, 2, QH])
        zero_exp = sb("zero_exp", [P, 2, QH])
        denom = sb("denom", [P, QH])
        inv_denom = sb("inv_denom", [P, QH])
        o_tok = sb("o_tok", [P, QH, DH])
        oT_hi = sb("oT_hi", [P, OC, P], F32R)
        oT_lo = sb("oT_lo", [P, OC, P], F32R)
        z = sb("z", [P, GS, DM])
        y_out = sb("y_out", [P, GS, DM])
        stats = sb("stats", [P, GS, 6])
        mean_var = sb("mean_var", [P, GS, 2])
        var_eps = sb("var_eps", [P, GS])
        half_bits = sb("half_bits", [P, GS], I32)
        rstd = sb("rstd", [P, GS])
        half_var = sb("half_var", [P, GS])
        newton_tmp = sb("newton_tmp", [P, GS])
        three_halves = sb("three_halves", [P, GS])

        acc = [bank(f"acc{i}") for i in range(2)]
        score_bank = [bank(f"score_bank{i}") for i in range(2)]
        pT_bank = bank("pT_bank")
        av_bank = bank("av_bank")
        qk_bank = bank("qk_bank")
        v_bank = bank("v_bank")
        oT_bank = v_bank[:, QF:2 * QF]
        av = av_bank[:, 0:QH * (DH + 1)].rearrange("p (h d) -> p h d", h=QH)

        w_loaded = [sem(f"w_loaded{i}") for i in range(QUADS)]
        wo_loaded = sem("wo_loaded")
        bo_loaded = sem("bo_loaded")
        x_loaded = sem("x_loaded")
        xres_loaded = sem("xres_loaded")
        consts = sem("consts")
        w_hi_ready = sem("w_hi_ready")
        w_ready = sem("w_ready")
        wo_hi_ready = sem("wo_hi_ready")
        wo_ready = sem("wo_ready")
        bo_ready = sem("bo_ready")
        xT_done = sem("xT_done")
        xT_hi_ready = sem("xT_hi_ready")
        xT_lo_ready = sem("xT_lo_ready")
        block_done = sem("block_done")
        block_out = sem("block_out")
        v_done = sem("v_done")
        v_out = sem("v_out")
        scores_done = sem("scores_done")
        masked_done = sem("masked_done")
        neg_max_ready = sem("neg_max_ready")
        exp_done = sem("exp_done")
        zero_exp_ready = sem("zero_exp_ready")
        pT_done = sem("pT_done")
        pT_out = sem("pT_out")
        av_done = sem("av_done")
        denom_ready = sem("denom_ready")
        inv_ready = sem("inv_ready")
        o_ready = sem("o_ready")
        oT_done = sem("oT_done")
        oT_hi_ready = sem("oT_hi_ready")
        oT_lo_ready = sem("oT_lo_ready")
        wo_done = sem("wo_done")
        xres_ready = sem("xres_ready")
        z_ready = sem("z_ready")
        stats_ready = sem("stats_ready")
        mean_var_ready = sem("mean_var_ready")
        var_eps_ready = sem("var_eps_ready")
        half_ready = sem("half_ready")
        seed_ready = sem("seed_ready")
        newton_done = sem("newton_done")
        y_done = sem("y_done")
        y_stored = sem("y_stored")
        half_var_ready = sem("half_var_ready")
        dve_passed = sem("dve_passed")
        pool_passed = sem("pool_passed")

        blocks = ctx.enter_context(ExitStack())
        block = blocks.enter_context(nc.Block())

        def x_group(j):
            return x[bass.ds(j * GS, GS)].rearrange("b t d -> t b d")

        w_view = [(wq, 0, 0), (wkv, 0, INNER), (wkv, INNER, 2 * INNER)]

        def w_cols(q):
            return [slice(base + q * QF, base + (q + 1) * QF) for _, _, base in w_view]

        @block.sync
        def _(sp):
            sp.dma_start(x_in[:], x_group(0)).then_inc(x_loaded, 16)
            for q in range(QUADS):
                for src, col, base in w_view:
                    sp.dma_start(w_raw[:, :, base + q * QF:base + (q + 1) * QF],
                                 src[:, col + q * QF:col + (q + 1) * QF]
                                 .rearrange("(c p) n -> p c n", p=P)).then_inc(w_loaded[q], 16)
            sp.dma_start(bo_row[:], bo.rearrange("(a n) -> a n", a=1)).then_inc(bo_loaded, 16)
            sp.dma_start(x_res[:], x_group(0)).then_inc(xres_loaded, 16)
            sp.wait_ge(w_ready, 3 * QUADS)
            sp.dma_start(wo_raw, wo.rearrange("(c p) n -> p c n", p=P)).then_inc(wo_loaded, 16)

            def group(g):
                sp.wait_ge(xT_done, g + 1)
                sp.dma_start(x_in[:], x_group(g + 1)).then_inc(x_loaded, 16)
                sp.wait_ge(z_ready, 2 * (g + 1))
                sp.dma_start(x_res[:], x_group(g + 1)).then_inc(xres_loaded, 16)

            def store(j):
                sp.wait_ge(y_done, GS * (j + 1))
                sp.dma_start(y1[bass.ds(j * GS, GS)].rearrange("b t d -> t b d"), y_out[:]).then_inc(y_stored, 16)

            with sp.Fori(0, GROUPS - 1) as g:
                group(g)
                store(g)
            store(GROUPS - 1)
            sp.wait_ge(y_stored, 16 * GROUPS)

        @block.gpsimd
        def _(pool):
            pool.memset(ident[:], 0.0).then_inc(consts, 1)
            pool.memset(mask[:], 0.0).then_inc(consts, 1)
            pool.memset(three_halves[:], 1.5).then_inc(consts, 1)
            pool.memset(v_one[:, :, :, :, DH:DH + 1].rearrange("p a s h d -> p (a s h d)"), 1.0).then_inc(consts, 1)
            pool.wait_ge(consts, 4)
            pool.affine_select(out=ident[:], in_=ident[:], compare_op=ALU.not_equal, fill=1.0, base=0,
                               pattern=[[-1, P]], channel_multiplier=1).then_inc(consts, 1)
            pool.affine_select(out=mask[:], in_=mask[:], compare_op=ALU.is_ge, fill=MASKED, base=0,
                               pattern=[[-1, P]], channel_multiplier=1).then_inc(consts, 1)
            pool.wait_ge(bo_loaded, 16)
            pool.partition_broadcast(bo_all[:], bo_row[:]).then_inc(bo_ready, 1)
            pool.wait_ge(bo_ready, 1)

            def add_bias(j):
                pool.wait_ge(xres_loaded, 16 * (j + 1))
                for s in range(GS):
                    pool.tensor_tensor(x_res[:, s, :], x_res[:, s, :], bo_all[:], ALU.add).then_inc(xres_ready, 1)

            def normalise(j):
                pool.wait_ge(half_var_ready, j + 1)
                pool.wait_ge(seed_ready, j + 1)
                newton_rsqrt(pool, newton_done, NEWTON_OPS * j, rstd[:], half_var[:], newton_tmp[:], three_halves[:])
                pool.wait_ge(y_stored, 16 * j)
                stand_apart(pool, pool_passed)
                for s in range(GS):
                    pool.tensor_scalar(y_out[:, s, :], z[:, s, :],
                                       mean_var[:, s, 0:1], rstd[:, s:s + 1], ALU.subtract, ALU.mult)\
                        .then_inc(y_done, 1)

            add_bias(0)
            normalise(0)
            add_bias(1)
            with pool.Fori(1, GROUPS - 1) as j:
                normalise(j)
                add_bias(j + 1)
            normalise(GROUPS - 1)

        @block.scalar
        def _(act):
            def x_hi(j):
                for c, src in enumerate((qk_bank, pT_bank)):
                    if c == 0:
                        act.wait_ge(xT_done, j + 1)
                    act.activation(xT_hi[:, c, :], src[:], ACT.Copy).then_inc(xT_hi_ready, 1)

            def copy_block(n, q, b):
                act.wait_ge(block_done, n + 1)
                act.activation(qkT[:, q % 2, b, :], qk_bank[:], ACT.Copy).then_inc(block_out, 1)

            def output_hi(n):
                act.wait_ge(oT_done, n)
                act.activation(oT_hi[:].rearrange("p c t -> p (c t)"), oT_bank, ACT.Copy).then_inc(oT_hi_ready, 1)

            def exponentials(n, u):
                act.wait_ge(neg_max_ready, n + 1)
                for h in range(QH):
                    act.activation(probs[:, u % 2, h, :], probs[:, u % 2, h, :], ACT.Exp,
                                   bias=neg_max[:, u % 2, h:h + 1], scale=ATT_SCALE).then_inc(exp_done, 1)
                act.activation(zero_exp[:, u % 2, :], neg_max[:, u % 2, :], ACT.Exp).then_inc(zero_exp_ready, 1)

            x_hi(0)
            for k in range(AHEAD):
                copy_block(k, k // BLOCKS, k % BLOCKS)
            exponentials(0, 0)

            def group(g, first=False, last=False):
                for u in range(UNITS):
                    n = g * UNITS + u
                    if not (first and u == 0):
                        output_hi(n)
                    if not (last and u == UNITS - 1):
                        exponentials(n + 1, u + 1)
                    if u == SWITCH and not last:
                        x_hi(g + 1)
                    if not (last and u + AHEAD >= UNITS):
                        copy_block(n + AHEAD, (u + AHEAD) // BLOCKS, (u + AHEAD) % BLOCKS)

            group(0, first=True)
            with act.Fori(1, GROUPS - 1) as g:
                group(g)
            group(GROUPS - 1, last=True)
            output_hi(GROUPS * UNITS)

        @block.vector
        def _(dve):
            def split_weights(q):
                dve.wait_ge(w_loaded[q], 16 * 3)
                for i, cols in enumerate(w_cols(q)):
                    dve.tensor_copy(w_hi[:, :, cols], w_raw[:, :, cols]).then_inc(w_hi_ready, 1)
                for i, cols in enumerate(w_cols(q)):
                    dve.wait_ge(w_hi_ready, 3 * q + i + 1)
                    dve.tensor_tensor(w_lo[:, :, cols], w_raw[:, :, cols], w_hi[:, :, cols].bitcast(F32),
                                      ALU.subtract).then_inc(w_ready, 1)

            def x_lo(j):
                for c, src in enumerate((qk_bank, pT_bank)):
                    dve.wait_ge(xT_hi_ready, KC * j + c + 1)
                    dve.tensor_tensor(xT_lo[:, c, :], src[:], xT_hi[:, c, :].bitcast(F32), ALU.subtract)\
                        .then_inc(xT_lo_ready, 1)

            def copy_values(n, q, s):
                dve.wait_ge(v_done, n + 1)
                dve.tensor_copy(v_one[:, q % 2, s, :, 0:DH], v_bank[:, 0:QF].rearrange("p (h d) -> p h d", h=QH))\
                    .then_inc(v_out, 1)

            def output_lo(n):
                dve.wait_ge(oT_hi_ready, n)
                dve.tensor_tensor(oT_lo[:].rearrange("p c t -> p (c t)"), oT_bank,
                                  oT_hi[:].rearrange("p c t -> p (c t)").bitcast(F32), ALU.subtract)\
                    .then_inc(oT_lo_ready, 1)

            def residual(j):
                dve.wait_ge(wo_done, UNITS * (j + 1))
                dve.wait_ge(xres_ready, GS * (j + 1))
                dve.wait_ge(y_done, GS * j)
                for i in range(2):
                    dve.tensor_tensor(z[:, 2 * i:2 * i + 2, :].rearrange("p s d -> p (s d)"), acc[i][:],
                                      x_res[:, 2 * i:2 * i + 2, :].rearrange("p s d -> p (s d)"), ALU.add)\
                        .then_inc(z_ready, 1)

            def residual_stats(j):
                for s in range(GS):
                    dve.wait_ge(z_ready, 2 * j + s // 2 + 1)
                    dve.bn_stats(stats[:, s, :], z[:, s, :]).then_inc(stats_ready, 1)
                dve.wait_ge(stats_ready, GS * (j + 1))
                stand_apart(dve, dve_passed)
                for s in range(GS):
                    dve.bn_aggr(mean_var[:, s, :], stats[:, s, :]).then_inc(mean_var_ready, 1)
                dve.wait_ge(mean_var_ready, GS * (j + 1))
                dve.tensor_scalar(var_eps[:], mean_var[:, :, 1], LN_EPS, None, ALU.add).then_inc(var_eps_ready, 1)
                dve.wait_ge(var_eps_ready, j + 1)
                dve.tensor_scalar(half_var[:], var_eps[:], 0.5, None, ALU.mult).then_inc(half_var_ready, 1)
                dve.tensor_scalar(half_bits[:], var_eps[:].bitcast(I32), 1, None, ALU.logical_shift_right)\
                    .then_inc(half_ready, 1)
                dve.wait_ge(half_ready, j + 1)
                dve.tensor_scalar(rstd[:].bitcast(I32), half_bits[:], -1.0, float(RSQRT_SEED), ALU.mult, ALU.add)\
                    .then_inc(seed_ready, 1)

            def masked_scores(n, u):
                dve.wait_ge(scores_done, n + 1)
                if not (isinstance(n, int) and n < 2):
                    dve.wait_ge(pT_done, n - 1)
                stand_apart(dve, dve_passed)
                for h in range(QH):
                    dve.tensor_tensor_reduce(probs[:, u % 2, h, :], score_bank[h % 2][:, (h // 2) * P:(h // 2 + 1) * P],
                                             mask[:], 1.0, MASKED, ALU.add, ALU.max, row_max[:, u % 2, h:h + 1])\
                        .then_inc(masked_done, 1)
                dve.wait_ge(masked_done, QH * (n + 1))
                dve.tensor_scalar(neg_max[:, u % 2, :], row_max[:, u % 2, :], -ATT_SCALE, 0.0, ALU.mult, ALU.min)\
                    .then_inc(neg_max_ready, 1)

            def outputs(n, u):
                dve.wait_ge(av_done, n + 1)
                dve.wait_ge(zero_exp_ready, n + 1)
                dve.scalar_tensor_tensor(denom[:], zero_exp[:, u % 2, :], float(P), av[:, :, DH],
                                         ALU.mult, ALU.add).then_inc(denom_ready, 1)
                dve.wait_ge(denom_ready, n + 1)
                dve.reciprocal(inv_denom[:], denom[:]).then_inc(inv_ready, 1)
                dve.wait_ge(inv_ready, n + 1)
                dve.tensor_tensor(o_tok[:], av[:, :, 0:DH], inv_denom[:].unsqueeze(2).to_broadcast([P, QH, DH]),
                                  ALU.mult).then_inc(o_ready, 1)

            split_weights(0)
            x_lo(0)
            for s in range(GS):
                copy_values(s, 0, s)
            split_weights(1)
            dve.wait_ge(consts, 6)
            masked_scores(0, 0)
            for q in range(2, QUADS):
                split_weights(q)
            dve.wait_ge(wo_loaded, 16)
            dve.tensor_copy(wo_hi[:], wo_raw).then_inc(wo_hi_ready, 1)
            dve.wait_ge(wo_hi_ready, 1)
            dve.tensor_tensor(wo_lo[:], wo_raw, wo_hi[:].bitcast(F32), ALU.subtract).then_inc(wo_ready, 1)

            def group(g, first=False, last=False):
                for u in range(UNITS):
                    n = g * UNITS + u
                    q, s = divmod(u, GS)
                    if not (first and u == 0):
                        output_lo(n)
                    if u == 1 and not first:
                        residual(g - 1)
                    dve.wait_ge(pT_done, n + 1)
                    dve.tensor_copy(probsT[:].rearrange("p h t -> p (h t)"), pT_bank[:]).then_inc(pT_out, 1)
                    if not (last and u == UNITS - 1):
                        masked_scores(n + 1, u + 1)
                    if not (last and q == QUADS - 1):
                        copy_values(n + GS, q + 1, s)
                    outputs(n, u)
                    if u == SWITCH and not last:
                        x_lo(g + 1)
                    if u == 2 and not first:
                        residual_stats(g - 1)

            group(0, first=True)
            with dve.Fori(1, GROUPS - 1) as g:
                group(g)
            group(GROUPS - 1, last=True)
            output_lo(GROUPS * UNITS)
            residual(GROUPS - 1)
            residual_stats(GROUPS - 1)

        @block.tensor
        def _(pe):
            def transpose_x(j):
                pe.wait_ge(x_loaded, 16 * (j + 1))
                for c, dst in enumerate((qk_bank, pT_bank)):
                    for s in range(GS):
                        last = pe.transpose(dst[:, s * P:(s + 1) * P], x_in[:, s, c * P:(c + 1) * P], ident[:])
                last.then_inc(xT_done, 1)

            def project_block(q, b):
                col = (b // OC) * INNER + q * QF + (b % OC) * P
                k = 0
                for w, xT in ((w_hi, xT_hi), (w_lo, xT_hi), (w_hi, xT_lo)):
                    for c in range(KC):
                        last = pe.matmul(qk_bank[:], w[:, c, col:col + P], xT[:, c, :], start=(k == 0),
                                         stop=(k == 3 * KC - 1))
                        k += 1
                last.then_inc(block_done, 1)

            def project_values(q, s):
                col = 2 * INNER + q * QF
                k = 0
                for w, xT in ((w_hi, xT_hi), (w_hi, xT_lo), (w_lo, xT_hi)):
                    for c in range(KC):
                        last = pe.matmul(v_bank[:, 0:QF], xT[:, c, s * P:(s + 1) * P], w[:, c, col:col + QF],
                                         start=(k == 0), stop=(k == 3 * KC - 1))
                        k += 1
                last.then_inc(v_done, 1)

            def scores(n, u):
                q, s = divmod(u % UNITS, GS)
                if s == 0:
                    pe.wait_ge(block_out, n + BLOCKS)
                pe.wait_ge(masked_done, QH * n)
                toks = slice(s * P, (s + 1) * P)
                for h in range(QH):
                    rows = slice(DH * (h % 2), DH * (h % 2 + 1))
                    last = pe.matmul(score_bank[h % 2][:, (h // 2) * P:(h // 2 + 1) * P],
                                     qkT[rows, q % 2, h // 2, toks], qkT[rows, q % 2, OC + h // 2, toks],
                                     start=True, stop=True)
                last.then_inc(scores_done, 1)

            def transpose_output(n):
                pe.wait_ge(o_ready, n + 1)
                for c in range(OC):
                    last = pe.transpose(oT_bank[:, c * P:(c + 1) * P],
                                        o_tok[:, 2 * c:2 * c + 2, :].rearrange("p h d -> p (h d)"), ident[:])
                last.then_inc(oT_done, 1)

            def project_output(n, u):
                q, s = divmod(u, GS)
                pe.wait_ge(oT_lo_ready, n)
                out = acc[s // 2][:, (s % 2) * DM:(s % 2 + 1) * DM]
                k = 0
                for oT, w in ((oT_hi, wo_hi), (oT_hi, wo_lo), (oT_lo, wo_hi)):
                    for c in range(OC):
                        last = pe.matmul(out, oT[:, c, :], w[:, OC * q + c, :],
                                         start=(q == 0 and s % 2 == 0 and k == 0),
                                         stop=(q == QUADS - 1 and k == 3 * OC - 1), skip_group_check=True)
                        k += 1
                last.then_inc(wo_done, 1)

            pe.wait_ge(consts, 6)
            transpose_x(0)
            pe.wait_ge(w_ready, 3)
            pe.wait_ge(xT_lo_ready, KC)
            for k in range(AHEAD):
                if k:
                    pe.wait_ge(block_out, k)
                if k == BLOCKS:
                    pe.wait_ge(w_ready, 6)
                project_block(k // BLOCKS, k % BLOCKS)
                if k < GS:
                    if k:
                        pe.wait_ge(v_out, k)
                    project_values(0, k)
            scores(0, 0)

            def group(g, first=False, last=False):
                for u in range(UNITS):
                    n = g * UNITS + u
                    q, s = divmod(u, GS)
                    pe.wait_ge(exp_done, QH * (n + 1))
                    pe.wait_ge(pT_out, n)
                    if u == SWITCH + 1 and not last:
                        pe.wait_ge(xT_lo_ready, KC * (g + 2))
                    for h in range(QH):
                        last_mm = pe.transpose(pT_bank[:, h * P:(h + 1) * P], probs[:, u % 2, h, :], ident[:])
                    last_mm.then_inc(pT_done, 1)
                    if not (last and u == UNITS - 1):
                        scores(n + 1, u + 1)
                    if not (last and q == QUADS - 1):
                        if first and s == 0:
                            pe.wait_ge(w_ready, 3 * min(q + 2, QUADS))
                        if not (first and u == 0):
                            pe.wait_ge(oT_lo_ready, n)
                        pe.wait_ge(v_out, n + GS)
                        project_values((q + 1) % QUADS, s)
                    if u == SWITCH and not last:
                        pe.wait_ge(block_out, n + AHEAD)
                        pe.wait_ge(pT_out, n + 1)
                        transpose_x(g + 1)
                    pe.wait_ge(pT_out, n + 1)
                    if s == 0:
                        pe.wait_ge(v_out, GS * (g * QUADS + q + 1))
                    for h in range(QH):
                        last_mm = pe.matmul(av[:, h, :], probsT[:, h, :], v_one[:, q % 2, s, h, :],
                                            start=True, stop=True)
                    last_mm.then_inc(av_done, 1)

                    def next_block():
                        if not (last and u + AHEAD >= UNITS):
                            pe.wait_ge(block_out, n + AHEAD)
                            if u == SWITCH:
                                pe.wait_ge(xT_lo_ready, KC * (g + 2))
                            if first and s == GS - 1 and u < SWITCH:
                                pe.wait_ge(w_ready, 3 * min(q + 3, QUADS))
                            project_block((u + AHEAD) // BLOCKS % QUADS, (u + AHEAD) % BLOCKS)

                    if u != SWITCH:
                        next_block()
                    if not (first and u == 0):
                        if first and u == 1:
                            pe.wait_ge(wo_ready, 1)
                        if not first and u == 1:
                            pe.wait_ge(z_ready, 2 * g)
                        project_output(n, (u - 1) % UNITS)
                    transpose_output(n)
                    if u == SWITCH:
                        next_block()

            group(0, first=True)
            with pe.Fori(1, GROUPS - 1) as g:
                group(g)
            group(GROUPS - 1, last=True)
            project_output(GROUPS * UNITS, UNITS - 1)

        blocks.close()
        with nc.Block() as clearing:
            @clearing.gpsimd
            def _(pool):
                pool.sem_clear(range(w_loaded[0].num, pool_passed.num + 1))


def mlstm_and_experts(nc, out, y1, ctx_in, w_i, b_i, w_f, b_f, ln_w, w_r, b_r, w_gu, b_gu, w_d, b_d):
    with ExitStack() as ctx:
        def sb(name, shape, dt=F32):
            return ctx.enter_context(nc.sbuf_tensor(name, shape, dt))

        def bank(name):
            return ctx.enter_context(nc.psum_tensor(name, [P, 512], F32))

        def sem(name):
            return ctx.enter_context(nc.semaphore(name))

        gu_raw = sb("gu_raw", [P, KC, 2 * FI])
        d_raw = sb("d_raw", [P, FB, DM])
        gu_hi = sb("gu_hi", [P, E, KC, 2 * FI], F32R)
        gu_lo = sb("gu_lo", [P, E, KC, 2 * FI], F32R)
        d_hi = sb("d_hi", [P, E, FB, DM], F32R)
        d_lo = sb("d_lo", [P, E, FB, DM], F32R)
        gu_bias_rows = sb("gu_bias_rows", [E * 2 * FB, P])
        gu_bias = sb("gu_bias", [P, E * 2 * FB])
        d_bias = sb("d_bias", [GS * E, GS, DM])
        r_rows = sb("r_rows", [E, DM])
        r_hi = sb("r_hi", [P, KC, E], F32R)
        r_lo = sb("r_lo", [P, KC, E], F32R)
        r_bias = sb("r_bias", [P, E])
        row = sb("row", [1, E + 2 * MH + DM])
        row_all = sb("row_all", [P, E + 2 * MH + DM])
        gate_rows = sb("gate_rows", [2 * MH, 3 * DM])
        gate_T = sb("gate_T", [P, 3 * KC, 2 * MH])
        gate_w = sb("gate_w", [P, 2 * KC, 2 * MH])
        gate_bias = row_all[:, E:E + 2 * MH]
        head_scale = sb("head_scale", [P, DM])
        ident = sb("ident2", [P, P])
        ident_b = sb("ident_b", [P, P], BF16)
        ones_to = sb("ones_to", [P, P])
        after_b = sb("after_b", [P, MH, P], BF16)
        neg_sel_f = sb("neg_sel_f", [48, PAIRS])
        neg_sel = sb("neg_sel", [48, PAIRS, P], F32R)
        before = sb("before", [P, E, E])
        behind = sb("behind", [P, E, E])
        y_in = sb("y_in", [P, GS, DM])
        c_in = sb("c_in", [P, GS, DM])
        c_one = sb("c_one", [P, GS, MH, MD + 1])
        ycT = sb("ycT", [P, GS, 2 * KC, P])
        gates = sb("gates", [P, GS, 2 * MH])
        abs_f = sb("abs_f", [P, GS, MH])
        soft = sb("soft", [P, GS, MH])
        log_f = sb("log_f", [P, GS, MH])
        cum_f = sb("cum_f", [P, PAIRS])
        a_tok = sb("a_tok", [P, PAIRS])
        a_rows = sb("a_rows", [PAIRS, P])
        m_rows = sb("m_rows", [PAIRS, P])
        m_split = sb("m_split", [48, P], F32R)
        max_log = sb("max_log", [P, PAIRS])
        floor = sb("floor", [P, PAIRS])
        decay = sb("decay", [P, MH, P])
        cmat = sb("cmat", [P, MH, P])
        norm_abs = sb("norm_abs", [P, MH])
        norm_max = sb("norm_max", [P, MH])
        norm_inv = sb("norm_inv", [P, MH])
        y2 = sb("y2", [P, GS, DM])
        h_stats = sb("h_stats", [P, MH, 6])
        h_mv = sb("h_mv", [P, MH, 2])
        h_var = sb("h_var", [P, MH])
        h_half = sb("h_half", [P, MH], I32)
        h_rstd = sb("h_rstd", [P, MH])
        h_hvar = sb("h_hvar", [P, MH])
        h_tmp = sb("h_tmp", [P, MH])
        l_stats = sb("l_stats", [P, GS, 6])
        l_mv = sb("l_mv", [P, GS, 2])
        l_var = sb("l_var", [P, GS])
        l_half = sb("l_half", [P, GS], I32)
        l_rstd = sb("l_rstd", [P, GS])
        l_hvar = sb("l_hvar", [P, GS])
        l_tmp = sb("l_tmp", [P, GS])
        yT_hi = sb("yT_hi", [P, KC, GT], F32R)
        yT_lo = sb("yT_lo", [P, KC, GT], F32R)
        logits = sb("logits", [P, GS, E])
        beats = sb("beats", [P, GS * E, E])
        ties = sb("ties", [P, GS * E, E])
        rank = sb("rank", [P, GS * E])
        top = sb("top", [P, GS * E])
        peak = sb("peak", [P, GS])
        r_exp = sb("r_exp", [P, GS, E])
        r_sum = sb("r_sum", [P, GS])
        r_inv = sb("r_inv", [P, GS])
        share = sb("share", [P, GS, E])
        half_share = sb("half_share", [P, GS, E])
        share_T = sb("share_T", [GS * E, P])
        gate = sb("gate", [P, FB, GT])
        tanh = sb("tanh", [P, FB, GT])
        up = sb("up", [P, FB, GT])
        act_hi = sb("act_hi", [P, 2, FB, GT], F32R)
        act_lo = sb("act_lo", [P, 2, FB, GT], F32R)
        acc = sb("acc", [P, GS, DM])
        e_stats = sb("e_stats", [P, GS, 6])
        e_mv = sb("e_mv", [P, GS, 2])
        e_var = sb("e_var", [P, GS])
        e_half = sb("e_half", [P, GS], I32)
        e_rstd = sb("e_rstd", [P, GS])
        e_hvar = sb("e_hvar", [P, GS])
        e_tmp = sb("e_tmp", [P, GS])
        y_out = sb("y_out2", [P, GS, DM])
        three_halves = sb("three_halves2", [P, GS])

        up_bank = [bank(f"up_bank{i}") for i in range(2)]
        down_bank = [bank(f"down_bank{i}") for i in range(2)]
        pair_bank = [bank(f"pair_bank{i}") for i in range(2)]
        log_bank = bank("log_bank")
        small_bank = bank("small_bank")
        head_out = small_bank[:, 0:MH * (MD + 1)].rearrange("p (h d) -> p h d", h=MH)
        gates_ps = small_bank[:, 0:GS * 2 * MH].rearrange("p (s k) -> p s k", s=GS)
        logits_ps = small_bank[:, 0:GS * E].rearrange("p (s e) -> p s e", s=GS)

        names = """rows_loaded r_loaded gbias_loaded gate_loaded row_loaded dbias_loaded gu_loaded d_loaded
            y_loaded cin_loaded c_loaded consts setup_T setup_out row_ready gate_w_ready gu_hi_ready gu_ready d_hi_ready
            d_ready yc_done yc_out gates_done gates_ready abs_ready gate_exp soft_ready log_f_ready cum_done
            cum_ready a_ready aT_done a_rows_ready m_ready m_hi_ready m_lo_ready mT_done max_log_ready
            floor_exp floor_ready log_done decay_ready qk_done cmat_ready av_done abs_norm norm_ready inv_ready
            h_ready h_stats_ready h_mv_ready h_var_ready h_half_ready h_seed h_newton h_norm h_scaled z_ready
            l_stats_ready l_mv_ready l_var_ready l_half_ready l_seed l_newton y2_ready yT_done yT_hi_ready
            yT_lo_ready logits_done logits_ready beats_raw ties_raw beats_cut ties_cut beats_sum rank_ready
            top_ready peak_ready shifted r_exp_ready r_sum_ready r_inv_ready top_exp share_ready
            half_share_ready shareT_done shareT_out dbias_done acc_ready up_done gate_ready tanh_ready
            up_ready clip_ready tanh_gate act_ready act_hi_ready act_lo_ready down_done added e_stats_ready
            e_mv_ready e_var_ready e_half_ready e_seed e_newton y_done y_stored
            h_half_var l_half_var e_half_var dve_passed pool_passed pe_passed"""
        S = {n: sem("m_" + n) for n in names.split()}

        block = ctx.enter_context(nc.Block())

        def rows_of(t, j):
            return t[bass.ds(j * GS, GS)].rearrange("b t d -> t b d")

        @block.sync
        def _(sp):
            sp.dma_start(y_in[:], rows_of(y1, 0)).then_inc(S["y_loaded"], 16)
            sp.dma_start(c_in[:], rows_of(ctx_in, 0)).then_inc(S["cin_loaded"], 16)
            for s in range(GS):
                sp.dma_start(c_one[:, s, :, 0:MD], ctx_in[s].rearrange("t (h d) -> t h d", h=MH))\
                    .then_inc(S["c_loaded"], 16)
            sp.dma_start(gate_rows[0:MH, :], w_i).then_inc(S["gate_loaded"], 16)
            sp.dma_start(gate_rows[MH:2 * MH, :], w_f).then_inc(S["gate_loaded"], 16)
            for src, at, n in ((b_r, 0, E), (b_i, E, MH), (b_f, E + MH, MH), (ln_w, E + 2 * MH, DM)):
                sp.dma_start(row[:, at:at + n], src.rearrange("(a n) -> a n", a=1)).then_inc(S["row_loaded"], 16)
            sp.dma_start(r_rows[:], w_r).then_inc(S["r_loaded"], 16)
            sp.dma_start(gu_bias_rows[:], b_gu.rearrange("e (b p) -> (e b) p", p=P)).then_inc(S["gbias_loaded"], 16)
            sp.wait_ge(S["consts"], 2)
            for s in range(GS):
                sp.dma_start(d_bias[s * E:(s + 1) * E, s, :], b_d).then_inc(S["dbias_loaded"], 16)

            for e in range(E):
                sp.wait_ge(S["gu_ready"], e)
                sp.dma_start(gu_raw[:], w_gu[e].rearrange("(c p) n -> p c n", p=P)).then_inc(S["gu_loaded"], 16)
                sp.wait_ge(S["d_ready"], e)
                sp.dma_start(d_raw[:], w_d[e].rearrange("(c p) n -> p c n", p=P)).then_inc(S["d_loaded"], 16)

            def load(j):
                sp.wait_ge(S["z_ready"], GS * j)
                sp.dma_start(y_in[:], rows_of(y1, j)).then_inc(S["y_loaded"], 16)
                sp.dma_start(c_in[:], rows_of(ctx_in, j)).then_inc(S["cin_loaded"], 16)
                for s in range(GS):
                    sp.dma_start(c_one[:, s, :, 0:MD],
                                 ctx_in[bass.ds(j * GS + s, 1)].rearrange("b t (h d) -> (b t) h d", h=MH))\
                        .then_inc(S["c_loaded"], 16)

            def store(g):
                sp.wait_ge(S["y_done"], GS * (g + 1))
                sp.dma_start(rows_of(out, g), y_out[:]).then_inc(S["y_stored"], 16)

            load(1)
            with sp.Fori(0, GROUPS - 2) as g:
                load(g + 2)
                store(g)
            store(GROUPS - 2)
            store(GROUPS - 1)
            sp.wait_ge(S["y_stored"], 16 * GROUPS)

        @block.gpsimd
        def _(pool):
            pool.memset(d_bias[:], 0.0).then_inc(S["consts"], 1)
            pool.memset(c_one[:, :, :, MD:MD + 1].rearrange("p s h d -> p (s h d)"), 1.0).then_inc(S["consts"], 1)
            pool.memset(ident[:], 0.0).then_inc(S["consts"], 1)
            pool.memset(ones_to[:], 1.0).then_inc(S["consts"], 1)
            pool.memset(after_b[:], 0.0).then_inc(S["consts"], 1)
            pool.memset(neg_sel_f[:], 0.0).then_inc(S["consts"], 1)
            pool.memset(before[:], 0.0).then_inc(S["consts"], 1)
            pool.memset(behind[:], 0.0).then_inc(S["consts"], 1)
            pool.memset(three_halves[:], 1.5).then_inc(S["consts"], 1)
            pool.wait_ge(S["consts"], 9)
            pool.affine_select(out=ident[:], in_=ident[:], compare_op=ALU.not_equal, fill=1.0, base=0,
                               pattern=[[-1, P]], channel_multiplier=1).then_inc(S["consts"], 1)
            pool.affine_select(out=ones_to[:], in_=ones_to[:], compare_op=ALU.is_ge, fill=0.0, base=0,
                               pattern=[[1, P]], channel_multiplier=-1).then_inc(S["consts"], 1)
            pool.affine_select(out=after_b[:], in_=after_b[:], compare_op=ALU.is_ge, fill=MASKED, base=0,
                               pattern=[[0, MH], [1, P]], channel_multiplier=-1).then_inc(S["consts"], 1)
            pool.affine_select(out=before[:], in_=before[:], compare_op=ALU.is_ge, fill=1.0, base=0,
                               pattern=[[-1, E], [1, E]], channel_multiplier=0).then_inc(S["consts"], 1)
            pool.affine_select(out=behind[:], in_=behind[:], compare_op=ALU.is_ge, fill=1.0, base=0,
                               pattern=[[1, E], [-1, E]], channel_multiplier=0).then_inc(S["consts"], 1)
            for k, at in enumerate((0, 32)):
                pool.affine_select(out=neg_sel_f[:], in_=neg_sel_f[:], compare_op=ALU.not_equal, fill=-1.0,
                                   base=-at, pattern=[[-1, PAIRS]], channel_multiplier=1).then_inc(S["consts"], 1)
                pool.wait_ge(S["consts"], 15 + k)
            pool.wait_ge(S["row_loaded"], 64)
            pool.partition_broadcast(row_all[:], row[:]).then_inc(S["row_ready"], 1)
            pool.wait_ge(S["row_ready"], 1)
            pool.tensor_scalar(head_scale[:], row_all[:, E + 2 * MH:], 1.0, None, ALU.add).then_inc(S["row_ready"], 1)

            def head_norm(j, s):
                n = j * GS + s
                pool.wait_ge(S["h_half_var"], n + 1)
                pool.wait_ge(S["h_seed"], n + 1)
                newton_rsqrt(pool, S["h_newton"], NEWTON_OPS * n, h_rstd[:], h_hvar[:], h_tmp[:], three_halves[:])
                stand_apart(pool, S["pool_passed"])
                for h in range(MH):
                    part = y2[:, s, h * MD:(h + 1) * MD]
                    pool.tensor_scalar(part, part, h_mv[:, h, 0:1], h_rstd[:, h:h + 1], ALU.subtract, ALU.mult)\
                        .then_inc(S["h_norm"], 1)
                pool.wait_ge(S["h_norm"], MH * (n + 1))
                pool.tensor_tensor(y2[:, s, :], y2[:, s, :], head_scale[:], ALU.mult).then_inc(S["h_scaled"], 1)
                pool.wait_ge(S["h_scaled"], n + 1)
                pool.tensor_tensor(y2[:, s, :], y2[:, s, :], y_in[:, s, :], ALU.add).then_inc(S["z_ready"], 1)

            def layer_norm(j):
                pool.wait_ge(S["l_half_var"], j + 1)
                pool.wait_ge(S["l_seed"], j + 1)
                newton_rsqrt(pool, S["l_newton"], NEWTON_OPS * j, l_rstd[:], l_hvar[:], l_tmp[:], three_halves[:])
                stand_apart(pool, S["pool_passed"])
                for s in range(GS):
                    pool.tensor_scalar(y2[:, s, :], y2[:, s, :], l_mv[:, s, 0:1], l_rstd[:, s:s + 1],
                                       ALU.subtract, ALU.mult).then_inc(S["y2_ready"], 1)

            def lower_act(g, e):
                for fb in range(FB):
                    n = (g * E + e) * FB + fb
                    pool.wait_ge(S["act_hi_ready"], n + 1)
                    pool.tensor_tensor(act_lo[:, e % 2, fb, :], gate[:, fb, :], act_hi[:, e % 2, fb, :].bitcast(F32),
                                       ALU.subtract).then_inc(S["act_lo_ready"], 1)

            def output_norm(g):
                pool.wait_ge(S["e_half_var"], g + 1)
                pool.wait_ge(S["e_seed"], g + 1)
                newton_rsqrt(pool, S["e_newton"], NEWTON_OPS * g, e_rstd[:], e_hvar[:], e_tmp[:], three_halves[:])
                pool.wait_ge(S["y_stored"], 16 * g)
                stand_apart(pool, S["pool_passed"])
                for s in range(GS):
                    pool.tensor_scalar(y_out[:, s, :], acc[:, s, :], e_mv[:, s, 0:1], e_rstd[:, s:s + 1],
                                       ALU.subtract, ALU.mult).then_inc(S["y_done"], 1)

            def mlstm_part(j, e):
                if 2 <= e < 2 + GS:
                    head_norm(j, e - 2)
                if e == 6:
                    layer_norm(j)

            def body(g, last=False):
                for e in range(E):
                    lower_act(g, e)
                    if not last:
                        mlstm_part(g + 1, e)
                output_norm(g)

            for e in range(E):
                mlstm_part(0, e)
            body(0)
            with pool.Fori(1, GROUPS - 1) as g:
                body(g)
            body(GROUPS - 1, last=True)

        @block.scalar
        def _(act):
            act.wait_ge(S["setup_T"], 1)
            act.activation(gate_T[:].rearrange("p c k -> p (c k)"), small_bank[:, 0:3 * KC * 2 * MH], ACT.Copy)\
                .then_inc(S["setup_out"], 1)
            act.activation(gu_bias[:], small_bank[:, 64:64 + E * 2 * FB], ACT.Copy).then_inc(S["setup_out"], 1)
            act.activation(r_hi[:].rearrange("p c e -> p (c e)"), small_bank[:, 128:128 + KC * E], ACT.Copy)\
                .then_inc(S["setup_out"], 1)

            def mlstm_a(j, e):
                if e == 0:
                    for s in range(GS):
                        act.wait_ge(S["yc_done"], j * GS + s + 1)
                        act.activation(ycT[:, s, :, :].rearrange("p c t -> p (c t)"), pair_bank[s % 2][:], ACT.Copy)\
                            .then_inc(S["yc_out"], 1)
                if e == 2:
                    act.wait_ge(S["max_log_ready"], j + 1)
                    act.activation(floor[:], max_log[:], ACT.Exp, scale=-1.0).then_inc(S["floor_exp"], 1)
                if 2 <= e < 2 + GS:
                    n = j * GS + e - 2
                    act.wait_ge(S["log_done"], n + 1)
                    act.wait_ge(S["cmat_ready"], 2 * n)
                    for h in range(MH):
                        act.activation(decay[:, h, :], log_bank[:, h * P:(h + 1) * P], ACT.Exp,
                                       bias=a_tok[:, (e - 2) * MH + h:(e - 2) * MH + h + 1])\
                            .then_inc(S["decay_ready"], 1)

            def mlstm_b(j, e):
                if e == 0:
                    act.wait_ge(S["abs_ready"], j + 1)
                    act.activation(soft[:], abs_f[:], ACT.Exp, scale=-1.0).then_inc(S["gate_exp"], 1)
                    act.wait_ge(S["gate_exp"], j + 1)
                    act.activation(soft[:], soft[:], ACT.Ln, bias=1.0).then_inc(S["soft_ready"], 1)
                if 2 <= e < 2 + GS:
                    n = j * GS + e - 2
                    act.wait_ge(S["av_done"], n + 1)
                    act.wait_ge(S["norm_ready"], n)
                    act.activation(norm_abs[:], head_out[:, :, MD], ACT.Abs).then_inc(S["abs_norm"], 1)

            def expert(g, e):
                for fb in range(FB):
                    n = (g * E + e) * FB + fb
                    act.wait_ge(S["gate_ready"], n + 1)
                    act.activation(tanh[:, fb, :], gate[:, fb, :], ACT.Tanh, scale=ALPHA / 2)\
                        .then_inc(S["tanh_ready"], 1)
                    act.wait_ge(S["up_done"], 2 * n + 2)
                    act.activation(up[:, fb, :], up_bank[1][:], ACT.Identity,
                                   bias=gu_bias[:, e * 2 * FB + FB + fb:e * 2 * FB + FB + fb + 1])\
                        .then_inc(S["up_ready"], 1)
                    act.wait_ge(S["act_ready"], n + 1)
                    act.activation(act_hi[:, e % 2, fb, :], gate[:, fb, :], ACT.Copy).then_inc(S["act_hi_ready"], 1)

            def transposed_y2(j):
                act.wait_ge(S["yT_done"], j + 1)
                for c in range(KC):
                    act.activation(yT_hi[:, c, :], pair_bank[c][:], ACT.Copy).then_inc(S["yT_hi_ready"], 1)

            def router_exp(j):
                act.wait_ge(S["shifted"], j + 1)
                act.activation(r_exp[:], r_exp[:], ACT.Exp).then_inc(S["r_exp_ready"], 1)

            def share_transposed(g):
                act.wait_ge(S["shareT_done"], g + 1)
                act.activation(share_T[:], small_bank[0:GS * E, 0:P], ACT.Copy).then_inc(S["shareT_out"], 1)

            for e in range(E):
                mlstm_a(0, e)
                mlstm_b(0, e)
            transposed_y2(0)
            router_exp(0)

            def body(g, last=False):
                for e in range(E):
                    if not last:
                        mlstm_a(g + 1, e)
                    expert(g, e)
                    if e == 0:
                        share_transposed(g)
                    if not last:
                        mlstm_b(g + 1, e)
                if not last:
                    transposed_y2(g + 1)
                    router_exp(g + 1)

            body(0)
            with act.Fori(1, GROUPS - 1) as g:
                body(g)
            body(GROUPS - 1, last=True)

        @block.vector
        def _(dve):
            dve.memset(m_split[:].bitcast(F32), 0.0).then_inc(S["m_lo_ready"], 1)
            dve.wait_ge(S["consts"], 16)
            dve.tensor_copy(neg_sel[:], neg_sel_f[:].unsqueeze(2).to_broadcast([48, PAIRS, P]))\
                .then_inc(S["gate_w_ready"], 1)
            dve.tensor_copy(ident_b[:], ident[:]).then_inc(S["gate_w_ready"], 1)
            dve.wait_ge(S["setup_out"], 3)
            dve.tensor_copy(gate_w[:, 0:KC, :], gate_T[:, 0:KC, :]).then_inc(S["gate_w_ready"], 1)
            dve.tensor_tensor(gate_w[:, KC:2 * KC, :], gate_T[:, KC:2 * KC, :], gate_T[:, 2 * KC:3 * KC, :], ALU.add)\
                .then_inc(S["gate_w_ready"], 1)
            dve.tensor_tensor(r_lo[:].rearrange("p c e -> p (c e)"), small_bank[:, 128:128 + KC * E],
                              r_hi[:].rearrange("p c e -> p (c e)").bitcast(F32), ALU.subtract)\
                .then_inc(S["gate_w_ready"], 1)
            dve.wait_ge(S["row_ready"], 2)

            def split_expert(e):
                dve.wait_ge(S["gu_loaded"], 16 * (e + 1))
                dve.tensor_copy(gu_hi[:, e], gu_raw[:]).then_inc(S["gu_hi_ready"], 1)
                dve.wait_ge(S["d_loaded"], 16 * (e + 1))
                dve.tensor_copy(d_hi[:, e], d_raw[:]).then_inc(S["d_hi_ready"], 1)
                dve.wait_ge(S["gu_hi_ready"], e + 1)
                dve.tensor_tensor(gu_lo[:, e], gu_raw[:], gu_hi[:, e].bitcast(F32), ALU.subtract)\
                    .then_inc(S["gu_ready"], 1)
                dve.wait_ge(S["d_hi_ready"], e + 1)
                dve.tensor_tensor(d_lo[:, e], d_raw[:], d_hi[:, e].bitcast(F32), ALU.subtract)\
                    .then_inc(S["d_ready"], 1)

            def seed(var, half_var, mv, half, rstd, k, ready, n):
                dve.wait_ge(S[k + "_mv_ready"], ready)
                dve.tensor_scalar(var, mv, LN_EPS, None, ALU.add).then_inc(S[k + "_var_ready"], 1)
                dve.wait_ge(S[k + "_var_ready"], n + 1)
                dve.tensor_scalar(half_var, var, 0.5, None, ALU.mult).then_inc(S[k + "_half_var"], 1)
                dve.tensor_scalar(half, var.bitcast(I32), 1, None, ALU.logical_shift_right)\
                    .then_inc(S[k + "_half_ready"], 1)
                dve.wait_ge(S[k + "_half_ready"], n + 1)
                dve.tensor_scalar(rstd.bitcast(I32), half, -1.0, float(RSQRT_SEED), ALU.mult, ALU.add)\
                    .then_inc(S[k + "_seed"], 1)

            def mlstm_a(j, e):
                if e == 1:
                    dve.wait_ge(S["cum_done"], j + 1)
                    dve.tensor_copy(cum_f[:], small_bank[:, 0:PAIRS]).then_inc(S["cum_ready"], 1)
                    dve.wait_ge(S["cum_ready"], j + 1)
                    dve.tensor_tensor(a_tok[:].rearrange("p (s h) -> p s h", s=GS), gates[:, :, 0:MH],
                                      cum_f[:].rearrange("p (s h) -> p s h", s=GS), ALU.subtract)\
                        .then_inc(S["a_ready"], 1)
                if e == 2:
                    dve.wait_ge(S["mT_done"], j + 1)
                    dve.tensor_tensor(max_log[:], small_bank[:, 0:PAIRS], cum_f[:], ALU.add)\
                        .then_inc(S["max_log_ready"], 1)
                    dve.wait_ge(S["floor_exp"], j + 1)
                    dve.tensor_scalar(floor[:], floor[:], NORM_EPS, None, ALU.add).then_inc(S["floor_ready"], 1)
                if 2 <= e < 2 + GS:
                    n = j * GS + e - 2
                    dve.wait_ge(S["qk_done"], n + 1)
                    dve.wait_ge(S["decay_ready"], MH * (n + 1))
                    dve.wait_ge(S["av_done"], n)
                    for i in range(2):
                        dve.scalar_tensor_tensor(cmat[:, i::2, :],
                                                 pair_bank[i][:, 0:2 * P].rearrange("p (h t) -> p h t", h=2),
                                                 QK_SCALE, decay[:, i::2, :], ALU.mult, ALU.mult)\
                            .then_inc(S["cmat_ready"], 1)

            def mlstm_b(j, e):
                if e == 0:
                    dve.wait_ge(S["gates_done"], j + 1)
                    dve.tensor_tensor(gates[:], gates_ps, gate_bias.unsqueeze(1).to_broadcast([P, GS, 2 * MH]), ALU.add)\
                        .then_inc(S["gates_ready"], 1)
                    dve.wait_ge(S["gates_ready"], j + 1)
                    dve.scalar_tensor_tensor(abs_f[:], gates[:, :, MH:], -1.0, gates[:, :, MH:], ALU.mult, ALU.max)\
                        .then_inc(S["abs_ready"], 1)
                    dve.wait_ge(S["soft_ready"], j + 1)
                    dve.scalar_tensor_tensor(log_f[:], gates[:, :, MH:], 0.0, soft[:], ALU.min, ALU.subtract)\
                        .then_inc(S["log_f_ready"], 1)
                if e == 1:
                    dve.wait_ge(S["aT_done"], j + 1)
                    dve.tensor_copy(a_rows[:], small_bank[0:PAIRS, 0:P]).then_inc(S["a_rows_ready"], 1)
                    dve.wait_ge(S["a_rows_ready"], j + 1)
                    dve.tensor_tensor_scan(m_rows[:], a_rows[:], a_rows[:], MASKED, ALU.max, ALU.max)\
                        .then_inc(S["m_ready"], 1)
                    dve.wait_ge(S["m_ready"], j + 1)
                    dve.tensor_copy(m_split[0:PAIRS, :], m_rows[:]).then_inc(S["m_hi_ready"], 1)
                    dve.wait_ge(S["m_hi_ready"], j + 1)
                    dve.tensor_tensor(m_split[32:32 + PAIRS, :], m_rows[:], m_split[0:PAIRS, :].bitcast(F32),
                                      ALU.subtract).then_inc(S["m_lo_ready"], 1)
                if 2 <= e < 2 + GS:
                    s = e - 2
                    n = j * GS + s
                    dve.wait_ge(S["abs_norm"], n + 1)
                    dve.scalar_tensor_tensor(norm_max[:], norm_abs[:], NORM_EPS, floor[:, s * MH:(s + 1) * MH],
                                             ALU.add, ALU.max).then_inc(S["norm_ready"], 1)
                    dve.wait_ge(S["norm_ready"], n + 1)
                    dve.reciprocal(norm_inv[:], norm_max[:]).then_inc(S["inv_ready"], 1)
                    dve.wait_ge(S["inv_ready"], n + 1)
                    if s == 0:
                        dve.wait_ge(S["acc_ready"], 2 * j)
                    dve.tensor_tensor(y2[:, s, :].rearrange("p (h d) -> p h d", h=MH), head_out[:, :, 0:MD],
                                      norm_inv[:].unsqueeze(2).to_broadcast([P, MH, MD]), ALU.mult)\
                        .then_inc(S["h_ready"], 1)
                    dve.wait_ge(S["h_ready"], n + 1)
                    dve.wait_ge(S["h_norm"], MH * n)
                    for h in range(MH):
                        dve.bn_stats(h_stats[:, h, :], y2[:, s, h * MD:(h + 1) * MD]).then_inc(S["h_stats_ready"], 1)
                    dve.wait_ge(S["h_stats_ready"], MH * (n + 1))
                    stand_apart(dve, S["dve_passed"])
                    for h in range(MH):
                        dve.bn_aggr(h_mv[:, h, :], h_stats[:, h, :]).then_inc(S["h_mv_ready"], 1)
                    seed(h_var[:], h_hvar[:], h_mv[:, :, 1], h_half[:], h_rstd[:], "h", MH * (n + 1), n)
                if e == 6:
                    for s in range(GS):
                        dve.wait_ge(S["z_ready"], GS * j + s + 1)
                        dve.bn_stats(l_stats[:, s, :], y2[:, s, :]).then_inc(S["l_stats_ready"], 1)
                    dve.wait_ge(S["l_stats_ready"], GS * (j + 1))
                    stand_apart(dve, S["dve_passed"])
                    for s in range(GS):
                        dve.bn_aggr(l_mv[:, s, :], l_stats[:, s, :]).then_inc(S["l_mv_ready"], 1)
                    seed(l_var[:], l_hvar[:], l_mv[:, :, 1], l_half[:], l_rstd[:], "l", GS * (j + 1), j)

            def gate_block(g, e, fb):
                n = (g * E + e) * FB + fb
                dve.wait_ge(S["up_done"], 2 * n + 1)
                dve.wait_ge(S["act_lo_ready"], n - FB + 1 if e else g * E * FB)
                dve.tensor_scalar(gate[:, fb, :], up_bank[0][:], gu_bias[:, e * 2 * FB + fb:e * 2 * FB + fb + 1],
                                  LIMIT, ALU.add, ALU.min).then_inc(S["gate_ready"], 1)
                dve.wait_ge(S["up_ready"], n + 1)
                dve.tensor_scalar(up[:, fb, :], up[:, fb, :], LIMIT, -LIMIT, ALU.min, ALU.max)\
                    .then_inc(S["clip_ready"], 1)
                dve.wait_ge(S["tanh_ready"], n + 1)
                dve.scalar_tensor_tensor(tanh[:, fb, :], tanh[:, fb, :], 1.0, gate[:, fb, :], ALU.add, ALU.mult)\
                    .then_inc(S["tanh_gate"], 1)
                dve.wait_ge(S["clip_ready"], n + 1)
                dve.wait_ge(S["tanh_gate"], n + 1)
                dve.scalar_tensor_tensor(gate[:, fb, :], up[:, fb, :], 1.0, tanh[:, fb, :], ALU.add, ALU.mult)\
                    .then_inc(S["act_ready"], 1)

            def add_expert(g, e):
                for i in range(2):
                    dve.wait_ge(S["down_done"], 2 * (g * E + e) + i + 1)
                    for s in (2 * i, 2 * i + 1):
                        if e == 0:
                            dve.wait_ge(S["acc_ready"], 2 * (g + 1))
                        else:
                            dve.wait_ge(S["added"], GS * (g * E + e - 1) + s + 1)
                        dve.scalar_tensor_tensor(acc[:, s, :], down_bank[i][:, (s % 2) * DM:(s % 2 + 1) * DM],
                                                 half_share[:, s, e:e + 1], acc[:, s, :], ALU.mult, ALU.add)\
                            .then_inc(S["added"], 1)

            def start_acc(g):
                dve.wait_ge(S["dbias_done"], g + 1)
                dve.wait_ge(S["y_done"], GS * g)
                for i in range(2):
                    dve.tensor_tensor(acc[:, 2 * i:2 * i + 2, :].rearrange("p s d -> p (s d)"), down_bank[i][:],
                                      y2[:, 2 * i:2 * i + 2, :].rearrange("p s d -> p (s d)"), ALU.add)\
                        .then_inc(S["acc_ready"], 1)

            def output_stats(g):
                for s in range(GS):
                    dve.wait_ge(S["added"], GS * (g * E + E - 1) + s + 1)
                    dve.bn_stats(e_stats[:, s, :], acc[:, s, :]).then_inc(S["e_stats_ready"], 1)
                dve.wait_ge(S["e_stats_ready"], GS * (g + 1))
                stand_apart(dve, S["dve_passed"])
                for s in range(GS):
                    dve.bn_aggr(e_mv[:, s, :], e_stats[:, s, :]).then_inc(S["e_mv_ready"], 1)
                seed(e_var[:], e_hvar[:], e_mv[:, :, 1], e_half[:], e_rstd[:], "e", GS * (g + 1), g)

            def lower_y2(j):
                for c in range(KC):
                    dve.wait_ge(S["yT_hi_ready"], KC * j + c + 1)
                    dve.tensor_tensor(yT_lo[:, c, :], pair_bank[c][:], yT_hi[:, c, :].bitcast(F32), ALU.subtract)\
                        .then_inc(S["yT_lo_ready"], 1)

            def route(j):
                dve.wait_ge(S["logits_done"], j + 1)
                dve.tensor_tensor(logits[:], logits_ps, row_all[:, 0:E].unsqueeze(1).to_broadcast([P, GS, E]), ALU.add)\
                    .then_inc(S["logits_ready"], 1)
                dve.wait_ge(S["logits_ready"], j + 1)
                dve.tensor_reduce(peak[:], logits[:], AX.X, ALU.max).then_inc(S["peak_ready"], 1)
                dve.wait_ge(S["peak_ready"], j + 1)
                dve.tensor_tensor(r_exp[:], logits[:], peak[:].unsqueeze(2).to_broadcast([P, GS, E]), ALU.subtract)\
                    .then_inc(S["shifted"], 1)
                this = logits[:].unsqueeze(3).to_broadcast([P, GS, E, E])
                other = logits[:].unsqueeze(2).to_broadcast([P, GS, E, E])
                grid = "p (s k) e -> p s k e"
                dve.tensor_tensor(beats[:].rearrange(grid, s=GS), other, this, ALU.is_gt).then_inc(S["beats_raw"], 1)
                dve.tensor_tensor(ties[:].rearrange(grid, s=GS), other, this, ALU.is_ge).then_inc(S["ties_raw"], 1)
                dve.wait_ge(S["beats_raw"], j + 1)
                dve.tensor_tensor(beats[:].rearrange(grid, s=GS), beats[:].rearrange(grid, s=GS),
                                  behind[:].unsqueeze(1).to_broadcast([P, GS, E, E]), ALU.mult)\
                    .then_inc(S["beats_cut"], 1)
                dve.wait_ge(S["ties_raw"], j + 1)
                dve.tensor_tensor(ties[:].rearrange(grid, s=GS), ties[:].rearrange(grid, s=GS),
                                  before[:].unsqueeze(1).to_broadcast([P, GS, E, E]), ALU.mult)\
                    .then_inc(S["ties_cut"], 1)
                dve.wait_ge(S["beats_cut"], j + 1)
                dve.wait_ge(S["ties_cut"], j + 1)
                dve.tensor_tensor(beats[:], beats[:], ties[:], ALU.add).then_inc(S["beats_sum"], 1)
                dve.wait_ge(S["beats_sum"], j + 1)
                dve.tensor_reduce(rank[:], beats[:], AX.X, ALU.add).then_inc(S["rank_ready"], 1)
                dve.wait_ge(S["rank_ready"], j + 1)
                dve.tensor_scalar(top[:], rank[:], 2.0, None, ALU.is_lt).then_inc(S["top_ready"], 1)
                dve.wait_ge(S["r_exp_ready"], j + 1)
                dve.tensor_reduce(r_sum[:], r_exp[:], AX.X, ALU.add).then_inc(S["r_sum_ready"], 1)
                dve.wait_ge(S["r_sum_ready"], j + 1)
                dve.reciprocal(r_inv[:], r_sum[:]).then_inc(S["r_inv_ready"], 1)
                dve.wait_ge(S["top_ready"], j + 1)
                dve.tensor_tensor(r_exp[:].rearrange("p s e -> p (s e)"), r_exp[:].rearrange("p s e -> p (s e)"), top[:],
                                  ALU.mult).then_inc(S["top_exp"], 1)
                dve.wait_ge(S["top_exp"], j + 1)
                dve.wait_ge(S["r_inv_ready"], j + 1)
                dve.tensor_tensor(share[:], r_exp[:], r_inv[:].unsqueeze(2).to_broadcast([P, GS, E]), ALU.mult)\
                    .then_inc(S["share_ready"], 1)
                dve.wait_ge(S["share_ready"], j + 1)
                dve.tensor_scalar(half_share[:], share[:], 0.5, None, ALU.mult).then_inc(S["half_share_ready"], 1)

            for e in range(E):
                mlstm_a(0, e)
                mlstm_b(0, e)
                split_expert(e)
            lower_y2(0)
            route(0)

            def body(g, last=False):
                for e in range(E):
                    if not last:
                        mlstm_a(g + 1, e)
                    for fb in range(FB):
                        gate_block(g, e, fb)
                    if e == 0:
                        dve.wait_ge(S["half_share_ready"], g + 1)
                        start_acc(g)
                    if not last:
                        mlstm_b(g + 1, e)
                    if e:
                        add_expert(g, e - 1)
                if not last:
                    lower_y2(g + 1)
                add_expert(g, E - 1)
                output_stats(g)
                if not last:
                    route(g + 1)

            body(0)
            with dve.Fori(1, GROUPS - 1) as g:
                body(g)
            body(GROUPS - 1, last=True)

        @block.tensor
        def _(pe):
            pe.wait_ge(S["consts"], 16)
            pe.wait_ge(S["gate_loaded"], 32)
            pe.wait_ge(S["gbias_loaded"], 16)
            pe.wait_ge(S["r_loaded"], 16)
            for c in range(3 * KC):
                pe.transpose(small_bank[:, c * 2 * MH:(c + 1) * 2 * MH], gate_rows[:, c * P:(c + 1) * P],
                             ident[0:2 * MH, 0:2 * MH])
            pe.transpose(small_bank[:, 64:64 + E * 2 * FB], gu_bias_rows[:], ident[0:E * 2 * FB, 0:E * 2 * FB])
            for c in range(KC):
                last_mm = pe.transpose(small_bank[:, 128 + c * E:128 + (c + 1) * E], r_rows[:, c * P:(c + 1) * P],
                                       ident[0:E, 0:E])
            last_mm.then_inc(S["setup_T"], 1)
            pe.wait_ge(S["gate_w_ready"], 5)

            def mlstm_a(j, e):
                if e == 0:
                    pe.wait_ge(S["y_loaded"], 16 * (j + 1))
                    pe.wait_ge(S["cin_loaded"], 16 * (j + 1))
                    pe.wait_ge(S["yT_lo_ready"], KC * j)
                    for s in range(GS):
                        if s >= 2:
                            pe.wait_ge(S["yc_out"], GS * j + s - 1)
                        for c in range(KC):
                            pe.transpose(pair_bank[s % 2][:, c * P:(c + 1) * P], y_in[:, s, c * P:(c + 1) * P],
                                         ident[:])
                        for c in range(KC):
                            last = pe.transpose(pair_bank[s % 2][:, (KC + c) * P:(KC + c + 1) * P],
                                                c_in[:, s, c * P:(c + 1) * P], ident[:])
                        last.then_inc(S["yc_done"], 1)
                if e == 1:
                    pe.wait_ge(S["log_f_ready"], j + 1)
                    pe.matmul(small_bank[:, 0:PAIRS], ones_to[:], log_f[:].rearrange("p s h -> p (s h)"),
                              start=True, stop=True).then_inc(S["cum_done"], 1)
                if e == 2:
                    pe.wait_ge(S["m_lo_ready"], j + 2)
                    stand_apart(pe, S["pe_passed"])
                    pe.transpose(small_bank[:, 0:PAIRS], m_rows[:], ident[0:PAIRS, 0:PAIRS]).then_inc(S["mT_done"], 1)
                if 2 <= e < 2 + GS:
                    s = e - 2
                    n = j * GS + s
                    pe.wait_ge(S["decay_ready"], MH * n)
                    pe.matmul(log_bank[:], ident_b[:], after_b[:].rearrange("p h t -> p (h t)"), start=True,
                              stop=False, skip_group_check=True)
                    for h in range(MH):
                        last = pe.matmul(log_bank[:, h * P:(h + 1) * P], neg_sel[:, s * MH + h, :], m_split[:],
                                         start=False, stop=(h == MH - 1), skip_group_check=True)
                    last.then_inc(S["log_done"], 1)
                    if s == 0:
                        pe.wait_ge(S["yc_out"], GS * (j + 1))
                    pe.wait_ge(S["cmat_ready"], 2 * n)
                    for h in range(MH):
                        rows = slice(MD * (h % 2), MD * (h % 2 + 1))
                        last = pe.matmul(pair_bank[h % 2][:, (h // 2) * P:(h // 2 + 1) * P],
                                         ycT[rows, s, KC + h // 2, :], ycT[rows, s, h // 2, :], start=True, stop=True)
                    last.then_inc(S["qk_done"], 1)

            def mlstm_b(j, e):
                if e == 0:
                    pe.wait_ge(S["yc_out"], GS * (j + 1))
                    for s in range(GS):
                        for c in range(2 * KC):
                            last = pe.matmul(gates_ps[:, s, :], ycT[:, s, c, :], gate_w[:, c, :], start=(c == 0),
                                             stop=(c == 2 * KC - 1))
                    last.then_inc(S["gates_done"], 1)
                if e == 1:
                    pe.wait_ge(S["a_ready"], j + 1)
                    pe.transpose(small_bank[0:PAIRS, 0:P], a_tok[:], ident[:]).then_inc(S["aT_done"], 1)
                if 2 <= e < 2 + GS:
                    s = e - 2
                    n = j * GS + s
                    pe.wait_ge(S["cmat_ready"], 2 * (n + 1))
                    if s == 0:
                        pe.wait_ge(S["c_loaded"], 16 * GS * (j + 1))
                        pe.wait_ge(S["max_log_ready"], j + 1)
                    pe.wait_ge(S["h_ready"], n)
                    for h in range(MH):
                        last = pe.matmul(head_out[:, h, :], cmat[:, h, :], c_one[:, s, h, :], start=True, stop=True)
                    last.then_inc(S["av_done"], 1)

            def transpose_y2(j):
                pe.wait_ge(S["y2_ready"], GS * (j + 1))
                for c in range(KC):
                    for s in range(GS):
                        last = pe.transpose(pair_bank[c][:, s * P:(s + 1) * P], y2[:, s, c * P:(c + 1) * P], ident[:])
                last.then_inc(S["yT_done"], 1)

            def route(j):
                pe.wait_ge(S["yT_lo_ready"], KC * (j + 1))
                for s in range(GS):
                    toks = slice(s * P, (s + 1) * P)
                    k = 0
                    for yT, w in ((yT_hi, r_hi), (yT_hi, r_lo), (yT_lo, r_hi)):
                        for c in range(KC):
                            last = pe.matmul(logits_ps[:, s, :], yT[:, c, toks], w[:, c, :], start=(k == 0),
                                             stop=(k == 3 * KC - 1))
                            k += 1
                last.then_inc(S["logits_done"], 1)

            def up_projections(g, e):
                for fb in range(FB):
                    for i in range(2):
                        n = (g * E + e) * FB + fb
                        pe.wait_ge(S["gate_ready" if i == 0 else "up_ready"], n)
                        col = i * FI + fb * P
                        k = 0
                        for w, yT in ((gu_hi, yT_hi), (gu_lo, yT_hi), (gu_hi, yT_lo)):
                            for c in range(KC):
                                last = pe.matmul(up_bank[i][:], w[:, e, c, col:col + P], yT[:, c, :],
                                                 start=(k == 0), stop=(k == 3 * KC - 1))
                                k += 1
                        last.then_inc(S["up_done"], 1)

            def down_projection(g, e):
                for i in range(2):
                    if i == 0:
                        pe.wait_ge(S["act_lo_ready"], FB * (g * E + e + 1))
                    if e == 0:
                        pe.wait_ge(S["acc_ready"], 2 * (g + 1))
                    else:
                        pe.wait_ge(S["added"], GS * (g * E + e - 1) + 2 * i + 2)
                    for s in (2 * i, 2 * i + 1):
                        toks = slice(s * P, (s + 1) * P)
                        k = 0
                        for a, w in ((act_hi, d_hi), (act_hi, d_lo), (act_lo, d_hi)):
                            for fb in range(FB):
                                last = pe.matmul(down_bank[i][:, (s % 2) * DM:(s % 2 + 1) * DM],
                                                 a[:, e % 2, fb, toks], w[:, e, fb, :], start=(k == 0),
                                                 stop=(k == 3 * FB - 1))
                                k += 1
                    last.then_inc(S["down_done"], 1)

            def bias_shares(g):
                pe.wait_ge(S["half_share_ready"], g + 1)
                pe.transpose(small_bank[0:GS * E, 0:P], share[:].rearrange("p s e -> p (s e)"), ident[:])\
                    .then_inc(S["shareT_done"], 1)
                pe.wait_ge(S["shareT_out"], g + 1)
                pe.wait_ge(S["added"], GS * E * g)
                for s in range(GS):
                    last = pe.matmul(down_bank[s // 2][:, (s % 2) * DM:(s % 2 + 1) * DM], share_T[:], d_bias[:, s, :],
                                     start=True, stop=True)
                last.then_inc(S["dbias_done"], 1)

            for e in range(E):
                mlstm_a(0, e)
                mlstm_b(0, e)
            pe.wait_ge(S["gu_ready"], E)
            pe.wait_ge(S["d_ready"], E)
            pe.wait_ge(S["dbias_loaded"], 16 * GS)
            transpose_y2(0)
            route(0)

            def body(g, last=False):
                for e in range(E):
                    if not last:
                        mlstm_a(g + 1, e)
                    up_projections(g, e)
                    if e == 0:
                        bias_shares(g)
                    if not last:
                        mlstm_b(g + 1, e)
                    if e:
                        down_projection(g, e - 1)
                if not last:
                    transpose_y2(g + 1)
                down_projection(g, E - 1)
                if not last:
                    route(g + 1)

            body(0)
            with pe.Fori(1, GROUPS - 1) as g:
                body(g)
            body(GROUPS - 1, last=True)


def decoder(nc, ins, out):
    y1 = nc.dram_tensor("y1_dram", [NSEQ, P, DM], F32, kind="Internal").ap()
    attention(nc, y1, ins["x"], *(ins["L0_attn_" + n] for n in ("wq", "wkv", "wo", "bo")))
    mlstm_and_experts(nc, out, y1, ins["ctx_1024"],
                      *(ins["L0_xattn_" + n] for n in ("w_igate", "b_igate", "w_fgate", "b_fgate", "ln_weight")),
                      *(ins["L0_ffn_" + n] for n in ("router_weight", "router_bias", "gate_up_proj",
                                                     "gate_up_bias", "down_proj", "down_bias")))


_INS = ['x', 'ctx_1024', 'L0_attn_wq', 'L0_attn_wkv', 'L0_attn_wo', 'L0_attn_bo', 'L0_xattn_w_igate',
        'L0_xattn_b_igate', 'L0_xattn_w_fgate', 'L0_xattn_b_fgate', 'L0_xattn_ln_weight',
        'L0_ffn_router_weight', 'L0_ffn_router_bias', 'L0_ffn_gate_up_proj', 'L0_ffn_gate_up_bias',
        'L0_ffn_down_proj', 'L0_ffn_down_bias']
_OUTS = [((32, 128, 256), 'float32')]


def kernel(**inputs):
    import numpy as _np
    import concourse.bacc as _bacc
    from concourse import mybir as _mybir
    from concourse.bass_utils import run_bass_kernel_spmd as _run

    nc = _bacc.Bacc("TRN2", target_bir_lowering=False, num_devices=1)
    arrays, aps = {}, {}
    for name in _INS:
        a = _np.ascontiguousarray(inputs[name])
        arrays[f"in_{name}_dram"] = a
        aps[name] = nc.dram_tensor(f"in_{name}_dram", a.shape, _mybir.dt.from_np(a.dtype), kind="ExternalInput").ap()
    shape, dtype = _OUTS[0]
    out = nc.dram_tensor("out_0_dram", shape, _mybir.dt.from_np(_np.dtype(dtype)), kind="ExternalOutput").ap()
    decoder(nc, aps, out)
    r = _run(nc, [arrays], core_ids=[0])
    return r.results[0]["out_0_dram"]
```

```python
from contextlib import ExitStack

import concourse.bass as bass
from concourse import mybir

F32 = mybir.dt.float32
F32R = mybir.dt.float32r
BF16 = mybir.dt.bfloat16
I32 = mybir.dt.int32
ALU = mybir.AluOpType
ACT = mybir.ActivationFunctionType
AX = mybir.AxisListType

P = 128
NSEQ = 32
DM = 256
KC = DM // P
GS = 4
GROUPS = NSEQ // GS
GT = GS * P

HEADS = 16
DH = 64
INNER = HEADS * DH
QH = 4
QUADS = HEADS // QH
UNITS = QUADS * GS
QF = QH * DH
OC = QF // P
BLOCKS = 2 * OC
AHEAD = BLOCKS + 1
SWITCH = UNITS - AHEAD
ATT_SCALE = DH**-0.5
MASKED = -3.0e38
LN_EPS = 1e-5
RSQRT_SEED = 0x5F3759DF
NEWTON = 3
NEWTON_OPS = 4 * NEWTON

MH = 4
MD = DM // MH
QK_SCALE = MD**-0.5
NORM_EPS = 1e-6
PAIRS = GS * MH
T_SLOT = 4

E = 8
FI = 256
FB = FI // P
LIMIT = 7.0
ALPHA = 1.702


def stand_apart(eng, passed):
    eng.sem_inc(passed, 1)


def newton_rsqrt(pool, done, base, y, half_v, tmp, three_halves):
    k = 0

    def step(ins):
        nonlocal k
        k += 1
        ins.then_inc(done, 1)
        pool.wait_ge(done, base + k)

    for _ in range(NEWTON):
        step(pool.tensor_tensor(tmp, y, y, ALU.mult))
        step(pool.tensor_tensor(tmp, tmp, half_v, ALU.mult))
        step(pool.tensor_tensor(tmp, three_halves, tmp, ALU.subtract))
        step(pool.tensor_tensor(y, y, tmp, ALU.mult))


def norm_shift(pool, done, base, shift, mean, y, passed):
    pool.tensor_tensor(shift, mean, y, ALU.mult).then_inc(done, 1)
    pool.wait_ge(done, base + 1)
    stand_apart(pool, passed)
    pool.tensor_scalar(shift, shift, -1.0, None, ALU.mult).then_inc(done, 1)


def attention(nc, y1, x, wq, wkv, wo, bo):
    with ExitStack() as ctx:
        def sb(name, shape, dt=F32):
            return ctx.enter_context(nc.sbuf_tensor(name, shape, dt))

        def bank(name):
            return ctx.enter_context(nc.psum_tensor(name, [P, 512], F32))

        def sem(name):
            return ctx.enter_context(nc.semaphore(name))

        w_raw = sb("w_raw", [P, KC, 3 * INNER])
        w_hi = sb("w_hi", [P, KC, 3 * INNER], F32R)
        w_lo = sb("w_lo", [P, KC, 3 * INNER], F32R)
        wo_raw = w_raw[:, 0, 0:8 * DM].rearrange("p (c n) -> p c n", c=8)
        wo_hi = sb("wo_hi", [P, INNER // P, DM], F32R)
        wo_lo = sb("wo_lo", [P, INNER // P, DM], F32R)
        bo_row = sb("bo_row", [1, DM])
        bo_all = sb("bo_all", [P, DM])
        ident = sb("ident", [P, P])
        mask = sb("mask", [P, P])
        x_in = sb("x_in", [P, GS, DM])
        x_res = sb("x_res", [P, GS, DM])
        xT_hi = sb("xT_hi", [P, KC, GT], F32R)
        xT_lo = sb("xT_lo", [P, KC, GT], F32R)
        qkT = sb("qkT", [P, 2, BLOCKS, GT])
        v_one = sb("v_one", [P, 2, GS, QH, DH + 1])
        probs = sb("probs", [P, 2, QH, P])
        probsT = sb("probsT", [P, QH, P])
        row_max = sb("row_max", [P, 2, QH])
        neg_max = sb("neg_max", [P, 2, QH])
        zero_exp = sb("zero_exp", [P, 2, QH])
        denom = sb("denom", [P, QH])
        inv_denom = sb("inv_denom", [P, QH])
        o_tok = sb("o_tok", [P, QH, DH])
        oT_hi = sb("oT_hi", [P, OC, P], F32R)
        oT_lo = sb("oT_lo", [P, OC, P], F32R)
        z = sb("z", [P, GS, DM])
        y_out = sb("y_out", [P, GS, DM])
        stats = sb("stats", [P, GS, 6])
        mean_var = sb("mean_var", [P, GS, 2])
        var_eps = sb("var_eps", [P, GS])
        half_bits = sb("half_bits", [P, GS], I32)
        rstd = sb("rstd", [P, GS])
        half_var = sb("half_var", [P, GS])
        newton_tmp = sb("newton_tmp", [P, GS])
        three_halves = sb("three_halves", [P, GS])

        acc = [bank(f"acc{i}") for i in range(2)]
        score_bank = [bank(f"score_bank{i}") for i in range(2)]
        pT_bank = bank("pT_bank")
        av_bank = bank("av_bank")
        qk_bank = bank("qk_bank")
        v_bank = bank("v_bank")
        oT_bank = v_bank[:, QF:2 * QF]
        av = av_bank[:, 0:QH * (DH + 1)].rearrange("p (h d) -> p h d", h=QH)

        w_loaded = [sem(f"w_loaded{i}") for i in range(QUADS)]
        wo_loaded = sem("wo_loaded")
        bo_loaded = sem("bo_loaded")
        x_loaded = sem("x_loaded")
        xres_loaded = sem("xres_loaded")
        consts = sem("consts")
        w_hi_ready = sem("w_hi_ready")
        w_ready = sem("w_ready")
        wo_hi_ready = sem("wo_hi_ready")
        wo_ready = sem("wo_ready")
        bo_ready = sem("bo_ready")
        xT_done = sem("xT_done")
        xT_hi_ready = sem("xT_hi_ready")
        xT_lo_ready = sem("xT_lo_ready")
        block_done = sem("block_done")
        block_out = sem("block_out")
        v_done = sem("v_done")
        v_out = sem("v_out")
        scores_done = sem("scores_done")
        masked_done = sem("masked_done")
        neg_max_ready = sem("neg_max_ready")
        exp_done = sem("exp_done")
        zero_exp_ready = sem("zero_exp_ready")
        pT_done = sem("pT_done")
        pT_out = sem("pT_out")
        av_done = sem("av_done")
        denom_ready = sem("denom_ready")
        inv_ready = sem("inv_ready")
        o_ready = sem("o_ready")
        oT_done = sem("oT_done")
        oT_hi_ready = sem("oT_hi_ready")
        oT_lo_ready = sem("oT_lo_ready")
        wo_done = sem("wo_done")
        xres_ready = sem("xres_ready")
        z_ready = sem("z_ready")
        stats_ready = sem("stats_ready")
        mean_var_ready = sem("mean_var_ready")
        var_eps_ready = sem("var_eps_ready")
        half_ready = sem("half_ready")
        seed_ready = sem("seed_ready")
        newton_done = sem("newton_done")
        y_done = sem("y_done")
        y_stored = sem("y_stored")
        half_var_ready = sem("half_var_ready")
        dve_passed = sem("dve_passed")
        pool_passed = sem("pool_passed")

        blocks = ctx.enter_context(ExitStack())
        block = blocks.enter_context(nc.Block())

        def x_group(j):
            return x[bass.ds(j * GS, GS)].rearrange("b t d -> t b d")

        w_view = [(wq, 0, 0), (wkv, 0, INNER), (wkv, INNER, 2 * INNER)]

        def w_cols(q):
            return [slice(base + q * QF, base + (q + 1) * QF) for _, _, base in w_view]

        @block.sync
        def _(sp):
            sp.dma_start(x_in[:], x_group(0)).then_inc(x_loaded, 16)
            for q in range(QUADS):
                for src, col, base in w_view:
                    sp.dma_start(w_raw[:, :, base + q * QF:base + (q + 1) * QF],
                                 src[:, col + q * QF:col + (q + 1) * QF]
                                 .rearrange("(c p) n -> p c n", p=P)).then_inc(w_loaded[q], 16)
            sp.dma_start(bo_row[:], bo.rearrange("(a n) -> a n", a=1)).then_inc(bo_loaded, 16)
            sp.dma_start(x_res[:], x_group(0)).then_inc(xres_loaded, 16)
            sp.wait_ge(w_ready, 3 * QUADS)
            sp.dma_start(wo_raw, wo.rearrange("(c p) n -> p c n", p=P)).then_inc(wo_loaded, 16)

            def group(g):
                sp.wait_ge(xT_done, g + 1)
                sp.dma_start(x_in[:], x_group(g + 1)).then_inc(x_loaded, 16)
                sp.wait_ge(z_ready, 2 * (g + 1))
                sp.dma_start(x_res[:], x_group(g + 1)).then_inc(xres_loaded, 16)

            def store(j):
                sp.wait_ge(y_done, GS * (j + 1))
                sp.dma_start(y1[bass.ds(j * GS, GS)].rearrange("b t d -> t b d"), y_out[:]).then_inc(y_stored, 16)

            with sp.Fori(0, GROUPS - 1) as g:
                group(g)
                store(g)
            store(GROUPS - 1)
            sp.wait_ge(y_stored, 16 * GROUPS)

        @block.gpsimd
        def _(pool):
            pool.memset(ident[:], 0.0).then_inc(consts, 1)
            pool.memset(mask[:], 0.0).then_inc(consts, 1)
            pool.memset(three_halves[:], 1.5).then_inc(consts, 1)
            pool.memset(v_one[:, :, :, :, DH:DH + 1].rearrange("p a s h d -> p (a s h d)"), 1.0).then_inc(consts, 1)
            pool.wait_ge(consts, 4)
            pool.affine_select(out=ident[:], in_=ident[:], compare_op=ALU.not_equal, fill=1.0, base=0,
                               pattern=[[-1, P]], channel_multiplier=1).then_inc(consts, 1)
            pool.affine_select(out=mask[:], in_=mask[:], compare_op=ALU.is_ge, fill=MASKED, base=0,
                               pattern=[[-1, P]], channel_multiplier=1).then_inc(consts, 1)
            pool.wait_ge(bo_loaded, 16)
            pool.partition_broadcast(bo_all[:], bo_row[:]).then_inc(bo_ready, 1)
            pool.wait_ge(bo_ready, 1)

            def add_bias(j):
                pool.wait_ge(xres_loaded, 16 * (j + 1))
                for s in range(GS):
                    pool.tensor_tensor(x_res[:, s, :], x_res[:, s, :], bo_all[:], ALU.add).then_inc(xres_ready, 1)

            def normalise(j):
                pool.wait_ge(half_var_ready, j + 1)
                pool.wait_ge(seed_ready, j + 1)
                newton_rsqrt(pool, newton_done, NEWTON_OPS * j, rstd[:], half_var[:], newton_tmp[:], three_halves[:])
                pool.wait_ge(y_stored, 16 * j)
                stand_apart(pool, pool_passed)
                for s in range(GS):
                    pool.tensor_scalar(y_out[:, s, :], z[:, s, :],
                                       mean_var[:, s, 0:1], rstd[:, s:s + 1], ALU.subtract, ALU.mult)\
                        .then_inc(y_done, 1)

            add_bias(0)
            normalise(0)
            add_bias(1)
            with pool.Fori(1, GROUPS - 1) as j:
                normalise(j)
                add_bias(j + 1)
            normalise(GROUPS - 1)

        @block.scalar
        def _(act):
            def x_hi(j):
                for c, src in enumerate((qk_bank, pT_bank)):
                    if c == 0:
                        act.wait_ge(xT_done, j + 1)
                    act.activation(xT_hi[:, c, :], src[:], ACT.Copy).then_inc(xT_hi_ready, 1)

            def copy_block(n, q, b):
                act.wait_ge(block_done, n + 1)
                act.activation(qkT[:, q % 2, b, :], qk_bank[:], ACT.Copy).then_inc(block_out, 1)

            def output_hi(n):
                act.wait_ge(oT_done, n)
                act.activation(oT_hi[:].rearrange("p c t -> p (c t)"), oT_bank, ACT.Copy).then_inc(oT_hi_ready, 1)

            def exponentials(n, u):
                act.wait_ge(neg_max_ready, n + 1)
                for h in range(QH):
                    act.activation(probs[:, u % 2, h, :], probs[:, u % 2, h, :], ACT.Exp,
                                   bias=neg_max[:, u % 2, h:h + 1], scale=ATT_SCALE).then_inc(exp_done, 1)
                act.activation(zero_exp[:, u % 2, :], neg_max[:, u % 2, :], ACT.Exp).then_inc(zero_exp_ready, 1)

            x_hi(0)
            for k in range(AHEAD):
                copy_block(k, k // BLOCKS, k % BLOCKS)
            exponentials(0, 0)

            def group(g, first=False, last=False):
                for u in range(UNITS):
                    n = g * UNITS + u
                    if not (first and u == 0):
                        output_hi(n)
                    if not (last and u == UNITS - 1):
                        exponentials(n + 1, u + 1)
                    if u == SWITCH and not last:
                        x_hi(g + 1)
                    if not (last and u + AHEAD >= UNITS):
                        copy_block(n + AHEAD, (u + AHEAD) // BLOCKS, (u + AHEAD) % BLOCKS)

            group(0, first=True)
            with act.Fori(1, GROUPS - 1) as g:
                group(g)
            group(GROUPS - 1, last=True)
            output_hi(GROUPS * UNITS)

        @block.vector
        def _(dve):
            def split_weights(q):
                dve.wait_ge(w_loaded[q], 16 * 3)
                for i, cols in enumerate(w_cols(q)):
                    dve.tensor_copy(w_hi[:, :, cols], w_raw[:, :, cols]).then_inc(w_hi_ready, 1)
                for i, cols in enumerate(w_cols(q)):
                    dve.wait_ge(w_hi_ready, 3 * q + i + 1)
                    dve.tensor_tensor(w_lo[:, :, cols], w_raw[:, :, cols], w_hi[:, :, cols].bitcast(F32),
                                      ALU.subtract).then_inc(w_ready, 1)

            def x_lo(j):
                for c, src in enumerate((qk_bank, pT_bank)):
                    dve.wait_ge(xT_hi_ready, KC * j + c + 1)
                    dve.tensor_tensor(xT_lo[:, c, :], src[:], xT_hi[:, c, :].bitcast(F32), ALU.subtract)\
                        .then_inc(xT_lo_ready, 1)

            def copy_values(n, q, s):
                dve.wait_ge(v_done, n + 1)
                dve.tensor_copy(v_one[:, q % 2, s, :, 0:DH], v_bank[:, 0:QF].rearrange("p (h d) -> p h d", h=QH))\
                    .then_inc(v_out, 1)

            def output_lo(n):
                dve.wait_ge(oT_hi_ready, n)
                dve.tensor_tensor(oT_lo[:].rearrange("p c t -> p (c t)"), oT_bank,
                                  oT_hi[:].rearrange("p c t -> p (c t)").bitcast(F32), ALU.subtract)\
                    .then_inc(oT_lo_ready, 1)

            def residual(j):
                dve.wait_ge(wo_done, UNITS * (j + 1))
                dve.wait_ge(xres_ready, GS * (j + 1))
                dve.wait_ge(y_done, GS * j)
                for i in range(2):
                    dve.tensor_tensor(z[:, 2 * i:2 * i + 2, :].rearrange("p s d -> p (s d)"), acc[i][:],
                                      x_res[:, 2 * i:2 * i + 2, :].rearrange("p s d -> p (s d)"), ALU.add)\
                        .then_inc(z_ready, 1)

            def residual_stats(j):
                for s in range(GS):
                    dve.wait_ge(z_ready, 2 * j + s // 2 + 1)
                    dve.bn_stats(stats[:, s, :], z[:, s, :]).then_inc(stats_ready, 1)
                dve.wait_ge(stats_ready, GS * (j + 1))
                stand_apart(dve, dve_passed)
                for s in range(GS):
                    dve.bn_aggr(mean_var[:, s, :], stats[:, s, :]).then_inc(mean_var_ready, 1)
                dve.wait_ge(mean_var_ready, GS * (j + 1))
                dve.tensor_scalar(var_eps[:], mean_var[:, :, 1], LN_EPS, None, ALU.add).then_inc(var_eps_ready, 1)
                dve.wait_ge(var_eps_ready, j + 1)
                dve.tensor_scalar(half_var[:], var_eps[:], 0.5, None, ALU.mult).then_inc(half_var_ready, 1)
                dve.tensor_scalar(half_bits[:], var_eps[:].bitcast(I32), 1, None, ALU.logical_shift_right)\
                    .then_inc(half_ready, 1)
                dve.wait_ge(half_ready, j + 1)
                dve.tensor_scalar(rstd[:].bitcast(I32), half_bits[:], -1.0, float(RSQRT_SEED), ALU.mult, ALU.add)\
                    .then_inc(seed_ready, 1)

            def masked_scores(n, u):
                dve.wait_ge(scores_done, n + 1)
                if not (isinstance(n, int) and n < 2):
                    dve.wait_ge(pT_done, n - 1)
                stand_apart(dve, dve_passed)
                for h in range(QH):
                    dve.tensor_tensor_reduce(probs[:, u % 2, h, :], score_bank[h % 2][:, (h // 2) * P:(h // 2 + 1) * P],
                                             mask[:], 1.0, MASKED, ALU.add, ALU.max, row_max[:, u % 2, h:h + 1])\
                        .then_inc(masked_done, 1)
                dve.wait_ge(masked_done, QH * (n + 1))
                dve.tensor_scalar(neg_max[:, u % 2, :], row_max[:, u % 2, :], -ATT_SCALE, 0.0, ALU.mult, ALU.min)\
                    .then_inc(neg_max_ready, 1)

            def outputs(n, u):
                dve.wait_ge(av_done, n + 1)
                dve.wait_ge(zero_exp_ready, n + 1)
                dve.scalar_tensor_tensor(denom[:], zero_exp[:, u % 2, :], float(P), av[:, :, DH],
                                         ALU.mult, ALU.add).then_inc(denom_ready, 1)
                dve.wait_ge(denom_ready, n + 1)
                dve.reciprocal(inv_denom[:], denom[:]).then_inc(inv_ready, 1)
                dve.wait_ge(inv_ready, n + 1)
                dve.tensor_tensor(o_tok[:], av[:, :, 0:DH], inv_denom[:].unsqueeze(2).to_broadcast([P, QH, DH]),
                                  ALU.mult).then_inc(o_ready, 1)

            split_weights(0)
            x_lo(0)
            for s in range(GS):
                copy_values(s, 0, s)
            split_weights(1)
            dve.wait_ge(consts, 6)
            masked_scores(0, 0)
            for q in range(2, QUADS):
                split_weights(q)
            dve.wait_ge(wo_loaded, 16)
            dve.tensor_copy(wo_hi[:], wo_raw).then_inc(wo_hi_ready, 1)
            dve.wait_ge(wo_hi_ready, 1)
            dve.tensor_tensor(wo_lo[:], wo_raw, wo_hi[:].bitcast(F32), ALU.subtract).then_inc(wo_ready, 1)

            def group(g, first=False, last=False):
                for u in range(UNITS):
                    n = g * UNITS + u
                    q, s = divmod(u, GS)
                    if not (first and u == 0):
                        output_lo(n)
                    if u == 1 and not first:
                        residual(g - 1)
                    dve.wait_ge(pT_done, n + 1)
                    dve.tensor_copy(probsT[:].rearrange("p h t -> p (h t)"), pT_bank[:]).then_inc(pT_out, 1)
                    if not (last and u == UNITS - 1):
                        masked_scores(n + 1, u + 1)
                    if not (last and q == QUADS - 1):
                        copy_values(n + GS, q + 1, s)
                    outputs(n, u)
                    if u == SWITCH and not last:
                        x_lo(g + 1)
                    if u == 2 and not first:
                        residual_stats(g - 1)

            group(0, first=True)
            with dve.Fori(1, GROUPS - 1) as g:
                group(g)
            group(GROUPS - 1, last=True)
            output_lo(GROUPS * UNITS)
            residual(GROUPS - 1)
            residual_stats(GROUPS - 1)

        @block.tensor
        def _(pe):
            def transpose_x(j):
                pe.wait_ge(x_loaded, 16 * (j + 1))
                for c, dst in enumerate((qk_bank, pT_bank)):
                    for s in range(GS):
                        last = pe.transpose(dst[:, s * P:(s + 1) * P], x_in[:, s, c * P:(c + 1) * P], ident[:])
                last.then_inc(xT_done, 1)

            def project_block(q, b):
                col = (b // OC) * INNER + q * QF + (b % OC) * P
                k = 0
                for w, xT in ((w_hi, xT_hi), (w_lo, xT_hi), (w_hi, xT_lo)):
                    for c in range(KC):
                        last = pe.matmul(qk_bank[:], w[:, c, col:col + P], xT[:, c, :], start=(k == 0),
                                         stop=(k == 3 * KC - 1))
                        k += 1
                last.then_inc(block_done, 1)

            def project_values(q, s):
                col = 2 * INNER + q * QF
                k = 0
                for w, xT in ((w_hi, xT_hi), (w_hi, xT_lo), (w_lo, xT_hi)):
                    for c in range(KC):
                        last = pe.matmul(v_bank[:, 0:QF], xT[:, c, s * P:(s + 1) * P], w[:, c, col:col + QF],
                                         start=(k == 0), stop=(k == 3 * KC - 1))
                        k += 1
                last.then_inc(v_done, 1)

            def scores(n, u):
                q, s = divmod(u % UNITS, GS)
                if s == 0:
                    pe.wait_ge(block_out, n + BLOCKS)
                pe.wait_ge(masked_done, QH * n)
                toks = slice(s * P, (s + 1) * P)
                for h in range(QH):
                    rows = slice(DH * (h % 2), DH * (h % 2 + 1))
                    last = pe.matmul(score_bank[h % 2][:, (h // 2) * P:(h // 2 + 1) * P],
                                     qkT[rows, q % 2, h // 2, toks], qkT[rows, q % 2, OC + h // 2, toks],
                                     start=True, stop=True)
                last.then_inc(scores_done, 1)

            def transpose_output(n):
                pe.wait_ge(o_ready, n + 1)
                for c in range(OC):
                    last = pe.transpose(oT_bank[:, c * P:(c + 1) * P],
                                        o_tok[:, 2 * c:2 * c + 2, :].rearrange("p h d -> p (h d)"), ident[:])
                last.then_inc(oT_done, 1)

            def project_output(n, u):
                q, s = divmod(u, GS)
                pe.wait_ge(oT_lo_ready, n)
                out = acc[s // 2][:, (s % 2) * DM:(s % 2 + 1) * DM]
                k = 0
                for oT, w in ((oT_hi, wo_hi), (oT_hi, wo_lo), (oT_lo, wo_hi)):
                    for c in range(OC):
                        last = pe.matmul(out, oT[:, c, :], w[:, OC * q + c, :],
                                         start=(q == 0 and s % 2 == 0 and k == 0),
                                         stop=(q == QUADS - 1 and k == 3 * OC - 1), skip_group_check=True)
                        k += 1
                last.then_inc(wo_done, 1)

            pe.wait_ge(consts, 6)
            transpose_x(0)
            pe.wait_ge(w_ready, 3)
            pe.wait_ge(xT_lo_ready, KC)
            for k in range(AHEAD):
                if k:
                    pe.wait_ge(block_out, k)
                if k == BLOCKS:
                    pe.wait_ge(w_ready, 6)
                project_block(k // BLOCKS, k % BLOCKS)
                if k < GS:
                    if k:
                        pe.wait_ge(v_out, k)
                    project_values(0, k)
            scores(0, 0)

            def group(g, first=False, last=False):
                for u in range(UNITS):
                    n = g * UNITS + u
                    q, s = divmod(u, GS)
                    pe.wait_ge(exp_done, QH * (n + 1))
                    pe.wait_ge(pT_out, n)
                    if u == SWITCH + 1 and not last:
                        pe.wait_ge(xT_lo_ready, KC * (g + 2))
                    for h in range(QH):
                        last_mm = pe.transpose(pT_bank[:, h * P:(h + 1) * P], probs[:, u % 2, h, :], ident[:])
                    last_mm.then_inc(pT_done, 1)
                    if not (last and u == UNITS - 1):
                        scores(n + 1, u + 1)
                    if not (last and q == QUADS - 1):
                        if first and s == 0:
                            pe.wait_ge(w_ready, 3 * min(q + 2, QUADS))
                        if not (first and u == 0):
                            pe.wait_ge(oT_lo_ready, n)
                        pe.wait_ge(v_out, n + GS)
                        project_values((q + 1) % QUADS, s)
                    if u == SWITCH and not last:
                        pe.wait_ge(block_out, n + AHEAD)
                        pe.wait_ge(pT_out, n + 1)
                        transpose_x(g + 1)
                    pe.wait_ge(pT_out, n + 1)
                    if s == 0:
                        pe.wait_ge(v_out, GS * (g * QUADS + q + 1))
                    for h in range(QH):
                        last_mm = pe.matmul(av[:, h, :], probsT[:, h, :], v_one[:, q % 2, s, h, :],
                                            start=True, stop=True)
                    last_mm.then_inc(av_done, 1)

                    def next_block():
                        if not (last and u + AHEAD >= UNITS):
                            pe.wait_ge(block_out, n + AHEAD)
                            if u == SWITCH:
                                pe.wait_ge(xT_lo_ready, KC * (g + 2))
                            if first and s == GS - 1 and u < SWITCH:
                                pe.wait_ge(w_ready, 3 * min(q + 3, QUADS))
                            project_block((u + AHEAD) // BLOCKS % QUADS, (u + AHEAD) % BLOCKS)

                    if u != SWITCH:
                        next_block()
                    if not (first and u == 0):
                        if first and u == 1:
                            pe.wait_ge(wo_ready, 1)
                        if not first and u == 1:
                            pe.wait_ge(z_ready, 2 * g)
                        project_output(n, (u - 1) % UNITS)
                    transpose_output(n)
                    if u == SWITCH:
                        next_block()

            group(0, first=True)
            with pe.Fori(1, GROUPS - 1) as g:
                group(g)
            group(GROUPS - 1, last=True)
            project_output(GROUPS * UNITS, UNITS - 1)

        blocks.close()
        with nc.Block() as clearing:
            @clearing.gpsimd
            def _(pool):
                pool.sem_clear(range(w_loaded[0].num, pool_passed.num + 1))


def mlstm_and_experts(nc, out, y1, ctx_in, w_i, b_i, w_f, b_f, ln_w, w_r, b_r, w_gu, b_gu, w_d, b_d):
    with ExitStack() as ctx:
        def sb(name, shape, dt=F32):
            return ctx.enter_context(nc.sbuf_tensor(name, shape, dt))

        def bank(name):
            return ctx.enter_context(nc.psum_tensor(name, [P, 512], F32))

        def sem(name):
            return ctx.enter_context(nc.semaphore(name))

        gu_hi = sb("gu_hi", [P, E, KC, 2 * FI], F32R)
        gu_lo = sb("gu_lo", [P, E, KC, 2 * FI], F32R)
        d_hi = sb("d_hi", [P, E, FB, DM], F32R)
        d_lo = sb("d_lo", [P, E, FB, DM], F32R)
        gu_bias = sb("gu_bias", [P, E * 2 * FB])
        d_bias = sb("d_bias", [GS * E, GS, DM])
        r_hi = sb("r_hi", [P, KC, E], F32R)
        r_lo = sb("r_lo", [P, KC, E], F32R)
        r_bias = sb("r_bias", [P, E])
        row_all = sb("row_all", [P, E + 2 * MH + DM])
        gate_T = sb("gate_T", [P, 3 * KC, 2 * MH])
        gate_w = sb("gate_w", [P, 2 * KC, 2 * MH])
        gate_bias = row_all[:, E:E + 2 * MH]
        head_scale = sb("head_scale", [P, DM])
        ident = sb("ident2", [P, P])
        ident_b = sb("ident_b", [P, P], BF16)
        ones_to = sb("ones_to", [P, P])
        after_b = sb("after_b", [P, MH, P], BF16)
        neg_sel_f = sb("neg_sel_f", [48, PAIRS])
        neg_sel = sb("neg_sel", [48, PAIRS, P], F32R)
        before = sb("before", [P, E, E])
        behind = sb("behind", [P, E, E])
        acc = sb("acc", [P, GS, DM])
        y_out = sb("y_out2", [P, GS, DM])
        gu_raw = y_out[:].rearrange("p s d -> p (s d)").rearrange("p (c n) -> p c n", c=KC)
        d_raw = sb("d_raw", [P, FB, DM])
        y_in = sb("y_in", [P, GS, DM])
        y_res = sb("y_res", [P, GS, DM])
        c_in = sb("c_in", [P, GS, DM])
        c_one = sb("c_one", [P, GS, MH, MD + 1])
        ycT = sb("ycT", [P, GS, 2 * KC, P])
        gates_by_row = sb("gates_by_row", [2 * MH, GT])
        gates = sb("gates", [P, GS, 2 * MH])
        abs_f = sb("abs_f", [P, GS, MH])
        soft = sb("soft", [P, GS, MH])
        log_f = sb("log_f", [P, GS, MH])
        cum_f = sb("cum_f", [P, PAIRS])
        a_tok = sb("a_tok", [P, PAIRS])
        a_rows = sb("a_rows", [PAIRS, P])
        m_rows = sb("m_rows", [PAIRS, P])
        m_split = sb("m_split", [48, P], F32R)
        max_log = sb("max_log", [P, PAIRS])
        floor = sb("floor", [P, PAIRS])
        decay = sb("decay", [P, MH, P])
        cmat = sb("cmat", [P, MH, P])
        norm_abs = sb("norm_abs", [P, MH])
        norm_max = sb("norm_max", [P, MH])
        norm_inv = sb("norm_inv", [P, MH])
        y2 = sb("y2", [P, GS, DM])
        h_stats = sb("h_stats", [P, MH, 6])
        h_mv = sb("h_mv", [P, PAIRS, 2])
        h_var = sb("h_var", [P, PAIRS])
        h_half = sb("h_half", [P, PAIRS], I32)
        h_rstd = sb("h_rstd", [P, PAIRS])
        h_hvar = sb("h_hvar", [P, PAIRS])
        h_tmp = sb("h_tmp", [P, PAIRS])
        l_stats = sb("l_stats", [P, GS, 6])
        l_mv = sb("l_mv", [P, GS, 2])
        l_var = sb("l_var", [P, GS])
        l_half = sb("l_half", [P, GS], I32)
        l_rstd = sb("l_rstd", [P, GS])
        l_hvar = sb("l_hvar", [P, GS])
        l_tmp = sb("l_tmp", [P, GS])
        l_shift = sb("l_shift", [P, GS])
        yT_hi = sb("yT_hi", [P, KC, GT], F32R)
        yT_lo = sb("yT_lo", [P, KC, GT], F32R)
        logits = sb("logits", [P, GS, E])
        beats = sb("beats", [P, GS * E, E])
        ties = sb("ties", [P, GS * E, E])
        rank = sb("rank", [P, GS * E])
        top = sb("top", [P, GS * E])
        peak = sb("peak", [P, GS])
        r_exp = sb("r_exp", [P, GS, E])
        r_sum = sb("r_sum", [P, GS])
        r_inv = sb("r_inv", [P, GS])
        share = sb("share", [P, GS, E])
        half_share = sb("half_share", [P, GS, E])
        share_T = sb("share_T", [GS * E, P])
        gate = sb("gate", [P, FB, GT])
        tanh = sb("tanh", [P, FB, GT])
        up = sb("up", [P, FB, GT])
        gate_rows = gate[0:2 * MH].rearrange("p f t -> p (f t)")[:, 0:3 * DM]
        row = up[0:1].rearrange("p f t -> p (f t)")[:, 0:E + 2 * MH + DM]
        r_rows = tanh[0:E].rearrange("p f t -> p (f t)")[:, 0:DM]
        gu_bias_rows = tanh[0:E * 2 * FB].rearrange("p f t -> p (f t)")[:, DM:DM + P]
        act_hi = sb("act_hi", [P, 2, FB, GT], F32R)
        act_lo = sb("act_lo", [P, 2, FB, GT], F32R)
        e_stats = sb("e_stats", [P, GS, 6])
        e_mv = sb("e_mv", [P, GS, 2])
        e_var = sb("e_var", [P, GS])
        e_half = sb("e_half", [P, GS], I32)
        e_rstd = sb("e_rstd", [P, GS])
        e_hvar = sb("e_hvar", [P, GS])
        e_tmp = sb("e_tmp", [P, GS])
        e_shift = sb("e_shift", [P, GS])
        three_halves = sb("three_halves2", [P, PAIRS])

        up_bank = [bank(f"up_bank{i}") for i in range(2)]
        down_bank = [bank(f"down_bank{i}") for i in range(2)]
        pair_bank = [bank(f"pair_bank{i}") for i in range(2)]
        log_bank = bank("log_bank")
        small_bank = bank("small_bank")
        head_out = small_bank[:, 0:MH * (MD + 1)].rearrange("p (h d) -> p h d", h=MH)
        gates_ps = small_bank[:, 0:GS * 2 * MH].rearrange("p (s k) -> p s k", s=GS)
        logits_ps = small_bank[:, 0:GS * E].rearrange("p (s e) -> p s e", s=GS)

        names = """gu_loaded d_loaded r_loaded gbias_loaded gate_loaded row_loaded dbias_loaded
            y_loaded yres_loaded cin_loaded c_loaded consts setup_T setup_out row_ready gate_w_ready gu_hi_ready gu_ready d_hi_ready
            d_ready yc_done yc_out rows_done rows_out gates_done gates_ready gate_out abs_ready gate_exp soft_ready log_f_ready cum_done
            cum_ready a_ready aT_done a_rows_ready m_ready m_hi_ready m_lo_ready mT_done max_log_ready
            floor_exp floor_ready log_done decay_ready qk_done cmat_ready av_done abs_norm norm_ready inv_ready
            h_ready h_stats_ready h_mv_ready h_var_ready h_half_ready h_seed h_newton h_norm h_scaled z_ready
            l_stats_ready l_mv_ready l_var_ready l_half_ready l_seed l_newton y2_ready yT_done yT_hi_ready
            yT_lo_ready logits_done logits_ready beats_raw ties_raw beats_cut ties_cut beats_sum rank_ready
            top_ready peak_ready shifted r_exp_ready r_sum_ready r_inv_ready top_exp share_ready
            half_share_ready shareT_done shareT_out dbias_done acc_ready up_done gate_ready tanh_ready
            up_ready clip_ready tanh_gate act_ready act_hi_ready act_lo_ready down_done added e_stats_ready
            e_mv_ready e_var_ready e_half_ready e_seed e_newton y_done y_stored
            h_half_var l_half_var e_half_var h_centred l_shifted e_shifted dve_passed pool_passed pe_passed"""
        S = {n: sem("m_" + n) for n in names.split()}

        block = ctx.enter_context(nc.Block())

        def rows_of(t, j):
            return t[bass.ds(j * GS, GS)].rearrange("b t d -> t b d")

        @block.sync
        def _(sp):
            def load_gates(j):
                sp.dma_start(y_in[:], rows_of(y1, j)).then_inc(S["y_loaded"], 16)
                sp.dma_start(c_in[:], rows_of(ctx_in, j)).then_inc(S["cin_loaded"], 16)

            def load_heads(j):
                sp.dma_start(y_res[:], rows_of(y1, j)).then_inc(S["yres_loaded"], 16)
                for s in range(GS):
                    sp.dma_start(c_one[:, s, :, 0:MD],
                                 ctx_in[bass.ds(j * GS + s, 1)].rearrange("b t (h d) -> (b t) h d", h=MH))\
                        .then_inc(S["c_loaded"], 16)

            sp.dma_start(gate_rows[0:MH, :], w_i).then_inc(S["gate_loaded"], 16)
            sp.dma_start(gate_rows[MH:2 * MH, :], w_f).then_inc(S["gate_loaded"], 16)
            for src, at, n in ((b_r, 0, E), (b_i, E, MH), (b_f, E + MH, MH), (ln_w, E + 2 * MH, DM)):
                sp.dma_start(row[:, at:at + n], src.rearrange("(a n) -> a n", a=1)).then_inc(S["row_loaded"], 16)
            sp.dma_start(r_rows, w_r).then_inc(S["r_loaded"], 16)
            sp.dma_start(gu_bias_rows, b_gu.rearrange("e (b p) -> (e b) p", p=P)).then_inc(S["gbias_loaded"], 16)
            load_gates(0)
            load_heads(0)
            sp.wait_ge(S["consts"], 2)
            for s in range(GS):
                sp.dma_start(d_bias[s * E:(s + 1) * E, s, :], b_d).then_inc(S["dbias_loaded"], 16)

            def load_expert(e):
                if e:
                    sp.wait_ge(S["gu_ready"], e)
                    sp.wait_ge(S["d_ready"], e)
                sp.dma_start(gu_raw, w_gu[e].rearrange("(c p) n -> p c n", p=P)).then_inc(S["gu_loaded"], 16)
                sp.dma_start(d_raw[:], w_d[e].rearrange("(c p) n -> p c n", p=P)).then_inc(S["d_loaded"], 16)

            load_expert(0)
            sp.wait_ge(S["yc_done"], GS)
            load_gates(1)
            load_expert(1)

            def group(g):
                sp.wait_ge(S["yc_done"], GS * (g + 2))
                load_gates(g + 2)
                sp.wait_ge(S["z_ready"], GS * (g + 2))
                load_heads(g + 2)
                store(g)

            def store(g):
                sp.wait_ge(S["y_done"], GS * (g + 1))
                sp.dma_start(rows_of(out, g), y_out[:]).then_inc(S["y_stored"], 16)

            sp.wait_ge(S["z_ready"], GS)
            load_heads(1)
            sp.wait_ge(S["yc_done"], GS * 2)
            load_gates(2)
            for e in range(2, E):
                load_expert(e)
            sp.wait_ge(S["z_ready"], GS * 2)
            load_heads(2)
            store(0)
            with sp.Fori(1, GROUPS - 2) as g:
                group(g)
            store(GROUPS - 2)
            store(GROUPS - 1)
            sp.wait_ge(S["y_stored"], 16 * GROUPS)

        @block.gpsimd
        def _(pool):
            pool.memset(d_bias[:], 0.0).then_inc(S["consts"], 1)
            pool.memset(c_one[:, :, :, MD:MD + 1].rearrange("p s h d -> p (s h d)"), 1.0).then_inc(S["consts"], 1)
            pool.memset(ident[:], 0.0).then_inc(S["consts"], 1)
            pool.memset(ones_to[:], 1.0).then_inc(S["consts"], 1)
            pool.memset(after_b[:], 0.0).then_inc(S["consts"], 1)
            pool.memset(neg_sel_f[:], 0.0).then_inc(S["consts"], 1)
            pool.memset(before[:], 0.0).then_inc(S["consts"], 1)
            pool.memset(behind[:], 0.0).then_inc(S["consts"], 1)
            pool.memset(three_halves[:], 1.5).then_inc(S["consts"], 1)
            pool.wait_ge(S["consts"], 9)
            pool.affine_select(out=ident[:], in_=ident[:], compare_op=ALU.not_equal, fill=1.0, base=0,
                               pattern=[[-1, P]], channel_multiplier=1).then_inc(S["consts"], 1)
            pool.affine_select(out=ones_to[:], in_=ones_to[:], compare_op=ALU.is_ge, fill=0.0, base=0,
                               pattern=[[1, P]], channel_multiplier=-1).then_inc(S["consts"], 1)
            pool.affine_select(out=after_b[:], in_=after_b[:], compare_op=ALU.is_ge, fill=MASKED, base=0,
                               pattern=[[0, MH], [1, P]], channel_multiplier=-1).then_inc(S["consts"], 1)
            pool.affine_select(out=before[:], in_=before[:], compare_op=ALU.is_ge, fill=1.0, base=0,
                               pattern=[[-1, E], [1, E]], channel_multiplier=0).then_inc(S["consts"], 1)
            pool.affine_select(out=behind[:], in_=behind[:], compare_op=ALU.is_ge, fill=1.0, base=0,
                               pattern=[[1, E], [-1, E]], channel_multiplier=0).then_inc(S["consts"], 1)
            for k, at in enumerate((0, 32)):
                pool.affine_select(out=neg_sel_f[:], in_=neg_sel_f[:], compare_op=ALU.not_equal, fill=-1.0,
                                   base=-at, pattern=[[-1, PAIRS]], channel_multiplier=1).then_inc(S["consts"], 1)
                pool.wait_ge(S["consts"], 15 + k)
            pool.wait_ge(S["row_loaded"], 64)
            pool.partition_broadcast(row_all[:], row).then_inc(S["row_ready"], 1)
            pool.wait_ge(S["row_ready"], 1)
            pool.tensor_scalar(head_scale[:], row_all[:, E + 2 * MH:], 1.0, None, ALU.add).then_inc(S["row_ready"], 1)

            def head_scales(j):
                pool.wait_ge(S["h_half_var"], j + 1)
                pool.wait_ge(S["h_seed"], j + 1)
                newton_rsqrt(pool, S["h_newton"], NEWTON_OPS * j, h_rstd[:], h_hvar[:], h_tmp[:], three_halves[:])
                heads = y2[:].rearrange("p s (h d) -> p (s h) d", h=MH)
                for k in range(2):
                    part = slice(k * PAIRS // 2, (k + 1) * PAIRS // 2)
                    pool.tensor_tensor(heads[:, part], heads[:, part],
                                       h_mv[:, part, 0:1].to_broadcast([P, PAIRS // 2, MD]), ALU.subtract)\
                        .then_inc(S["h_centred"], 1)
                pool.wait_ge(S["h_newton"], NEWTON_OPS * (j + 1))
                for k in range(2):
                    part = slice(k * PAIRS // 2, (k + 1) * PAIRS // 2)
                    pool.wait_ge(S["h_centred"], 2 * j + k + 1)
                    pool.tensor_tensor(heads[:, part], heads[:, part],
                                       h_rstd[:, part].unsqueeze(2).to_broadcast([P, PAIRS // 2, MD]), ALU.mult)\
                        .then_inc(S["h_norm"], 1)

            def residual(j):
                pool.wait_ge(S["yres_loaded"], 16 * (j + 1))
                for s in range(GS):
                    n = j * GS + s
                    pool.wait_ge(S["h_norm"], 2 * j + s // 2 + 1)
                    pool.tensor_tensor(y2[:, s, :], y2[:, s, :], head_scale[:], ALU.mult).then_inc(S["h_scaled"], 1)
                for s in range(GS):
                    n = j * GS + s
                    pool.wait_ge(S["h_scaled"], n + 1)
                    pool.tensor_tensor(y2[:, s, :], y2[:, s, :], y_res[:, s, :], ALU.add).then_inc(S["z_ready"], 1)

            def layer_scales(j):
                pool.wait_ge(S["l_half_var"], j + 1)
                pool.wait_ge(S["l_seed"], j + 1)
                newton_rsqrt(pool, S["l_newton"], NEWTON_OPS * j, l_rstd[:], l_hvar[:], l_tmp[:], three_halves[:, 0:GS])
                norm_shift(pool, S["l_shifted"], 2 * j, l_shift[:], l_mv[:, :, 0], l_rstd[:], S["pool_passed"])

            def lower_act(g, e):
                for fb in range(FB):
                    n = (g * E + e) * FB + fb
                    pool.wait_ge(S["act_hi_ready"], n + 1)
                    pool.tensor_tensor(act_lo[:, e % 2, fb, :], tanh[:, fb, :], act_hi[:, e % 2, fb, :].bitcast(F32),
                                       ALU.subtract).then_inc(S["act_lo_ready"], 1)

            def output_scales(g):
                pool.wait_ge(S["e_half_var"], g + 1)
                pool.wait_ge(S["e_seed"], g + 1)
                newton_rsqrt(pool, S["e_newton"], NEWTON_OPS * g, e_rstd[:], e_hvar[:], e_tmp[:], three_halves[:, 0:GS])
                norm_shift(pool, S["e_shifted"], 2 * g, e_shift[:], e_mv[:, :, 0], e_rstd[:], S["pool_passed"])

            def heads_part(j, e):
                if e == GS:
                    head_scales(j)
                if e == GS + 1:
                    residual(j)
                if e == GS + 2:
                    layer_scales(j)

            def lower_weights(e):
                pool.wait_ge(S["gu_hi_ready"], e + 1)
                pool.tensor_tensor(gu_lo[:, e], gu_raw, gu_hi[:, e].bitcast(F32), ALU.subtract)\
                    .then_inc(S["gu_ready"], 1)
                pool.wait_ge(S["d_hi_ready"], e + 1)
                pool.tensor_tensor(d_lo[:, e], d_raw[:], d_hi[:, e].bitcast(F32), ALU.subtract)\
                    .then_inc(S["d_ready"], 1)

            def body(g, heads=True, split=False):
                for e in range(E):
                    if heads:
                        heads_part(g + 1, e)
                    if split and e + 1 < E:
                        lower_weights(e + 1)
                    lower_act(g, e)
                output_scales(g)

            lower_weights(0)
            for e in range(E):
                heads_part(0, e)
            body(0, split=True)
            with pool.Fori(1, GROUPS - 1) as g:
                body(g)
            body(GROUPS - 1, heads=False)

        @block.scalar
        def _(act):
            act.wait_ge(S["setup_T"], 1)
            act.activation(gate_T[:].rearrange("p c k -> p (c k)"), small_bank[:, 0:3 * KC * 2 * MH], ACT.Copy)\
                .then_inc(S["setup_out"], 1)
            act.activation(gu_bias[:], small_bank[:, 64:64 + E * 2 * FB], ACT.Copy).then_inc(S["setup_out"], 1)
            act.activation(r_hi[:].rearrange("p c e -> p (c e)"), small_bank[:, 128:128 + KC * E], ACT.Copy)\
                .then_inc(S["setup_out"], 1)

            def take_transposes(j, sequences):
                for s in sequences:
                    act.wait_ge(S["yc_done"], j * GS + s + 1)
                    act.activation(ycT[:, s, :, :].rearrange("p c t -> p (c t)"), pair_bank[s % 2][:], ACT.Copy)\
                        .then_inc(S["yc_out"], 1)

            def gates_mid(j, e):
                if e == T_SLOT:
                    take_transposes(j, range(GS // 2))
                if e == T_SLOT + 1:
                    act.wait_ge(S["rows_done"], j + 1)
                    act.activation(gates_by_row[:], log_bank[0:2 * MH, :], ACT.Copy).then_inc(S["rows_out"], 1)
                if e == T_SLOT + 2:
                    act.wait_ge(S["abs_ready"], j + 1)
                    act.activation(soft[:], abs_f[:], ACT.Exp, scale=-1.0).then_inc(S["gate_exp"], 1)
                    act.wait_ge(S["gate_exp"], j + 1)
                    act.activation(soft[:], soft[:], ACT.Ln, bias=1.0).then_inc(S["soft_ready"], 1)

            def gates_end(j, e):
                if e == T_SLOT:
                    take_transposes(j, range(GS // 2, GS))

            def heads_a(j, e):
                if e == 0:
                    act.wait_ge(S["max_log_ready"], j + 1)
                    act.activation(floor[:], max_log[:], ACT.Exp, scale=-1.0).then_inc(S["floor_exp"], 1)
                if e < GS:
                    n = j * GS + e
                    act.wait_ge(S["log_done"], n + 1)
                    act.wait_ge(S["cmat_ready"], 2 * n)
                    for h in range(MH):
                        act.activation(decay[:, h, :], log_bank[:, h * P:(h + 1) * P], ACT.Exp,
                                       bias=a_tok[:, e * MH + h:e * MH + h + 1]).then_inc(S["decay_ready"], 1)

            def heads_b(j, e):
                if e < GS:
                    n = j * GS + e
                    act.wait_ge(S["av_done"], n + 1)
                    act.wait_ge(S["norm_ready"], n)
                    act.activation(norm_abs[:], head_out[:, :, MD], ACT.Abs).then_inc(S["abs_norm"], 1)
                if e == GS + 2:
                    act.wait_ge(S["l_newton"], NEWTON_OPS * (j + 1))
                    act.wait_ge(S["l_shifted"], 2 * (j + 1))
                    for s in range(GS):
                        act.activation(y2[:, s, :], y2[:, s, :], ACT.Identity, bias=l_shift[:, s:s + 1],
                                       scale=l_rstd[:, s:s + 1]).then_inc(S["y2_ready"], 1)

            def take_gate(g, e, fb):
                n = (g * E + e) * FB + fb
                act.wait_ge(S["up_done"], 2 * n + 1)
                if not (isinstance(g, int) and g == 0 and e == 0):
                    act.wait_ge(S["tanh_gate"], n - FB + 1)
                act.activation(gate[:, fb, :], up_bank[0][:], ACT.Identity,
                               bias=gu_bias[:, e * 2 * FB + fb:e * 2 * FB + fb + 1]).then_inc(S["gate_out"], 1)

            def take_up(g, e, fb):
                n = (g * E + e) * FB + fb
                act.wait_ge(S["up_done"], 2 * n + 2)
                if not (isinstance(g, int) and g == 0 and e == 0):
                    act.wait_ge(S["act_ready"], n - FB + 1)
                act.activation(up[:, fb, :], up_bank[1][:], ACT.Identity,
                               bias=gu_bias[:, e * 2 * FB + FB + fb:e * 2 * FB + FB + fb + 1])\
                    .then_inc(S["up_ready"], 1)

            def gate_tanh(g, e, fb):
                n = (g * E + e) * FB + fb
                act.wait_ge(S["gate_ready"], n + 1)
                if not (isinstance(g, int) and g == 0 and e == 0):
                    act.wait_ge(S["act_lo_ready"], n - FB + 1)
                act.activation(tanh[:, fb, :], gate[:, fb, :], ACT.Tanh, scale=ALPHA / 2)\
                    .then_inc(S["tanh_ready"], 1)

            def upper_act(g, e, fb):
                n = (g * E + e) * FB + fb
                act.wait_ge(S["act_ready"], n + 1)
                act.activation(act_hi[:, e % 2, fb, :], tanh[:, fb, :], ACT.Copy).then_inc(S["act_hi_ready"], 1)

            def transposed_y2(j):
                act.wait_ge(S["yT_done"], j + 1)
                for c in range(KC):
                    act.activation(yT_hi[:, c, :], pair_bank[c][:], ACT.Copy).then_inc(S["yT_hi_ready"], 1)

            def raise_weights(e):
                act.wait_ge(S["gu_loaded"], 16 * (e + 1))
                act.activation(gu_hi[:, e], gu_raw, ACT.Copy).then_inc(S["gu_hi_ready"], 1)
                act.wait_ge(S["d_loaded"], 16 * (e + 1))
                act.activation(d_hi[:, e], d_raw[:], ACT.Copy).then_inc(S["d_hi_ready"], 1)

            def router_exp(j):
                act.wait_ge(S["shifted"], j + 1)
                act.activation(r_exp[:], r_exp[:], ACT.Exp).then_inc(S["r_exp_ready"], 1)

            def output_norm(g):
                act.wait_ge(S["e_newton"], NEWTON_OPS * (g + 1))
                act.wait_ge(S["e_shifted"], 2 * (g + 1))
                if not (isinstance(g, int) and g == 0):
                    act.wait_ge(S["y_stored"], 16 * g)
                for s in range(GS):
                    act.activation(y_out[:, s, :], acc[:, s, :], ACT.Identity, bias=e_shift[:, s:s + 1],
                                   scale=e_rstd[:, s:s + 1]).then_inc(S["y_done"], 1)

            def share_transposed(g):
                act.wait_ge(S["shareT_done"], g + 1)
                act.activation(share_T[:], small_bank[0:GS * E, 0:P], ACT.Copy).then_inc(S["shareT_out"], 1)

            for e in range(T_SLOT, E):
                gates_mid(0, e)
                gates_end(0, e)
            raise_weights(0)
            for e in range(GS):
                heads_a(0, e)
                heads_b(0, e)
            for e in range(T_SLOT, E):
                gates_mid(1, e)
                gates_end(1, e)
            for e in range(GS, E):
                heads_a(0, e)
                heads_b(0, e)
            transposed_y2(0)
            router_exp(0)

            def body(g, before=True, heads=True, gates=True, split=False):
                for e in range(E):
                    if heads:
                        heads_a(g + 1, e)
                    if split and e + 1 < E:
                        raise_weights(e + 1)
                    take_gate(g, e, 0)
                    take_up(g, e, 0)
                    gate_tanh(g, e, 0)
                    if gates:
                        gates_mid(g + 2, e)
                    if e == 0:
                        share_transposed(g)
                    take_gate(g, e, 1)
                    take_up(g, e, 1)
                    gate_tanh(g, e, 1)
                    if e == 0 and before:
                        output_norm(g - 1)
                    upper_act(g, e, 0)
                    if heads:
                        heads_b(g + 1, e)
                    if gates:
                        gates_end(g + 2, e)
                    upper_act(g, e, 1)
                if heads:
                    transposed_y2(g + 1)
                    router_exp(g + 1)

            body(0, before=False, split=True)
            with act.Fori(1, GROUPS - 2) as g:
                body(g)
            body(GROUPS - 2, gates=False)
            body(GROUPS - 1, heads=False, gates=False)
            output_norm(GROUPS - 1)

        @block.vector
        def _(dve):
            dve.memset(m_split[:].bitcast(F32), 0.0).then_inc(S["m_lo_ready"], 1)
            dve.wait_ge(S["consts"], 16)
            dve.tensor_copy(neg_sel[:], neg_sel_f[:].unsqueeze(2).to_broadcast([48, PAIRS, P]))\
                .then_inc(S["gate_w_ready"], 1)
            dve.tensor_copy(ident_b[:], ident[:]).then_inc(S["gate_w_ready"], 1)
            dve.wait_ge(S["setup_out"], 3)
            dve.tensor_copy(gate_w[:, 0:KC, :], gate_T[:, 0:KC, :]).then_inc(S["gate_w_ready"], 1)
            dve.tensor_tensor(gate_w[:, KC:2 * KC, :], gate_T[:, KC:2 * KC, :], gate_T[:, 2 * KC:3 * KC, :], ALU.add)\
                .then_inc(S["gate_w_ready"], 1)
            dve.tensor_tensor(r_lo[:].rearrange("p c e -> p (c e)"), small_bank[:, 128:128 + KC * E],
                              r_hi[:].rearrange("p c e -> p (c e)").bitcast(F32), ALU.subtract)\
                .then_inc(S["gate_w_ready"], 1)
            dve.wait_ge(S["row_ready"], 2)

            def seed(var, half_var, mv, half, rstd, k, ready, n):
                dve.wait_ge(S[k + "_mv_ready"], ready)
                dve.tensor_scalar(var, mv, LN_EPS, None, ALU.add).then_inc(S[k + "_var_ready"], 1)
                dve.wait_ge(S[k + "_var_ready"], n + 1)
                dve.tensor_scalar(half_var, var, 0.5, None, ALU.mult).then_inc(S[k + "_half_var"], 1)
                dve.tensor_scalar(half, var.bitcast(I32), 1, None, ALU.logical_shift_right)\
                    .then_inc(S[k + "_half_ready"], 1)
                dve.wait_ge(S[k + "_half_ready"], n + 1)
                dve.tensor_scalar(rstd.bitcast(I32), half, -1.0, float(RSQRT_SEED), ALU.mult, ALU.add)\
                    .then_inc(S[k + "_seed"], 1)

            def gates_mid(j, e):
                if e == T_SLOT + 3:
                    dve.wait_ge(S["cum_done"], j + 1)
                    dve.tensor_copy(cum_f[:], small_bank[:, 0:PAIRS]).then_inc(S["cum_ready"], 1)
                    dve.wait_ge(S["cum_ready"], j + 1)
                    dve.tensor_tensor(a_tok[:].rearrange("p (s h) -> p s h", s=GS), gates[:, :, 0:MH],
                                      cum_f[:].rearrange("p (s h) -> p s h", s=GS), ALU.subtract)\
                        .then_inc(S["a_ready"], 1)

            def gates_end(j, e):
                if e == T_SLOT + 1:
                    dve.wait_ge(S["gates_done"], j + 1)
                    dve.tensor_tensor(gates[:], gates_ps, gate_bias.unsqueeze(1).to_broadcast([P, GS, 2 * MH]), ALU.add)\
                        .then_inc(S["gates_ready"], 1)
                    dve.wait_ge(S["gates_ready"], j + 1)
                    dve.scalar_tensor_tensor(abs_f[:], gates[:, :, MH:], -1.0, gates[:, :, MH:], ALU.mult, ALU.max)\
                        .then_inc(S["abs_ready"], 1)
                if e == T_SLOT + 2:
                    dve.wait_ge(S["soft_ready"], j + 1)
                    dve.scalar_tensor_tensor(log_f[:], gates[:, :, MH:], 0.0, soft[:], ALU.min, ALU.subtract)\
                        .then_inc(S["log_f_ready"], 1)
                if e == T_SLOT + 3:
                    dve.wait_ge(S["aT_done"], j + 1)
                    dve.tensor_copy(a_rows[:], small_bank[0:PAIRS, 0:P]).then_inc(S["a_rows_ready"], 1)
                    dve.wait_ge(S["a_rows_ready"], j + 1)
                    dve.tensor_tensor_scan(m_rows[:], a_rows[:], a_rows[:], MASKED, ALU.max, ALU.max)\
                        .then_inc(S["m_ready"], 1)
                    dve.wait_ge(S["m_ready"], j + 1)
                    dve.tensor_copy(m_split[0:PAIRS, :], m_rows[:]).then_inc(S["m_hi_ready"], 1)
                    dve.wait_ge(S["m_hi_ready"], j + 1)
                    dve.tensor_tensor(m_split[32:32 + PAIRS, :], m_rows[:], m_split[0:PAIRS, :].bitcast(F32),
                                      ALU.subtract).then_inc(S["m_lo_ready"], 1)

            def largest_log(j):
                dve.wait_ge(S["mT_done"], j + 1)
                dve.tensor_tensor(max_log[:], small_bank[:, 0:PAIRS], cum_f[:], ALU.add)\
                    .then_inc(S["max_log_ready"], 1)

            def heads_a(j, e):
                if e < GS:
                    n = j * GS + e
                    dve.wait_ge(S["qk_done"], n + 1)
                    dve.wait_ge(S["decay_ready"], MH * (n + 1))
                    dve.wait_ge(S["av_done"], n)
                    for i in range(2):
                        dve.scalar_tensor_tensor(cmat[:, i::2, :],
                                                 pair_bank[i][:, 0:2 * P].rearrange("p (h t) -> p h t", h=2),
                                                 QK_SCALE, decay[:, i::2, :], ALU.mult, ALU.mult)\
                            .then_inc(S["cmat_ready"], 1)

            def heads_b(j, e):
                if e < GS:
                    s = e
                    n = j * GS + s
                    if s == 0:
                        dve.wait_ge(S["floor_exp"], j + 1)
                        dve.tensor_scalar(floor[:], floor[:], NORM_EPS, None, ALU.add).then_inc(S["floor_ready"], 1)
                        dve.wait_ge(S["floor_ready"], j + 1)
                    dve.wait_ge(S["abs_norm"], n + 1)
                    dve.scalar_tensor_tensor(norm_max[:], norm_abs[:], NORM_EPS, floor[:, s * MH:(s + 1) * MH],
                                             ALU.add, ALU.max).then_inc(S["norm_ready"], 1)
                    dve.wait_ge(S["norm_ready"], n + 1)
                    dve.reciprocal(norm_inv[:], norm_max[:]).then_inc(S["inv_ready"], 1)
                    dve.wait_ge(S["inv_ready"], n + 1)
                    if s == 0:
                        dve.wait_ge(S["acc_ready"], 2 * j)
                    dve.tensor_tensor(y2[:, s, :].rearrange("p (h d) -> p h d", h=MH), head_out[:, :, 0:MD],
                                      norm_inv[:].unsqueeze(2).to_broadcast([P, MH, MD]), ALU.mult)\
                        .then_inc(S["h_ready"], 1)
                    dve.wait_ge(S["h_ready"], n + 1)
                    for h in range(MH):
                        dve.bn_stats(h_stats[:, h, :], y2[:, s, h * MD:(h + 1) * MD]).then_inc(S["h_stats_ready"], 1)
                    dve.wait_ge(S["h_stats_ready"], MH * (n + 1))
                    stand_apart(dve, S["dve_passed"])
                    for h in range(MH):
                        dve.bn_aggr(h_mv[:, s * MH + h, :], h_stats[:, h, :]).then_inc(S["h_mv_ready"], 1)
                if e == GS - 1:
                    seed(h_var[:], h_hvar[:], h_mv[:, :, 1], h_half[:], h_rstd[:], "h", PAIRS * (j + 1), j)
                if e == GS + 1:
                    for s in range(GS):
                        dve.wait_ge(S["z_ready"], GS * j + s + 1)
                        dve.bn_stats(l_stats[:, s, :], y2[:, s, :]).then_inc(S["l_stats_ready"], 1)
                    dve.wait_ge(S["l_stats_ready"], GS * (j + 1))
                    stand_apart(dve, S["dve_passed"])
                    for s in range(GS):
                        dve.bn_aggr(l_mv[:, s, :], l_stats[:, s, :]).then_inc(S["l_mv_ready"], 1)
                    seed(l_var[:], l_hvar[:], l_mv[:, :, 1], l_half[:], l_rstd[:], "l", GS * (j + 1), j)

            def clip_gate(g, e, fb):
                n = (g * E + e) * FB + fb
                dve.wait_ge(S["gate_out"], n + 1)
                dve.tensor_scalar(gate[:, fb, :], gate[:, fb, :], LIMIT, None, ALU.min).then_inc(S["gate_ready"], 1)

            def clip_up(g, e, fb):
                n = (g * E + e) * FB + fb
                dve.wait_ge(S["up_ready"], n + 1)
                dve.tensor_scalar(up[:, fb, :], up[:, fb, :], LIMIT, -LIMIT, ALU.min, ALU.max)\
                    .then_inc(S["clip_ready"], 1)

            def activate(g, e, fb):
                n = (g * E + e) * FB + fb
                dve.wait_ge(S["tanh_ready"], n + 1)
                dve.scalar_tensor_tensor(tanh[:, fb, :], tanh[:, fb, :], 1.0, gate[:, fb, :], ALU.add, ALU.mult)\
                    .then_inc(S["tanh_gate"], 1)
                dve.wait_ge(S["clip_ready"], n + 1)
                dve.wait_ge(S["tanh_gate"], n + 1)
                dve.scalar_tensor_tensor(tanh[:, fb, :], up[:, fb, :], 1.0, tanh[:, fb, :], ALU.add, ALU.mult)\
                    .then_inc(S["act_ready"], 1)

            def add_expert(g, e):
                for i in range(2):
                    dve.wait_ge(S["down_done"], 2 * (g * E + e) + i + 1)
                    for s in (2 * i, 2 * i + 1):
                        if e == 0:
                            dve.wait_ge(S["acc_ready"], 2 * (g + 1))
                        else:
                            dve.wait_ge(S["added"], GS * (g * E + e - 1) + s + 1)
                        dve.scalar_tensor_tensor(acc[:, s, :], down_bank[i][:, (s % 2) * DM:(s % 2 + 1) * DM],
                                                 half_share[:, s, e:e + 1], acc[:, s, :], ALU.mult, ALU.add)\
                            .then_inc(S["added"], 1)

            def start_acc(g):
                dve.wait_ge(S["dbias_done"], g + 1)
                dve.wait_ge(S["y_done"], GS * g)
                for i in range(2):
                    dve.tensor_tensor(acc[:, 2 * i:2 * i + 2, :].rearrange("p s d -> p (s d)"), down_bank[i][:],
                                      y2[:, 2 * i:2 * i + 2, :].rearrange("p s d -> p (s d)"), ALU.add)\
                        .then_inc(S["acc_ready"], 1)

            def output_stats(g):
                for s in range(GS):
                    dve.wait_ge(S["added"], GS * (g * E + E - 1) + s + 1)
                    dve.bn_stats(e_stats[:, s, :], acc[:, s, :]).then_inc(S["e_stats_ready"], 1)
                dve.wait_ge(S["e_stats_ready"], GS * (g + 1))
                stand_apart(dve, S["dve_passed"])
                for s in range(GS):
                    dve.bn_aggr(e_mv[:, s, :], e_stats[:, s, :]).then_inc(S["e_mv_ready"], 1)
                seed(e_var[:], e_hvar[:], e_mv[:, :, 1], e_half[:], e_rstd[:], "e", GS * (g + 1), g)

            def lower_y2(j):
                for c in range(KC):
                    dve.wait_ge(S["yT_hi_ready"], KC * j + c + 1)
                    dve.tensor_tensor(yT_lo[:, c, :], pair_bank[c][:], yT_hi[:, c, :].bitcast(F32), ALU.subtract)\
                        .then_inc(S["yT_lo_ready"], 1)

            def route(j):
                dve.wait_ge(S["logits_done"], j + 1)
                dve.tensor_tensor(logits[:], logits_ps, row_all[:, 0:E].unsqueeze(1).to_broadcast([P, GS, E]), ALU.add)\
                    .then_inc(S["logits_ready"], 1)
                dve.wait_ge(S["logits_ready"], j + 1)
                dve.tensor_reduce(peak[:], logits[:], AX.X, ALU.max).then_inc(S["peak_ready"], 1)
                dve.wait_ge(S["peak_ready"], j + 1)
                dve.tensor_tensor(r_exp[:], logits[:], peak[:].unsqueeze(2).to_broadcast([P, GS, E]), ALU.subtract)\
                    .then_inc(S["shifted"], 1)
                this = logits[:].unsqueeze(3).to_broadcast([P, GS, E, E])
                other = logits[:].unsqueeze(2).to_broadcast([P, GS, E, E])
                grid = "p (s k) e -> p s k e"
                dve.tensor_tensor(beats[:].rearrange(grid, s=GS), other, this, ALU.is_gt).then_inc(S["beats_raw"], 1)
                dve.tensor_tensor(ties[:].rearrange(grid, s=GS), other, this, ALU.is_ge).then_inc(S["ties_raw"], 1)
                dve.wait_ge(S["beats_raw"], j + 1)
                dve.tensor_tensor(beats[:].rearrange(grid, s=GS), beats[:].rearrange(grid, s=GS),
                                  behind[:].unsqueeze(1).to_broadcast([P, GS, E, E]), ALU.mult)\
                    .then_inc(S["beats_cut"], 1)
                dve.wait_ge(S["ties_raw"], j + 1)
                dve.tensor_tensor(ties[:].rearrange(grid, s=GS), ties[:].rearrange(grid, s=GS),
                                  before[:].unsqueeze(1).to_broadcast([P, GS, E, E]), ALU.mult)\
                    .then_inc(S["ties_cut"], 1)
                dve.wait_ge(S["beats_cut"], j + 1)
                dve.wait_ge(S["ties_cut"], j + 1)
                dve.tensor_tensor(beats[:], beats[:], ties[:], ALU.add).then_inc(S["beats_sum"], 1)
                dve.wait_ge(S["beats_sum"], j + 1)
                dve.tensor_reduce(rank[:], beats[:], AX.X, ALU.add).then_inc(S["rank_ready"], 1)
                dve.wait_ge(S["rank_ready"], j + 1)
                dve.tensor_scalar(top[:], rank[:], 2.0, None, ALU.is_lt).then_inc(S["top_ready"], 1)
                dve.wait_ge(S["r_exp_ready"], j + 1)
                dve.tensor_reduce(r_sum[:], r_exp[:], AX.X, ALU.add).then_inc(S["r_sum_ready"], 1)
                dve.wait_ge(S["r_sum_ready"], j + 1)
                dve.reciprocal(r_inv[:], r_sum[:]).then_inc(S["r_inv_ready"], 1)
                dve.wait_ge(S["top_ready"], j + 1)
                dve.tensor_tensor(r_exp[:].rearrange("p s e -> p (s e)"), r_exp[:].rearrange("p s e -> p (s e)"), top[:],
                                  ALU.mult).then_inc(S["top_exp"], 1)
                dve.wait_ge(S["top_exp"], j + 1)
                dve.wait_ge(S["r_inv_ready"], j + 1)
                dve.tensor_tensor(share[:], r_exp[:], r_inv[:].unsqueeze(2).to_broadcast([P, GS, E]), ALU.mult)\
                    .then_inc(S["share_ready"], 1)
                dve.wait_ge(S["share_ready"], j + 1)
                dve.tensor_scalar(half_share[:], share[:], 0.5, None, ALU.mult).then_inc(S["half_share_ready"], 1)

            for e in range(T_SLOT, E):
                gates_mid(0, e)
                gates_end(0, e)
            largest_log(0)
            for e in range(GS):
                heads_a(0, e)
                heads_b(0, e)
            for e in range(T_SLOT, E):
                gates_mid(1, e)
                gates_end(1, e)
            largest_log(1)
            for e in range(GS, E):
                heads_a(0, e)
                heads_b(0, e)
            lower_y2(0)
            route(0)

            def body(g, heads=True, gates=True):
                for e in range(E):
                    if heads:
                        heads_a(g + 1, e)
                    clip_gate(g, e, 0)
                    clip_up(g, e, 0)
                    activate(g, e, 0)
                    if gates:
                        gates_mid(g + 2, e)
                    clip_gate(g, e, 1)
                    clip_up(g, e, 1)
                    activate(g, e, 1)
                    if e == 0:
                        dve.wait_ge(S["half_share_ready"], g + 1)
                        start_acc(g)
                    if heads:
                        heads_b(g + 1, e)
                    if gates:
                        gates_end(g + 2, e)
                    if e:
                        add_expert(g, e - 1)
                if gates:
                    largest_log(g + 2)
                if heads:
                    lower_y2(g + 1)
                add_expert(g, E - 1)
                output_stats(g)
                if heads:
                    route(g + 1)

            body(0)
            with dve.Fori(1, GROUPS - 2) as g:
                body(g)
            body(GROUPS - 2, gates=False)
            body(GROUPS - 1, heads=False, gates=False)

        @block.tensor
        def _(pe):
            pe.wait_ge(S["consts"], 16)
            pe.wait_ge(S["gate_loaded"], 32)
            pe.wait_ge(S["gbias_loaded"], 16)
            pe.wait_ge(S["r_loaded"], 16)
            for c in range(3 * KC):
                pe.transpose(small_bank[:, c * 2 * MH:(c + 1) * 2 * MH], gate_rows[:, c * P:(c + 1) * P],
                             ident[0:2 * MH, 0:2 * MH])
            pe.transpose(small_bank[:, 64:64 + E * 2 * FB], gu_bias_rows, ident[0:E * 2 * FB, 0:E * 2 * FB])
            for c in range(KC):
                last_mm = pe.transpose(small_bank[:, 128 + c * E:128 + (c + 1) * E], r_rows[:, c * P:(c + 1) * P],
                                       ident[0:E, 0:E])
            last_mm.then_inc(S["setup_T"], 1)
            pe.wait_ge(S["gate_w_ready"], 5)

            def transpose_inputs(j, sequences):
                for s in sequences:
                    if s >= 2:
                        pe.wait_ge(S["yc_out"], GS * j + s - 1)
                    for c in range(KC):
                        pe.transpose(pair_bank[s % 2][:, c * P:(c + 1) * P], y_in[:, s, c * P:(c + 1) * P], ident[:])
                    for c in range(KC):
                        last = pe.transpose(pair_bank[s % 2][:, (KC + c) * P:(KC + c + 1) * P],
                                            c_in[:, s, c * P:(c + 1) * P], ident[:])
                    last.then_inc(S["yc_done"], 1)

            def gates_mid(j, e):
                if e == T_SLOT:
                    pe.wait_ge(S["y_loaded"], 16 * (j + 1))
                    pe.wait_ge(S["cin_loaded"], 16 * (j + 1))
                    pe.wait_ge(S["cmat_ready"], 2 * GS * j)
                    transpose_inputs(j, range(GS // 2))
                if e == T_SLOT + 1:
                    pe.wait_ge(S["yc_out"], GS * (j + 1))
                    pe.wait_ge(S["decay_ready"], MH * GS * j)
                    for c in range(2 * KC):
                        last = pe.matmul(log_bank[0:2 * MH, :].rearrange("p (s t) -> p s t", s=GS), gate_w[:, c, :],
                                         ycT[:, :, c, :], start=(c == 0), stop=(c == 2 * KC - 1))
                    last.then_inc(S["rows_done"], 1)
                if e == T_SLOT + 3:
                    pe.wait_ge(S["log_f_ready"], j + 1)
                    pe.matmul(small_bank[:, 0:PAIRS], ones_to[:], log_f[:].rearrange("p s h -> p (s h)"),
                              start=True, stop=True).then_inc(S["cum_done"], 1)

            def gates_end(j, e):
                if e == T_SLOT:
                    transpose_inputs(j, range(GS // 2, GS))
                if e == T_SLOT + 1:
                    pe.wait_ge(S["rows_out"], j + 1)
                    pe.wait_ge(S["h_ready"], GS * j)
                    stand_apart(pe, S["pe_passed"])
                    for s in range(GS):
                        last = pe.transpose(gates_ps[:, s, :], gates_by_row[:, s * P:(s + 1) * P],
                                            ident[0:2 * MH, 0:2 * MH])
                    last.then_inc(S["gates_done"], 1)
                if e == T_SLOT + 3:
                    pe.wait_ge(S["a_ready"], j + 1)
                    pe.transpose(small_bank[0:PAIRS, 0:P], a_tok[:], ident[:]).then_inc(S["aT_done"], 1)

            def transpose_maxima(j):
                pe.wait_ge(S["m_lo_ready"], j + 2)
                stand_apart(pe, S["pe_passed"])
                pe.transpose(small_bank[:, 0:PAIRS], m_rows[:], ident[0:PAIRS, 0:PAIRS]).then_inc(S["mT_done"], 1)

            def heads_a(j, e):
                if e < GS:
                    s = e
                    n = j * GS + s
                    if s == 0:
                        pe.wait_ge(S["m_lo_ready"], j + 2)
                        pe.wait_ge(S["rows_out"], j + 1)
                    pe.wait_ge(S["decay_ready"], MH * n)
                    pe.matmul(log_bank[:], ident_b[:], after_b[:].rearrange("p h t -> p (h t)"), start=True,
                              stop=False, skip_group_check=True)
                    for h in range(MH):
                        last = pe.matmul(log_bank[:, h * P:(h + 1) * P], neg_sel[:, s * MH + h, :], m_split[:],
                                         start=False, stop=(h == MH - 1), skip_group_check=True)
                    last.then_inc(S["log_done"], 1)
                    if s == 0:
                        pe.wait_ge(S["yc_out"], GS * (j + 1))
                        pe.wait_ge(S["yT_lo_ready"], KC * j)
                    pe.wait_ge(S["cmat_ready"], 2 * n)
                    for h in range(MH):
                        rows = slice(MD * (h % 2), MD * (h % 2 + 1))
                        last = pe.matmul(pair_bank[h % 2][:, (h // 2) * P:(h // 2 + 1) * P],
                                         ycT[rows, s, KC + h // 2, :], ycT[rows, s, h // 2, :], start=True, stop=True)
                    last.then_inc(S["qk_done"], 1)

            def heads_b(j, e):
                if e < GS:
                    s = e
                    n = j * GS + s
                    pe.wait_ge(S["cmat_ready"], 2 * (n + 1))
                    if s == 0:
                        pe.wait_ge(S["c_loaded"], 16 * GS * (j + 1))
                        if isinstance(j, int) and j == 0:
                            pe.wait_ge(S["max_log_ready"], 1)
                        else:
                            pe.wait_ge(S["shareT_out"], j)
                    pe.wait_ge(S["h_ready"], n)
                    for h in range(MH):
                        last = pe.matmul(head_out[:, h, :], cmat[:, h, :], c_one[:, s, h, :], start=True, stop=True)
                    last.then_inc(S["av_done"], 1)

            def transpose_y2(j, gates):
                pe.wait_ge(S["y2_ready"], GS * (j + 1))
                if gates:
                    pe.wait_ge(S["yc_out"], GS * (j + 2))
                for c in range(KC):
                    for s in range(GS):
                        last = pe.transpose(pair_bank[c][:, s * P:(s + 1) * P], y2[:, s, c * P:(c + 1) * P], ident[:])
                last.then_inc(S["yT_done"], 1)

            def route(j, gates):
                pe.wait_ge(S["yT_lo_ready"], KC * (j + 1))
                if gates:
                    pe.wait_ge(S["max_log_ready"], j + 2)
                for s in range(GS):
                    toks = slice(s * P, (s + 1) * P)
                    k = 0
                    for yT, w in ((yT_hi, r_hi), (yT_hi, r_lo), (yT_lo, r_hi)):
                        for c in range(KC):
                            last = pe.matmul(logits_ps[:, s, :], yT[:, c, toks], w[:, c, :], start=(k == 0),
                                             stop=(k == 3 * KC - 1))
                            k += 1
                last.then_inc(S["logits_done"], 1)

            def up_projections(g, e, gates):
                for fb in range(FB):
                    if e == 0 and fb == 1:
                        transpose_shares(g)
                    if gates and fb == 1:
                        gates_mid(g + 2, e)
                    for i in range(2):
                        n = (g * E + e) * FB + fb
                        pe.wait_ge(S["gate_out" if i == 0 else "up_ready"], n)
                        col = i * FI + fb * P
                        k = 0
                        for w, yT in ((gu_hi, yT_hi), (gu_lo, yT_hi), (gu_hi, yT_lo)):
                            for c in range(KC):
                                last = pe.matmul(up_bank[i][:], w[:, e, c, col:col + P], yT[:, c, :],
                                                 start=(k == 0), stop=(k == 3 * KC - 1))
                                k += 1
                        last.then_inc(S["up_done"], 1)

            def down_projection(g, e):
                for i in range(2):
                    if i == 0:
                        pe.wait_ge(S["act_lo_ready"], FB * (g * E + e + 1))
                    if e == 0:
                        pe.wait_ge(S["acc_ready"], 2 * (g + 1))
                    else:
                        pe.wait_ge(S["added"], GS * (g * E + e - 1) + 2 * i + 2)
                    for s in (2 * i, 2 * i + 1):
                        toks = slice(s * P, (s + 1) * P)
                        k = 0
                        for a, w in ((act_hi, d_hi), (act_hi, d_lo), (act_lo, d_hi)):
                            for fb in range(FB):
                                last = pe.matmul(down_bank[i][:, (s % 2) * DM:(s % 2 + 1) * DM],
                                                 a[:, e % 2, fb, toks], w[:, e, fb, :], start=(k == 0),
                                                 stop=(k == 3 * FB - 1))
                                k += 1
                    last.then_inc(S["down_done"], 1)

            def transpose_shares(g):
                pe.wait_ge(S["half_share_ready"], g + 1)
                pe.wait_ge(S["logits_ready"], g + 1)
                pe.transpose(small_bank[0:GS * E, 0:P], share[:].rearrange("p s e -> p (s e)"), ident[:])\
                    .then_inc(S["shareT_done"], 1)

            def bias_shares(g):
                pe.wait_ge(S["shareT_out"], g + 1)
                pe.wait_ge(S["added"], GS * E * g)
                for s in range(GS):
                    last = pe.matmul(down_bank[s // 2][:, (s % 2) * DM:(s % 2 + 1) * DM], share_T[:], d_bias[:, s, :],
                                     start=True, stop=True)
                last.then_inc(S["dbias_done"], 1)

            for e in range(T_SLOT, E):
                gates_mid(0, e)
                gates_end(0, e)
            transpose_maxima(0)
            for e in range(GS):
                heads_a(0, e)
                heads_b(0, e)
            for e in range(T_SLOT, E):
                gates_mid(1, e)
                gates_end(1, e)
            transpose_maxima(1)
            pe.wait_ge(S["dbias_loaded"], 16 * GS)
            transpose_y2(0, gates=True)
            route(0, gates=True)

            def body(g, heads=True, gates=True, split=False):
                for e in range(E):
                    if heads:
                        heads_a(g + 1, e)
                    if split:
                        pe.wait_ge(S["gu_ready"], e + 1)
                        pe.wait_ge(S["d_ready"], e + 1)
                    up_projections(g, e, gates)
                    if e == 0:
                        bias_shares(g)
                    if heads:
                        heads_b(g + 1, e)
                    if gates:
                        gates_end(g + 2, e)
                    if e:
                        down_projection(g, e - 1)
                if gates:
                    transpose_maxima(g + 2)
                if heads:
                    transpose_y2(g + 1, gates)
                down_projection(g, E - 1)
                if heads:
                    route(g + 1, gates)

            body(0, split=True)
            with pe.Fori(1, GROUPS - 2) as g:
                body(g)
            body(GROUPS - 2, gates=False)
            body(GROUPS - 1, heads=False, gates=False)


def decoder(nc, ins, out):
    y1 = nc.dram_tensor("y1_dram", [NSEQ, P, DM], F32, kind="Internal").ap()
    attention(nc, y1, ins["x"], *(ins["L0_attn_" + n] for n in ("wq", "wkv", "wo", "bo")))
    mlstm_and_experts(nc, out, y1, ins["ctx_1024"],
                      *(ins["L0_xattn_" + n] for n in ("w_igate", "b_igate", "w_fgate", "b_fgate", "ln_weight")),
                      *(ins["L0_ffn_" + n] for n in ("router_weight", "router_bias", "gate_up_proj",
                                                     "gate_up_bias", "down_proj", "down_bias")))


_INS = ['x', 'ctx_1024', 'L0_attn_wq', 'L0_attn_wkv', 'L0_attn_wo', 'L0_attn_bo', 'L0_xattn_w_igate',
        'L0_xattn_b_igate', 'L0_xattn_w_fgate', 'L0_xattn_b_fgate', 'L0_xattn_ln_weight',
        'L0_ffn_router_weight', 'L0_ffn_router_bias', 'L0_ffn_gate_up_proj', 'L0_ffn_gate_up_bias',
        'L0_ffn_down_proj', 'L0_ffn_down_bias']
_OUTS = [((32, 128, 256), 'float32')]


def kernel(**inputs):
    import numpy as _np
    import concourse.bacc as _bacc
    from concourse import mybir as _mybir
    from concourse.bass_utils import run_bass_kernel_spmd as _run

    nc = _bacc.Bacc("TRN2", target_bir_lowering=False, num_devices=1)
    arrays, aps = {}, {}
    for name in _INS:
        a = _np.ascontiguousarray(inputs[name])
        arrays[f"in_{name}_dram"] = a
        aps[name] = nc.dram_tensor(f"in_{name}_dram", a.shape, _mybir.dt.from_np(a.dtype), kind="ExternalInput").ap()
    shape, dtype = _OUTS[0]
    out = nc.dram_tensor("out_0_dram", shape, _mybir.dt.from_np(_np.dtype(dtype)), kind="ExternalOutput").ap()
    decoder(nc, aps, out)
    r = _run(nc, [arrays], core_ids=[0])
    return r.results[0]["out_0_dram"]
```

```python
from contextlib import ExitStack

import concourse.bass as bass
from concourse import mybir

F32 = mybir.dt.float32
F32R = mybir.dt.float32r
BF16 = mybir.dt.bfloat16
I32 = mybir.dt.int32
ALU = mybir.AluOpType
ACT = mybir.ActivationFunctionType
AX = mybir.AxisListType

P = 128
NSEQ = 32
DM = 256
KC = DM // P
GS = 4
GROUPS = NSEQ // GS
GT = GS * P

HEADS = 16
DH = 64
INNER = HEADS * DH
QH = 4
QUADS = HEADS // QH
UNITS = QUADS * GS
QF = QH * DH
OC = QF // P
BLOCKS = 2 * OC
AHEAD = BLOCKS + 1
SWITCH = UNITS - AHEAD
NORM = 7
ATT_SCALE = DH**-0.5
MASKED = -3.0e38
LN_EPS = 1e-5
RSQRT_SEED = 0x5F3759DF
NEWTON = 3
NEWTON_OPS = 4 * NEWTON

MH = 4
MD = DM // MH
QK_SCALE = MD**-0.5
NORM_EPS = 1e-6
PAIRS = GS * MH
T_SLOT = 4

E = 8
FI = 256
FB = FI // P
SPLIT_FIRST = 4
LIMIT = 7.0
ALPHA = 1.702


def stand_apart(eng, passed):
    eng.sem_inc(passed, 1)


def newton_rsqrt(pool, done, base, y, half_v, tmp, three_halves):
    k = 0

    def step(ins):
        nonlocal k
        k += 1
        ins.then_inc(done, 1)
        pool.wait_ge(done, base + k)

    for _ in range(NEWTON):
        step(pool.tensor_tensor(tmp, y, y, ALU.mult))
        step(pool.tensor_tensor(tmp, tmp, half_v, ALU.mult))
        step(pool.tensor_tensor(tmp, three_halves, tmp, ALU.subtract))
        step(pool.tensor_tensor(y, y, tmp, ALU.mult))


def norm_shift(pool, done, base, shift, mean, y, passed):
    pool.tensor_tensor(shift, mean, y, ALU.mult).then_inc(done, 1)
    pool.wait_ge(done, base + 1)
    stand_apart(pool, passed)
    pool.tensor_scalar(shift, shift, -1.0, None, ALU.mult).then_inc(done, 1)


def attention(nc, y1, x, wq, wkv, wo, bo):
    with ExitStack() as ctx:
        def sb(name, shape, dt=F32):
            return ctx.enter_context(nc.sbuf_tensor(name, shape, dt))

        def bank(name):
            return ctx.enter_context(nc.psum_tensor(name, [P, 512], F32))

        def sem(name):
            return ctx.enter_context(nc.semaphore(name))

        w_raw = sb("w_raw", [P, KC, 3 * INNER])
        w_hi = sb("w_hi", [P, KC, 3 * INNER], F32R)
        w_lo = sb("w_lo", [P, KC, 3 * INNER], F32R)
        wo_raw = sb("wo_raw", [P, INNER // P, DM])
        wo_hi = sb("wo_hi", [P, INNER // P, DM], F32R)
        wo_lo = sb("wo_lo", [P, INNER // P, DM], F32R)
        bo_row = sb("bo_row", [1, DM])
        bo_all = sb("bo_all", [P, DM])
        ident = sb("ident", [P, P])
        mask = sb("mask", [P, P])
        x_in = sb("x_in", [P, GS, DM])
        x_res = sb("x_res", [P, GS, DM])
        xT_hi = sb("xT_hi", [P, KC, GT], F32R)
        xT_lo = sb("xT_lo", [P, KC, GT], F32R)
        qkT = sb("qkT", [P, 2, BLOCKS, GT])
        values = sb("values", [P, 2, GS, QF])
        probs = sb("probs", [P, 2, QH, P])
        probsT = sb("probsT", [P, QH, P])
        row_max = sb("row_max", [P, 2, QH])
        neg_max = sb("neg_max", [P, 2, QH])
        zero_exp = sb("zero_exp", [P, 2, QH])
        row_sum = sb("row_sum", [P, 2, QH])
        denom = sb("denom", [P, QH])
        inv_denom = sb("inv_denom", [P, QH])
        oT_hi = sb("oT_hi", [P, OC, P], F32R)
        oT_lo = sb("oT_lo", [P, OC, P], F32R)
        z = sb("z", [P, GS, DM])
        y_out = sb("y_out", [P, GS, DM])
        stats = sb("stats", [P, GS, 6])
        mean_var = sb("mean_var", [P, GS, 2])
        var_eps = sb("var_eps", [P, GS])
        half_bits = sb("half_bits", [P, GS], I32)
        rstd = sb("rstd", [P, GS])
        half_var = sb("half_var", [P, GS])
        newton_tmp = sb("newton_tmp", [P, GS])
        shift = sb("shift", [P, GS])
        three_halves = sb("three_halves", [P, GS])

        acc = [bank(f"acc{i}") for i in range(2)]
        score_bank = [bank(f"score_bank{i}") for i in range(2)]
        pT_bank = bank("pT_bank")
        av_bank = bank("av_bank")
        qk_bank = bank("qk_bank")
        v_bank = bank("v_bank")
        oT_bank = av_bank[:, 0:OC * P]

        w_loaded = [sem(f"w_loaded{i}") for i in range(QUADS)]
        first_w_loaded = [sem(f"first_w_loaded{i}") for i in range(3)]
        wo_loaded = sem("wo_loaded")
        bo_loaded = sem("bo_loaded")
        x_loaded = sem("x_loaded")
        xres_loaded = sem("xres_loaded")
        consts = sem("consts")
        w_hi_ready = sem("w_hi_ready")
        w_ready = sem("w_ready")
        later_w_ready = sem("later_w_ready")
        wo_hi_ready = sem("wo_hi_ready")
        wo_ready = sem("wo_ready")
        bo_ready = sem("bo_ready")
        xT_done = sem("xT_done")
        xT_hi_ready = sem("xT_hi_ready")
        xT_lo_ready = sem("xT_lo_ready")
        block_done = sem("block_done")
        block_out = sem("block_out")
        v_done = sem("v_done")
        v_out = sem("v_out")
        scores_done = sem("scores_done")
        masked_done = sem("masked_done")
        neg_max_ready = sem("neg_max_ready")
        exp_done = sem("exp_done")
        zero_exp_ready = sem("zero_exp_ready")
        pT_done = sem("pT_done")
        pT_out = sem("pT_out")
        oT_done = sem("oT_done")
        denom_ready = sem("denom_ready")
        inv_ready = sem("inv_ready")
        weights_ready = sem("weights_ready")
        oT_hi_ready = sem("oT_hi_ready")
        oT_lo_ready = sem("oT_lo_ready")
        wo_done = sem("wo_done")
        xres_ready = sem("xres_ready")
        z_ready = sem("z_ready")
        stats_ready = sem("stats_ready")
        mean_var_ready = sem("mean_var_ready")
        var_eps_ready = sem("var_eps_ready")
        half_ready = sem("half_ready")
        seed_ready = sem("seed_ready")
        newton_done = sem("newton_done")
        shift_ready = sem("shift_ready")
        y_done = sem("y_done")
        y_stored = sem("y_stored")
        half_var_ready = sem("half_var_ready")
        dve_passed = sem("dve_passed")
        pool_passed = sem("pool_passed")

        blocks = ctx.enter_context(ExitStack())
        block = blocks.enter_context(nc.Block())

        def x_group(j):
            return x[bass.ds(j * GS, GS)].rearrange("b t d -> t b d")

        w_view = [(wq, 0, 0), (wkv, 0, INNER), (wkv, INNER, 2 * INNER)]

        def w_cols(q):
            return [slice(base + q * QF, base + (q + 1) * QF) for _, _, base in w_view]

        @block.sync
        def _(sp):
            sp.dma_start(x_in[:], x_group(0)).then_inc(x_loaded, 16)
            for q in range(QUADS):
                for i, (src, col, base) in enumerate(w_view):
                    sp.dma_start(w_raw[:, :, base + q * QF:base + (q + 1) * QF],
                                 src[:, col + q * QF:col + (q + 1) * QF]
                                 .rearrange("(c p) n -> p c n", p=P)).then_inc(w_loaded[q] if q else first_w_loaded[i], 16)
                if q == 1:
                    sp.dma_start(wo_raw[:], wo.rearrange("(c p) n -> p c n", p=P)).then_inc(wo_loaded, 16)
            sp.dma_start(bo_row[:], bo.rearrange("(a n) -> a n", a=1)).then_inc(bo_loaded, 16)
            sp.dma_start(x_res[:], x_group(0)).then_inc(xres_loaded, 16)

            def group(g):
                sp.wait_ge(xT_done, g + 1)
                sp.dma_start(x_in[:], x_group(g + 1)).then_inc(x_loaded, 16)
                sp.wait_ge(z_ready, 2 * (g + 1))
                sp.dma_start(x_res[:], x_group(g + 1)).then_inc(xres_loaded, 16)

            def store(j):
                sp.wait_ge(y_done, GS * (j + 1))
                sp.dma_start(y1[bass.ds(j * GS, GS)].rearrange("b t d -> t b d"), y_out[:]).then_inc(y_stored, 16)

            with sp.Fori(0, GROUPS - 1) as g:
                group(g)
                store(g)
            store(GROUPS - 1)
            sp.wait_ge(y_stored, 16 * GROUPS)

        @block.gpsimd
        def _(pool):
            pool.memset(ident[:], 0.0).then_inc(consts, 1)
            pool.memset(mask[:], 0.0).then_inc(consts, 1)
            pool.memset(three_halves[:], 1.5).then_inc(consts, 1)
            pool.wait_ge(consts, 3)
            pool.affine_select(out=ident[:], in_=ident[:], compare_op=ALU.not_equal, fill=1.0, base=0,
                               pattern=[[-1, P]], channel_multiplier=1).then_inc(consts, 1)
            pool.affine_select(out=mask[:], in_=mask[:], compare_op=ALU.is_ge, fill=MASKED, base=0,
                               pattern=[[-1, P]], channel_multiplier=1).then_inc(consts, 1)
            def lower_weights(q):
                for i, cols in enumerate(w_cols(q)):
                    pool.wait_ge(w_hi_ready, 3 * q + i + 1)
                    pool.tensor_tensor(w_lo[:, :, cols], w_raw[:, :, cols], w_hi[:, :, cols].bitcast(F32),
                                       ALU.subtract).then_inc(later_w_ready, 1)

            lower_weights(1)
            pool.wait_ge(wo_hi_ready, 1)
            pool.tensor_tensor(wo_lo[:], wo_raw[:], wo_hi[:].bitcast(F32), ALU.subtract).then_inc(wo_ready, 1)
            for q in range(2, QUADS):
                lower_weights(q)
            pool.wait_ge(bo_loaded, 16)
            pool.partition_broadcast(bo_all[:], bo_row[:]).then_inc(bo_ready, 1)
            pool.wait_ge(bo_ready, 1)

            def add_bias(j):
                pool.wait_ge(xres_loaded, 16 * (j + 1))
                for s in range(GS):
                    pool.tensor_tensor(x_res[:, s, :], x_res[:, s, :], bo_all[:], ALU.add).then_inc(xres_ready, 1)

            def norm_scales(j):
                pool.wait_ge(half_var_ready, j + 1)
                pool.wait_ge(seed_ready, j + 1)
                newton_rsqrt(pool, newton_done, NEWTON_OPS * j, rstd[:], half_var[:], newton_tmp[:], three_halves[:])
                norm_shift(pool, shift_ready, 2 * j, shift[:], mean_var[:, :, 0], rstd[:], pool_passed)

            add_bias(0)
            norm_scales(0)
            add_bias(1)
            with pool.Fori(1, GROUPS - 1) as j:
                norm_scales(j)
                add_bias(j + 1)
            norm_scales(GROUPS - 1)

        @block.scalar
        def _(act):
            def x_hi(j):
                for c, src in enumerate((qk_bank, pT_bank)):
                    if c == 0:
                        act.wait_ge(xT_done, j + 1)
                    act.activation(xT_hi[:, c, :], src[:], ACT.Copy).then_inc(xT_hi_ready, 1)

            def copy_block(n, q, b):
                act.wait_ge(block_done, n + 1)
                act.activation(qkT[:, q % 2, b, :], qk_bank[:], ACT.Copy).then_inc(block_out, 1)

            def output_hi(n):
                act.wait_ge(oT_done, n)
                if not (isinstance(n, int) and n == 1):
                    act.wait_ge(wo_done, n - 1)
                act.activation(oT_hi[:].rearrange("p c t -> p (c t)"), oT_bank, ACT.Copy).then_inc(oT_hi_ready, 1)

            def exponentials(n, u):
                act.wait_ge(neg_max_ready, n + 1)
                for h in range(QH):
                    act.activation(probs[:, u % 2, h, :], probs[:, u % 2, h, :], ACT.Exp,
                                   bias=neg_max[:, u % 2, h:h + 1], scale=ATT_SCALE,
                                   accum_out=row_sum[:, u % 2, h:h + 1]).then_inc(exp_done, 1)
                act.activation(zero_exp[:, u % 2, :], neg_max[:, u % 2, :], ACT.Exp).then_inc(zero_exp_ready, 1)

            def normalise(j):
                act.wait_ge(newton_done, NEWTON_OPS * (j + 1))
                act.wait_ge(shift_ready, 2 * (j + 1))
                if not (isinstance(j, int) and j == 0):
                    act.wait_ge(y_stored, 16 * j)
                for s in range(GS):
                    act.activation(y_out[:, s, :], z[:, s, :], ACT.Identity, bias=shift[:, s:s + 1],
                                   scale=rstd[:, s:s + 1]).then_inc(y_done, 1)

            x_hi(0)
            for k in range(AHEAD):
                copy_block(k, k // BLOCKS, k % BLOCKS)
            exponentials(0, 0)

            def group(g, first=False, last=False):
                for u in range(UNITS):
                    n = g * UNITS + u
                    if not (first and u == 0):
                        output_hi(n)
                    if u == SWITCH + 1 and not last:
                        copy_block(n - 1 + AHEAD, 0, 0)
                    if not (last and u == UNITS - 1):
                        exponentials(n + 1, u + 1)
                    if u == NORM and not first:
                        normalise(g - 1)
                    if u == SWITCH and not last:
                        x_hi(g + 1)
                    if u != SWITCH and not (last and u + AHEAD >= UNITS):
                        copy_block(n + AHEAD, (u + AHEAD) // BLOCKS, (u + AHEAD) % BLOCKS)

            group(0, first=True)
            with act.Fori(1, GROUPS - 1) as g:
                group(g)
            group(GROUPS - 1, last=True)
            output_hi(GROUPS * UNITS)
            normalise(GROUPS - 1)

        @block.vector
        def _(dve):
            def raise_weights(q):
                dve.wait_ge(w_loaded[q], 16 * 3)
                for i, cols in enumerate(w_cols(q)):
                    dve.tensor_copy(w_hi[:, :, cols], w_raw[:, :, cols]).then_inc(w_hi_ready, 1)

            def x_lo(j):
                for c, src in enumerate((qk_bank, pT_bank)):
                    dve.wait_ge(xT_hi_ready, KC * j + c + 1)
                    dve.tensor_tensor(xT_lo[:, c, :], src[:], xT_hi[:, c, :].bitcast(F32), ALU.subtract)\
                        .then_inc(xT_lo_ready, 1)

            def copy_values(n, q, s):
                dve.wait_ge(v_done, n + 1)
                dve.tensor_copy(values[:, q % 2, s, :], v_bank[:, 0:QF]).then_inc(v_out, 1)

            def output_lo(n):
                dve.wait_ge(oT_hi_ready, n)
                dve.tensor_tensor(oT_lo[:].rearrange("p c t -> p (c t)"), oT_bank,
                                  oT_hi[:].rearrange("p c t -> p (c t)").bitcast(F32), ALU.subtract)\
                    .then_inc(oT_lo_ready, 1)

            def residual(j, i):
                if i == 0:
                    dve.wait_ge(wo_done, UNITS * (j + 1))
                    dve.wait_ge(xres_ready, GS * (j + 1))
                    dve.wait_ge(y_done, GS * j)
                dve.tensor_tensor(z[:, 2 * i:2 * i + 2, :].rearrange("p s d -> p (s d)"), acc[i][:],
                                  x_res[:, 2 * i:2 * i + 2, :].rearrange("p s d -> p (s d)"), ALU.add)\
                    .then_inc(z_ready, 1)

            def residual_stats(j, i):
                dve.wait_ge(z_ready, 2 * j + i + 1)
                for s in (2 * i, 2 * i + 1):
                    dve.bn_stats(stats[:, s, :], z[:, s, :]).then_inc(stats_ready, 1)

            def residual_seed(j):
                dve.wait_ge(stats_ready, GS * (j + 1))
                stand_apart(dve, dve_passed)
                for s in range(GS):
                    dve.bn_aggr(mean_var[:, s, :], stats[:, s, :]).then_inc(mean_var_ready, 1)
                dve.wait_ge(mean_var_ready, GS * (j + 1))
                dve.tensor_scalar(var_eps[:], mean_var[:, :, 1], LN_EPS, None, ALU.add).then_inc(var_eps_ready, 1)
                dve.wait_ge(var_eps_ready, j + 1)
                dve.tensor_scalar(half_var[:], var_eps[:], 0.5, None, ALU.mult).then_inc(half_var_ready, 1)
                dve.tensor_scalar(half_bits[:], var_eps[:].bitcast(I32), 1, None, ALU.logical_shift_right)\
                    .then_inc(half_ready, 1)
                dve.wait_ge(half_ready, j + 1)
                dve.tensor_scalar(rstd[:].bitcast(I32), half_bits[:], -1.0, float(RSQRT_SEED), ALU.mult, ALU.add)\
                    .then_inc(seed_ready, 1)

            def masked_scores(n, u):
                dve.wait_ge(scores_done, n + 1)
                if not (isinstance(n, int) and n < 2):
                    dve.wait_ge(pT_done, n - 1)
                stand_apart(dve, dve_passed)
                for h in range(QH):
                    dve.tensor_tensor_reduce(probs[:, u % 2, h, :], score_bank[h % 2][:, (h // 2) * P:(h // 2 + 1) * P],
                                             mask[:], 1.0, MASKED, ALU.add, ALU.max, row_max[:, u % 2, h:h + 1])\
                        .then_inc(masked_done, 1)
                dve.wait_ge(masked_done, QH * (n + 1))
                dve.tensor_scalar(neg_max[:, u % 2, :], row_max[:, u % 2, :], -ATT_SCALE, 0.0, ALU.mult, ALU.min)\
                    .then_inc(neg_max_ready, 1)

            def weights(n, u):
                dve.wait_ge(exp_done, QH * (n + 1))
                dve.wait_ge(zero_exp_ready, n + 1)
                dve.scalar_tensor_tensor(denom[:], zero_exp[:, u % 2, :], float(P), row_sum[:, u % 2, :],
                                         ALU.mult, ALU.add).then_inc(denom_ready, 1)
                dve.wait_ge(denom_ready, n + 1)
                dve.reciprocal(inv_denom[:], denom[:]).then_inc(inv_ready, 1)
                dve.wait_ge(inv_ready, n + 1)
                dve.tensor_tensor(probs[:, u % 2], probs[:, u % 2], inv_denom[:].unsqueeze(2).to_broadcast([P, QH, P]),
                                  ALU.mult).then_inc(weights_ready, 1)

            for i, cols in enumerate(w_cols(0)):
                dve.wait_ge(first_w_loaded[i], 16)
                dve.tensor_copy(w_hi[:, :, cols], w_raw[:, :, cols]).then_inc(w_hi_ready, 1)
                dve.wait_ge(w_hi_ready, i + 1)
                dve.tensor_tensor(w_lo[:, :, cols], w_raw[:, :, cols], w_hi[:, :, cols].bitcast(F32),
                                  ALU.subtract).then_inc(w_ready, 1)
                if i == 0:
                    x_lo(0)
            raise_weights(1)
            copy_values(0, 0, 0)
            dve.wait_ge(wo_loaded, 16)
            dve.tensor_copy(wo_hi[:], wo_raw[:]).then_inc(wo_hi_ready, 1)
            copy_values(1, 0, 1)
            raise_weights(2)
            copy_values(2, 0, 2)
            raise_weights(3)
            copy_values(3, 0, 3)
            dve.wait_ge(consts, 5)
            masked_scores(0, 0)
            weights(0, 0)

            def group(g, first=False, last=False):
                for u in range(UNITS):
                    n = g * UNITS + u
                    q, s = divmod(u, GS)
                    if not (last and u == UNITS - 1):
                        masked_scores(n + 1, u + 1)
                    if not (first and u == 0):
                        output_lo(n)
                    dve.wait_ge(pT_done, n + 1)
                    if not (isinstance(n, int) and n == 0):
                        dve.wait_ge(oT_done, n)
                    dve.tensor_copy(probsT[:].rearrange("p h t -> p (h t)"), pT_bank[:]).then_inc(pT_out, 1)
                    if not (last and q == QUADS - 1):
                        copy_values(n + GS, q + 1, s)
                    if not (last and u == UNITS - 1):
                        weights(n + 1, u + 1)
                    if u == SWITCH and not last:
                        x_lo(g + 1)
                    if u in (0, 1) and not first:
                        residual(g - 1, u)
                    if u in (2, 3) and not first:
                        residual_stats(g - 1, u - 2)
                    if u == 4 and not first:
                        residual_seed(g - 1)

            group(0, first=True)
            with dve.Fori(1, GROUPS - 1) as g:
                group(g)
            group(GROUPS - 1, last=True)
            output_lo(GROUPS * UNITS)
            for i in range(2):
                residual(GROUPS - 1, i)
            for i in range(2):
                residual_stats(GROUPS - 1, i)
            residual_seed(GROUPS - 1)

        @block.tensor
        def _(pe):
            def transpose_x(j):
                pe.wait_ge(x_loaded, 16 * (j + 1))
                for c, dst in enumerate((qk_bank, pT_bank)):
                    for s in range(GS):
                        last = pe.transpose(dst[:, s * P:(s + 1) * P], x_in[:, s, c * P:(c + 1) * P], ident[:])
                last.then_inc(xT_done, 1)

            def project_block(q, b):
                col = (b // OC) * INNER + q * QF + (b % OC) * P
                k = 0
                for w, xT in ((w_hi, xT_hi), (w_lo, xT_hi), (w_hi, xT_lo)):
                    for c in range(KC):
                        last = pe.matmul(qk_bank[:], w[:, c, col:col + P], xT[:, c, :], start=(k == 0),
                                         stop=(k == 3 * KC - 1))
                        k += 1
                last.then_inc(block_done, 1)

            def project_values(q, s):
                col = 2 * INNER + q * QF
                k = 0
                for w, xT in ((w_hi, xT_hi), (w_hi, xT_lo), (w_lo, xT_hi)):
                    for c in range(KC):
                        last = pe.matmul(v_bank[:, 0:QF], xT[:, c, s * P:(s + 1) * P], w[:, c, col:col + QF],
                                         start=(k == 0), stop=(k == 3 * KC - 1))
                        k += 1
                last.then_inc(v_done, 1)

            def scores(n, u):
                q, s = divmod(u % UNITS, GS)
                if s == 0:
                    pe.wait_ge(block_out, n + BLOCKS)
                pe.wait_ge(masked_done, QH * n)
                toks = slice(s * P, (s + 1) * P)
                for h in range(QH):
                    rows = slice(DH * (h % 2), DH * (h % 2 + 1))
                    last = pe.matmul(score_bank[h % 2][:, (h // 2) * P:(h // 2 + 1) * P],
                                     qkT[rows, q % 2, h // 2, toks], qkT[rows, q % 2, OC + h // 2, toks],
                                     start=True, stop=True)
                last.then_inc(scores_done, 1)

            def project_output(n, u):
                q, s = divmod(u, GS)
                pe.wait_ge(oT_lo_ready, n)
                out = acc[s // 2][:, (s % 2) * DM:(s % 2 + 1) * DM]
                k = 0
                for oT, w in ((oT_hi, wo_hi), (oT_hi, wo_lo), (oT_lo, wo_hi)):
                    for c in range(OC):
                        last = pe.matmul(out, oT[:, c, :], w[:, OC * q + c, :],
                                         start=(q == 0 and s % 2 == 0 and k == 0),
                                         stop=(q == QUADS - 1 and k == 3 * OC - 1), skip_group_check=True)
                        k += 1
                last.then_inc(wo_done, 1)

            pe.wait_ge(consts, 5)
            transpose_x(0)
            pe.wait_ge(w_ready, 1)
            pe.wait_ge(xT_lo_ready, KC)
            for k in range(AHEAD):
                if k:
                    pe.wait_ge(block_out, k)
                if k == BLOCKS:
                    pe.wait_ge(later_w_ready, 3)
                project_block(k // BLOCKS, k % BLOCKS)
                if k < GS:
                    if k:
                        pe.wait_ge(v_out, k)
                    else:
                        pe.wait_ge(w_ready, 3)
                    project_values(0, k)
            scores(0, 0)

            def group(g, first=False, last=False):
                def next_block(n, u):
                    if not (last and u + AHEAD >= UNITS):
                        pe.wait_ge(block_out, n + AHEAD)
                        if first and u % GS == GS - 1 and u < SWITCH:
                            pe.wait_ge(later_w_ready, 3 * (min(u // GS + 3, QUADS) - 1))
                        project_block((u + AHEAD) // BLOCKS % QUADS, (u + AHEAD) % BLOCKS)

                for u in range(UNITS):
                    n = g * UNITS + u
                    q, s = divmod(u, GS)
                    if not (last and u == UNITS - 1):
                        scores(n + 1, u + 1)
                    if u == SWITCH + 1 and not last:
                        pe.wait_ge(xT_lo_ready, KC * (g + 2))
                        next_block(n - 1, SWITCH)
                    pe.wait_ge(weights_ready, n + 1)
                    pe.wait_ge(pT_out, n)
                    for h in range(QH):
                        last_mm = pe.transpose(pT_bank[:, h * P:(h + 1) * P], probs[:, u % 2, h, :], ident[:])
                    last_mm.then_inc(pT_done, 1)
                    if not (last and q == QUADS - 1):
                        if first and s == 0:
                            pe.wait_ge(later_w_ready, 3 * (min(q + 2, QUADS) - 1))
                        pe.wait_ge(v_out, n + GS)
                        project_values((q + 1) % QUADS, s)
                    if u != SWITCH:
                        next_block(n, u)
                    if not (first and u == 0):
                        if first and u == 1:
                            pe.wait_ge(wo_ready, 1)
                        if not first and u in (1, 3):
                            pe.wait_ge(z_ready, 2 * g - (u == 1))
                        project_output(n, (u - 1) % UNITS)
                    if u == SWITCH and not last:
                        pe.wait_ge(block_out, n + AHEAD)
                        pe.wait_ge(pT_out, n + 1)
                        transpose_x(g + 1)
                    pe.wait_ge(pT_out, n + 1)
                    if s == 0:
                        pe.wait_ge(v_out, GS * (g * QUADS + q + 1))
                    if not (first and u == 0):
                        pe.wait_ge(oT_lo_ready, n)
                    for h in range(QH):
                        last_mm = pe.matmul(oT_bank[DH * (h % 2):DH * (h % 2 + 1), (h // 2) * P:(h // 2 + 1) * P],
                                            values[:, q % 2, s, h * DH:(h + 1) * DH], probsT[:, h, :],
                                            start=True, stop=True)
                    last_mm.then_inc(oT_done, 1)

            group(0, first=True)
            with pe.Fori(1, GROUPS - 1) as g:
                group(g)
            group(GROUPS - 1, last=True)
            project_output(GROUPS * UNITS, UNITS - 1)

        blocks.close()
        with nc.Block() as clearing:
            @clearing.gpsimd
            def _(pool):
                pool.sem_clear(range(w_loaded[0].num, pool_passed.num + 1))


def mlstm_and_experts(nc, out, y1, ctx_in, w_i, b_i, w_f, b_f, ln_w, w_r, b_r, w_gu, b_gu, w_d, b_d):
    with ExitStack() as ctx:
        def sb(name, shape, dt=F32):
            return ctx.enter_context(nc.sbuf_tensor(name, shape, dt))

        def bank(name):
            return ctx.enter_context(nc.psum_tensor(name, [P, 512], F32))

        def sem(name):
            return ctx.enter_context(nc.semaphore(name))

        gu_hi = sb("gu_hi", [P, E, KC, 2 * FI], F32R)
        gu_lo = sb("gu_lo", [P, E, KC, 2 * FI], F32R)
        d_hi = sb("d_hi", [P, E, FB, DM], F32R)
        d_lo = sb("d_lo", [P, E, FB, DM], F32R)
        gu_bias = sb("gu_bias", [P, E * 2 * FB])
        d_bias = sb("d_bias", [3 * GS * E, GS, DM], F32R)
        r_hi = sb("r_hi", [P, KC, E], F32R)
        r_lo = sb("r_lo", [P, KC, E], F32R)
        r_bias = sb("r_bias", [P, E])
        row_all = sb("row_all", [P, E + 2 * MH + DM])
        gate_T = sb("gate_T", [P, 3 * KC, 2 * MH])
        gate_w = sb("gate_w", [P, 2 * KC, 2 * MH])
        gate_bias = row_all[:, E:E + 2 * MH]
        head_scale = sb("head_scale", [P, DM])
        ident = sb("ident2", [P, P])
        ident_b = sb("ident_b", [P, P], BF16)
        ones_to = sb("ones_to", [P, P])
        after_b = sb("after_b", [P, MH, P], BF16)
        neg_sel_f = sb("neg_sel_f", [48, PAIRS])
        neg_sel = sb("neg_sel", [48, PAIRS, P], F32R)
        before = sb("before", [P, E, E])
        behind = sb("behind", [P, E, E])
        acc = sb("acc", [P, GS, DM])
        y_out = sb("y_out2", [P, GS, DM])
        d_bias_raw = acc[0:GS * E]
        gu_raw = y_out[:].rearrange("p s d -> p (s d)").rearrange("p (c n) -> p c n", c=KC)
        d_raw = sb("d_raw", [P, FB, DM])
        y_in = sb("y_in", [P, GS, DM])
        y_res = sb("y_res", [P, GS, DM])
        c_in = sb("c_in", [P, GS, DM])
        c_one = sb("c_one", [P, GS, MH, MD + 1])
        ycT = sb("ycT", [P, GS, 2 * KC, P])
        by_row = sb("by_row", [E, GT])
        gates = sb("gates", [P, GS, 2 * MH])
        abs_f = sb("abs_f", [P, GS, MH])
        soft = sb("soft", [P, GS, MH])
        log_f = sb("log_f", [P, GS, MH])
        cum_f = sb("cum_f", [P, PAIRS])
        a_tok = sb("a_tok", [P, PAIRS])
        a_rows = sb("a_rows", [PAIRS, P])
        m_rows = sb("m_rows", [PAIRS, P])
        m_split = sb("m_split", [48, P], F32R)
        max_log = sb("max_log", [P, PAIRS])
        floor = sb("floor", [P, PAIRS])
        decay = sb("decay", [P, MH, P])
        cmat = sb("cmat", [P, MH, P])
        norm_abs = sb("norm_abs", [P, MH])
        norm_max = sb("norm_max", [P, MH])
        norm_inv = sb("norm_inv", [P, MH])
        y2 = sb("y2", [P, GS, DM])
        h_stats = sb("h_stats", [P, MH, 6])
        h_mv = sb("h_mv", [P, PAIRS, 2])
        h_var = sb("h_var", [P, PAIRS])
        h_half = sb("h_half", [P, PAIRS], I32)
        h_rstd = sb("h_rstd", [P, PAIRS])
        h_hvar = sb("h_hvar", [P, PAIRS])
        h_tmp = sb("h_tmp", [P, PAIRS])
        l_stats = sb("l_stats", [P, GS, 6])
        l_mv = sb("l_mv", [P, GS, 2])
        l_var = sb("l_var", [P, GS])
        l_half = sb("l_half", [P, GS], I32)
        l_rstd = sb("l_rstd", [P, GS])
        l_hvar = sb("l_hvar", [P, GS])
        l_tmp = sb("l_tmp", [P, GS])
        l_shift = sb("l_shift", [P, GS])
        yT_hi = sb("yT_hi", [P, KC, GT], F32R)
        yT_lo = sb("yT_lo", [P, KC, GT], F32R)
        logits = sb("logits", [P, GS, E])
        beats = sb("beats", [P, GS * E, E])
        ties = sb("ties", [P, GS * E, E])
        rank = sb("rank", [P, GS * E])
        top = sb("top", [P, GS * E])
        peak = sb("peak", [P, GS])
        r_exp = sb("r_exp", [P, GS, E])
        r_sum = sb("r_sum", [P, GS])
        r_inv = sb("r_inv", [P, GS])
        share = sb("share", [P, GS, E])
        half_share = sb("half_share", [P, GS, E])
        share_T = sb("share_T", [3 * GS * E, P], F32R)
        gate = sb("gate", [P, FB, GT])
        tanh = sb("tanh", [P, FB, GT])
        up = sb("up", [P, FB, GT])
        gate_rows = gate[0:2 * MH].rearrange("p f t -> p (f t)")[:, 0:3 * DM]
        row = up[0:1].rearrange("p f t -> p (f t)")[:, 0:E + 2 * MH + DM]
        r_rows = tanh[0:E].rearrange("p f t -> p (f t)")[:, 0:DM]
        gu_bias_rows = tanh[0:E * 2 * FB].rearrange("p f t -> p (f t)")[:, DM:DM + P]
        act_hi = sb("act_hi", [P, 2, FB, GT], F32R)
        act_lo = sb("act_lo", [P, 2, FB, GT], F32R)
        e_stats = sb("e_stats", [P, GS, 6])
        e_mv = sb("e_mv", [P, GS, 2])
        e_var = sb("e_var", [P, GS])
        e_half = sb("e_half", [P, GS], I32)
        e_rstd = sb("e_rstd", [P, GS])
        e_hvar = sb("e_hvar", [P, GS])
        e_tmp = sb("e_tmp", [P, GS])
        e_shift = sb("e_shift", [P, GS])
        three_halves = sb("three_halves2", [P, PAIRS])

        up_bank = [bank(f"up_bank{i}") for i in range(2)]
        down_bank = [bank(f"down_bank{i}") for i in range(2)]
        pair_bank = [bank(f"pair_bank{i}") for i in range(2)]
        log_bank = bank("log_bank")
        small_bank = bank("small_bank")
        head_out = small_bank[:, 0:MH * (MD + 1)].rearrange("p (h d) -> p h d", h=MH)
        gates_ps = small_bank[:, 0:GS * 2 * MH].rearrange("p (s k) -> p s k", s=GS)
        logits_ps = small_bank[:, 0:GS * E].rearrange("p (s e) -> p s e", s=GS)

        names = """gu_loaded d_loaded r_loaded gbias_loaded gate_loaded row_loaded dbias_loaded
            y_loaded yres_loaded cin_loaded c_loaded consts setup_T setup_out row_ready gate_w_ready gu_hi_ready gu_ready d_hi_ready
            d_ready yc_done yc_out rows_done rows_out logit_rows_done logit_rows_out gates_done gates_ready gate_out abs_ready gate_exp soft_ready log_f_ready cum_done
            cum_ready a_ready aT_done a_rows_ready m_ready m_hi_ready m_lo_ready mT_done max_log_ready
            floor_exp floor_ready log_done decay_ready qk_done cmat_ready av_done abs_norm norm_ready inv_ready
            h_ready h_stats_ready h_mv_ready h_var_ready h_half_ready h_seed h_newton h_norm h_scaled z_ready
            l_stats_ready l_mv_ready l_var_ready l_half_ready l_seed l_newton y2_ready yT_done yT_hi_ready
            yT_lo_ready logits_done logits_ready beats_raw ties_raw beats_cut ties_cut beats_sum rank_ready
            top_ready peak_ready shifted r_exp_ready r_sum_ready r_inv_ready top_exp share_ready
            half_share_ready shareT_done shareT_out dbias_done shareT_hi dbias_split acc_ready up_done gate_ready tanh_ready
            up_ready clip_ready tanh_gate act_ready act_hi_ready act_lo_ready down_done added e_stats_ready
            e_mv_ready e_var_ready e_half_ready e_seed e_newton y_done y_stored
            h_half_var l_half_var e_half_var h_centred l_shifted e_shifted dve_passed pool_passed pe_passed"""
        S = {n: sem("m_" + n) for n in names.split()}

        block = ctx.enter_context(nc.Block())

        def rows_of(t, j):
            return t[bass.ds(j * GS, GS)].rearrange("b t d -> t b d")

        def normalise_heads(eng, j):
            eng.wait_ge(S["h_half_var"], j + 1)
            eng.wait_ge(S["h_seed"], j + 1)
            newton_rsqrt(eng, S["h_newton"], NEWTON_OPS * j, h_rstd[:], h_hvar[:], h_tmp[:], three_halves[:])
            heads = y2[:].rearrange("p s (h d) -> p (s h) d", h=MH)
            for k in range(2):
                part = slice(k * PAIRS // 2, (k + 1) * PAIRS // 2)
                eng.tensor_tensor(heads[:, part], heads[:, part],
                                   h_mv[:, part, 0:1].to_broadcast([P, PAIRS // 2, MD]), ALU.subtract)\
                    .then_inc(S["h_centred"], 1)
            eng.wait_ge(S["h_newton"], NEWTON_OPS * (j + 1))
            for k in range(2):
                part = slice(k * PAIRS // 2, (k + 1) * PAIRS // 2)
                eng.wait_ge(S["h_centred"], 2 * j + k + 1)
                eng.tensor_tensor(heads[:, part], heads[:, part],
                                   h_rstd[:, part].unsqueeze(2).to_broadcast([P, PAIRS // 2, MD]), ALU.mult)\
                    .then_inc(S["h_norm"], 1)

        def add_residual(eng, j):
            eng.wait_ge(S["yres_loaded"], 16 * (j + 1))
            for s in range(GS):
                n = j * GS + s
                eng.wait_ge(S["h_norm"], 2 * j + s // 2 + 1)
                eng.tensor_tensor(y2[:, s, :], y2[:, s, :], head_scale[:], ALU.mult).then_inc(S["h_scaled"], 1)
            for s in range(GS):
                n = j * GS + s
                eng.wait_ge(S["h_scaled"], n + 1)
                eng.tensor_tensor(y2[:, s, :], y2[:, s, :], y_res[:, s, :], ALU.add).then_inc(S["z_ready"], 1)

        @block.sync
        def _(sp):
            def load_gates(j):
                sp.dma_start(y_in[:], rows_of(y1, j)).then_inc(S["y_loaded"], 16)
                sp.dma_start(c_in[:], rows_of(ctx_in, j)).then_inc(S["cin_loaded"], 16)

            def load_heads(j):
                sp.dma_start(y_res[:], rows_of(y1, j)).then_inc(S["yres_loaded"], 16)
                for s in range(GS):
                    sp.dma_start(c_one[:, s, :, 0:MD],
                                 ctx_in[bass.ds(j * GS + s, 1)].rearrange("b t (h d) -> (b t) h d", h=MH))\
                        .then_inc(S["c_loaded"], 16)

            load_gates(0)
            sp.dma_start(gate_rows[0:MH, :], w_i).then_inc(S["gate_loaded"], 16)
            sp.dma_start(gate_rows[MH:2 * MH, :], w_f).then_inc(S["gate_loaded"], 16)
            for src, at, n in ((b_r, 0, E), (b_i, E, MH), (b_f, E + MH, MH), (ln_w, E + 2 * MH, DM)):
                sp.dma_start(row[:, at:at + n], src.rearrange("(a n) -> a n", a=1)).then_inc(S["row_loaded"], 16)
            sp.dma_start(r_rows, w_r).then_inc(S["r_loaded"], 16)
            sp.dma_start(gu_bias_rows, b_gu.rearrange("e (b p) -> (e b) p", p=P)).then_inc(S["gbias_loaded"], 16)
            load_heads(0)
            sp.wait_ge(S["consts"], 2)
            for s in range(GS):
                sp.dma_start(d_bias_raw[s * E:(s + 1) * E, s, :], b_d).then_inc(S["dbias_loaded"], 16)

            def load_expert(e):
                if e:
                    sp.wait_ge(S["gu_ready"], e)
                    sp.wait_ge(S["d_ready"], e)
                sp.dma_start(gu_raw, w_gu[e].rearrange("(c p) n -> p c n", p=P)).then_inc(S["gu_loaded"], 16)
                sp.dma_start(d_raw[:], w_d[e].rearrange("(c p) n -> p c n", p=P)).then_inc(S["d_loaded"], 16)

            load_expert(0)
            sp.wait_ge(S["yc_done"], GS)
            load_gates(1)
            for e in range(1, SPLIT_FIRST + 1):
                load_expert(e)

            def group(g):
                sp.wait_ge(S["yc_done"], GS * (g + 2))
                load_gates(g + 2)
                sp.wait_ge(S["z_ready"], GS * (g + 2))
                load_heads(g + 2)
                store(g)

            def store(g):
                sp.wait_ge(S["y_done"], GS * (g + 1))
                sp.dma_start(rows_of(out, g), y_out[:]).then_inc(S["y_stored"], 16)

            sp.wait_ge(S["z_ready"], GS)
            load_heads(1)
            sp.wait_ge(S["yc_done"], GS * 2)
            load_gates(2)
            for e in range(SPLIT_FIRST + 1, E):
                load_expert(e)
            sp.wait_ge(S["z_ready"], GS * 2)
            load_heads(2)
            store(0)
            with sp.Fori(1, GROUPS - 2) as g:
                group(g)
            store(GROUPS - 2)
            store(GROUPS - 1)
            sp.wait_ge(S["y_stored"], 16 * GROUPS)

        @block.gpsimd
        def _(pool):
            pool.memset(d_bias_raw, 0.0).then_inc(S["consts"], 1)
            pool.memset(c_one[:, :, :, MD:MD + 1].rearrange("p s h d -> p (s h d)"), 1.0).then_inc(S["consts"], 1)
            pool.memset(ident[:], 0.0).then_inc(S["consts"], 1)
            pool.memset(ones_to[:], 1.0).then_inc(S["consts"], 1)
            pool.memset(after_b[:], 0.0).then_inc(S["consts"], 1)
            pool.memset(neg_sel_f[:], 0.0).then_inc(S["consts"], 1)
            pool.memset(before[:], 0.0).then_inc(S["consts"], 1)
            pool.memset(behind[:], 0.0).then_inc(S["consts"], 1)
            pool.memset(three_halves[:], 1.5).then_inc(S["consts"], 1)
            pool.wait_ge(S["consts"], 9)
            pool.affine_select(out=ident[:], in_=ident[:], compare_op=ALU.not_equal, fill=1.0, base=0,
                               pattern=[[-1, P]], channel_multiplier=1).then_inc(S["consts"], 1)
            pool.affine_select(out=ones_to[:], in_=ones_to[:], compare_op=ALU.is_ge, fill=0.0, base=0,
                               pattern=[[1, P]], channel_multiplier=-1).then_inc(S["consts"], 1)
            pool.affine_select(out=after_b[:], in_=after_b[:], compare_op=ALU.is_ge, fill=MASKED, base=0,
                               pattern=[[0, MH], [1, P]], channel_multiplier=-1).then_inc(S["consts"], 1)
            pool.affine_select(out=before[:], in_=before[:], compare_op=ALU.is_ge, fill=1.0, base=0,
                               pattern=[[-1, E], [1, E]], channel_multiplier=0).then_inc(S["consts"], 1)
            pool.affine_select(out=behind[:], in_=behind[:], compare_op=ALU.is_ge, fill=1.0, base=0,
                               pattern=[[1, E], [-1, E]], channel_multiplier=0).then_inc(S["consts"], 1)
            for k, at in enumerate((0, 32)):
                pool.affine_select(out=neg_sel_f[:], in_=neg_sel_f[:], compare_op=ALU.not_equal, fill=-1.0,
                                   base=-at, pattern=[[-1, PAIRS]], channel_multiplier=1).then_inc(S["consts"], 1)
                pool.wait_ge(S["consts"], 15 + k)
            pool.wait_ge(S["row_loaded"], 64)
            pool.partition_broadcast(row_all[:], row).then_inc(S["row_ready"], 1)
            pool.wait_ge(S["row_ready"], 1)
            pool.tensor_scalar(head_scale[:], row_all[:, E + 2 * MH:], 1.0, None, ALU.add).then_inc(S["row_ready"], 1)

            def layer_scales(j):
                pool.wait_ge(S["l_half_var"], j + 1)
                pool.wait_ge(S["l_seed"], j + 1)
                newton_rsqrt(pool, S["l_newton"], NEWTON_OPS * j, l_rstd[:], l_hvar[:], l_tmp[:], three_halves[:, 0:GS])
                norm_shift(pool, S["l_shifted"], 2 * j, l_shift[:], l_mv[:, :, 0], l_rstd[:], S["pool_passed"])

            def lower_act(g, e):
                for fb in range(FB):
                    n = (g * E + e) * FB + fb
                    pool.wait_ge(S["act_hi_ready"], n + 1)
                    pool.tensor_tensor(act_lo[:, e % 2, fb, :], tanh[:, fb, :], act_hi[:, e % 2, fb, :].bitcast(F32),
                                       ALU.subtract).then_inc(S["act_lo_ready"], 1)

            def output_scales(g):
                pool.wait_ge(S["e_half_var"], g + 1)
                pool.wait_ge(S["e_seed"], g + 1)
                newton_rsqrt(pool, S["e_newton"], NEWTON_OPS * g, e_rstd[:], e_hvar[:], e_tmp[:], three_halves[:, 0:GS])
                norm_shift(pool, S["e_shifted"], 2 * g, e_shift[:], e_mv[:, :, 0], e_rstd[:], S["pool_passed"])

            def heads_part(j, e):
                if e == GS:
                    normalise_heads(pool, j)
                if e == GS + 1:
                    add_residual(pool, j)
                if e == GS + 2:
                    layer_scales(j)

            def lower_weights(e):
                pool.wait_ge(S["gu_hi_ready"], e + 1)
                pool.tensor_tensor(gu_lo[:, e], gu_raw, gu_hi[:, e].bitcast(F32), ALU.subtract)\
                    .then_inc(S["gu_ready"], 1)
                pool.wait_ge(S["d_hi_ready"], e + 1)
                pool.tensor_tensor(d_lo[:, e], d_raw[:], d_hi[:, e].bitcast(F32), ALU.subtract)\
                    .then_inc(S["d_ready"], 1)

            def body(g, heads=True, split=False):
                for e in range(E):
                    if heads:
                        heads_part(g + 1, e)
                    if split and e + SPLIT_FIRST < E:
                        lower_weights(e + SPLIT_FIRST)
                    lower_act(g, e)
                output_scales(g)

            for e in range(SPLIT_FIRST):
                lower_weights(e)
            layer_scales(0)
            body(0, split=True)
            with pool.Fori(1, GROUPS - 1) as g:
                body(g)
            body(GROUPS - 1, heads=False)

        @block.scalar
        def _(act):
            def take_transposes(j, sequences):
                for s in sequences:
                    act.wait_ge(S["yc_done"], j * GS + s + 1)
                    act.activation(ycT[:, s, :, :].rearrange("p c t -> p (c t)"), pair_bank[s % 2][:], ACT.Copy)\
                        .then_inc(S["yc_out"], 1)

            def gates_mid(j, e):
                if e == T_SLOT:
                    take_transposes(j, range(GS // 2))
                if e == T_SLOT + 1:
                    act.wait_ge(S["rows_done"], j + 1)
                    act.activation(by_row[:], log_bank[0:2 * MH, :], ACT.Copy).then_inc(S["rows_out"], 1)
                if e == T_SLOT + 2:
                    act.wait_ge(S["abs_ready"], j + 1)
                    act.activation(soft[:], abs_f[:], ACT.Exp, scale=-1.0).then_inc(S["gate_exp"], 1)
                    act.wait_ge(S["gate_exp"], j + 1)
                    act.activation(soft[:], soft[:], ACT.Ln, bias=1.0).then_inc(S["soft_ready"], 1)

            def gates_end(j, e):
                if e == T_SLOT:
                    take_transposes(j, range(GS // 2, GS))

            def heads_a(j, e):
                if e == 0:
                    act.wait_ge(S["max_log_ready"], j + 1)
                    act.activation(floor[:], max_log[:], ACT.Exp, scale=-1.0).then_inc(S["floor_exp"], 1)
                if e < GS:
                    n = j * GS + e
                    act.wait_ge(S["log_done"], n + 1)
                    act.wait_ge(S["cmat_ready"], 2 * n)
                    for h in range(MH):
                        act.activation(decay[:, h, :], log_bank[:, h * P:(h + 1) * P], ACT.Exp,
                                       bias=a_tok[:, e * MH + h:e * MH + h + 1]).then_inc(S["decay_ready"], 1)

            def heads_b(j, e):
                if e < GS:
                    n = j * GS + e
                    act.wait_ge(S["av_done"], n + 1)
                    act.wait_ge(S["norm_ready"], n)
                    act.activation(norm_abs[:], head_out[:, :, MD], ACT.Abs).then_inc(S["abs_norm"], 1)
                if e in (GS + 2, GS + 3):
                    act.wait_ge(S["l_newton"], NEWTON_OPS * (j + 1))
                    act.wait_ge(S["l_shifted"], 2 * (j + 1))
                    for s in range(2 * (e - GS - 2), 2 * (e - GS - 1)):
                        act.activation(y2[:, s, :], y2[:, s, :], ACT.Identity, bias=l_shift[:, s:s + 1],
                                       scale=l_rstd[:, s:s + 1]).then_inc(S["y2_ready"], 1)

            def take_gate(g, e, fb):
                n = (g * E + e) * FB + fb
                act.wait_ge(S["up_done"], 2 * n + 1)
                if not (isinstance(g, int) and g == 0 and e == 0):
                    act.wait_ge(S["tanh_gate"], n - FB + 1)
                act.activation(gate[:, fb, :], up_bank[0][:], ACT.Identity,
                               bias=gu_bias[:, e * 2 * FB + fb:e * 2 * FB + fb + 1]).then_inc(S["gate_out"], 1)

            def take_up(g, e, fb):
                n = (g * E + e) * FB + fb
                act.wait_ge(S["up_done"], 2 * n + 2)
                if not (isinstance(g, int) and g == 0 and e == 0):
                    act.wait_ge(S["act_ready"], n - FB + 1)
                act.activation(up[:, fb, :], up_bank[1][:], ACT.Identity,
                               bias=gu_bias[:, e * 2 * FB + FB + fb:e * 2 * FB + FB + fb + 1])\
                    .then_inc(S["up_ready"], 1)

            def gate_tanh(g, e, fb):
                n = (g * E + e) * FB + fb
                act.wait_ge(S["gate_ready"], n + 1)
                if not (isinstance(g, int) and g == 0 and e == 0):
                    act.wait_ge(S["act_lo_ready"], n - FB + 1)
                act.activation(tanh[:, fb, :], gate[:, fb, :], ACT.Tanh, scale=ALPHA / 2)\
                    .then_inc(S["tanh_ready"], 1)

            def upper_act(g, e, fb):
                n = (g * E + e) * FB + fb
                act.wait_ge(S["act_ready"], n + 1)
                act.activation(act_hi[:, e % 2, fb, :], tanh[:, fb, :], ACT.Copy).then_inc(S["act_hi_ready"], 1)

            def transposed_y2(j):
                act.wait_ge(S["yT_done"], j + 1)
                for c in range(KC):
                    act.activation(yT_hi[:, c, :], pair_bank[c][:], ACT.Copy).then_inc(S["yT_hi_ready"], 1)

            def raise_weights(e):
                act.wait_ge(S["gu_loaded"], 16 * (e + 1))
                act.activation(gu_hi[:, e], gu_raw, ACT.Copy).then_inc(S["gu_hi_ready"], 1)
                act.wait_ge(S["d_loaded"], 16 * (e + 1))
                act.activation(d_hi[:, e], d_raw[:], ACT.Copy).then_inc(S["d_hi_ready"], 1)

            def take_logit_rows(j):
                act.wait_ge(S["logit_rows_done"], j + 1)
                act.activation(by_row[:], log_bank[0:E, :], ACT.Copy).then_inc(S["logit_rows_out"], 1)

            def router_exp(j):
                act.wait_ge(S["shifted"], j + 1)
                act.activation(r_exp[:], r_exp[:], ACT.Exp).then_inc(S["r_exp_ready"], 1)

            def output_norm(g):
                act.wait_ge(S["e_newton"], NEWTON_OPS * (g + 1))
                act.wait_ge(S["e_shifted"], 2 * (g + 1))
                if not (isinstance(g, int) and g == 0):
                    act.wait_ge(S["y_stored"], 16 * g)
                for s in range(GS):
                    act.activation(y_out[:, s, :], acc[:, s, :], ACT.Identity, bias=e_shift[:, s:s + 1],
                                   scale=e_rstd[:, s:s + 1]).then_inc(S["y_done"], 1)

            def share_transposed(g):
                act.wait_ge(S["shareT_done"], g + 1)
                for k in range(2):
                    act.activation(share_T[k * GS * E:(k + 1) * GS * E, :], small_bank[0:GS * E, 0:P], ACT.Copy)\
                        .then_inc(S["shareT_hi"], 1)

            gates_mid(0, T_SLOT)
            gates_end(0, T_SLOT)
            act.wait_ge(S["setup_T"], 1)
            act.activation(gate_T[:].rearrange("p c k -> p (c k)"), small_bank[:, 0:3 * KC * 2 * MH], ACT.Copy)\
                .then_inc(S["setup_out"], 1)
            act.activation(gu_bias[:], small_bank[:, 64:64 + E * 2 * FB], ACT.Copy).then_inc(S["setup_out"], 1)
            act.activation(r_hi[:].rearrange("p c e -> p (c e)"), small_bank[:, 128:128 + KC * E], ACT.Copy)\
                .then_inc(S["setup_out"], 1)
            for e in range(T_SLOT + 1, E):
                gates_mid(0, e)
                gates_end(0, e)
            raise_weights(0)
            heads_a(0, 0)
            for e in range(GS):
                if e + 1 < GS:
                    heads_a(0, e + 1)
                heads_b(0, e)
                if e % 2:
                    raise_weights(1 + e // 2)
            for e in range(T_SLOT, E):
                gates_mid(1, e)
                gates_end(1, e)
                if e == T_SLOT + 1:
                    raise_weights(3)
            for e in range(GS, E):
                heads_a(0, e)
                heads_b(0, e)
            transposed_y2(0)
            take_logit_rows(0)
            router_exp(0)

            def body(g, before=True, heads=True, gates=True, split=False):
                for e in range(E):
                    if split and e + SPLIT_FIRST < E:
                        raise_weights(e + SPLIT_FIRST)
                    take_gate(g, e, 0)
                    if heads:
                        heads_a(g + 1, e)
                    take_up(g, e, 0)
                    if gates:
                        gates_mid(g + 2, e)
                    take_gate(g, e, 1)
                    if e == 0:
                        share_transposed(g)
                    gate_tanh(g, e, 0)
                    take_up(g, e, 1)
                    gate_tanh(g, e, 1)
                    if e == 0 and before:
                        output_norm(g - 1)
                    if heads:
                        heads_b(g + 1, e)
                    if gates:
                        gates_end(g + 2, e)
                    upper_act(g, e, 0)
                    upper_act(g, e, 1)
                if heads:
                    transposed_y2(g + 1)
                    take_logit_rows(g + 1)
                    router_exp(g + 1)

            body(0, before=False, split=True)
            with act.Fori(1, GROUPS - 2) as g:
                body(g)
            body(GROUPS - 2, gates=False)
            body(GROUPS - 1, heads=False, gates=False)
            output_norm(GROUPS - 1)

        @block.vector
        def _(dve):
            dve.memset(m_split[:].bitcast(F32), 0.0).then_inc(S["m_lo_ready"], 1)
            dve.wait_ge(S["consts"], 16)
            dve.tensor_copy(neg_sel[:], neg_sel_f[:].unsqueeze(2).to_broadcast([48, PAIRS, P]))\
                .then_inc(S["gate_w_ready"], 1)
            dve.tensor_copy(ident_b[:], ident[:]).then_inc(S["gate_w_ready"], 1)
            dve.wait_ge(S["setup_out"], 3)
            dve.tensor_copy(gate_w[:, 0:KC, :], gate_T[:, 0:KC, :]).then_inc(S["gate_w_ready"], 1)
            dve.tensor_tensor(gate_w[:, KC:2 * KC, :], gate_T[:, KC:2 * KC, :], gate_T[:, 2 * KC:3 * KC, :], ALU.add)\
                .then_inc(S["gate_w_ready"], 1)
            dve.tensor_tensor(r_lo[:].rearrange("p c e -> p (c e)"), small_bank[:, 128:128 + KC * E],
                              r_hi[:].rearrange("p c e -> p (c e)").bitcast(F32), ALU.subtract)\
                .then_inc(S["gate_w_ready"], 1)
            dve.wait_ge(S["row_ready"], 2)

            def seed(var, half_var, mv, half, rstd, k, ready, n):
                dve.wait_ge(S[k + "_mv_ready"], ready)
                dve.tensor_scalar(var, mv, LN_EPS, None, ALU.add).then_inc(S[k + "_var_ready"], 1)
                dve.wait_ge(S[k + "_var_ready"], n + 1)
                dve.tensor_scalar(half_var, var, 0.5, None, ALU.mult).then_inc(S[k + "_half_var"], 1)
                dve.tensor_scalar(half, var.bitcast(I32), 1, None, ALU.logical_shift_right)\
                    .then_inc(S[k + "_half_ready"], 1)
                dve.wait_ge(S[k + "_half_ready"], n + 1)
                dve.tensor_scalar(rstd.bitcast(I32), half, -1.0, float(RSQRT_SEED), ALU.mult, ALU.add)\
                    .then_inc(S[k + "_seed"], 1)

            def gates_mid(j, e):
                if e == T_SLOT + 2:
                    dve.wait_ge(S["soft_ready"], j + 1)
                    dve.scalar_tensor_tensor(log_f[:], gates[:, :, MH:], 0.0, soft[:], ALU.min, ALU.subtract)\
                        .then_inc(S["log_f_ready"], 1)
                if e == T_SLOT + 3:
                    dve.wait_ge(S["cum_done"], j + 1)
                    dve.tensor_copy(cum_f[:], small_bank[:, 0:PAIRS]).then_inc(S["cum_ready"], 1)
                    dve.wait_ge(S["cum_ready"], j + 1)
                    dve.tensor_tensor(a_tok[:].rearrange("p (s h) -> p s h", s=GS), gates[:, :, 0:MH],
                                      cum_f[:].rearrange("p (s h) -> p s h", s=GS), ALU.subtract)\
                        .then_inc(S["a_ready"], 1)

            def gates_end(j, e):
                if e == T_SLOT + 1:
                    dve.wait_ge(S["gates_done"], j + 1)
                    dve.tensor_tensor(gates[:], gates_ps, gate_bias.unsqueeze(1).to_broadcast([P, GS, 2 * MH]), ALU.add)\
                        .then_inc(S["gates_ready"], 1)
                    dve.wait_ge(S["gates_ready"], j + 1)
                    dve.scalar_tensor_tensor(abs_f[:], gates[:, :, MH:], -1.0, gates[:, :, MH:], ALU.mult, ALU.max)\
                        .then_inc(S["abs_ready"], 1)
                if e == T_SLOT + 3:
                    dve.wait_ge(S["aT_done"], j + 1)
                    dve.tensor_copy(a_rows[:], small_bank[0:PAIRS, 0:P]).then_inc(S["a_rows_ready"], 1)
                    dve.wait_ge(S["a_rows_ready"], j + 1)
                    dve.tensor_tensor_scan(m_rows[:], a_rows[:], a_rows[:], MASKED, ALU.max, ALU.max)\
                        .then_inc(S["m_ready"], 1)
                    dve.wait_ge(S["m_ready"], j + 1)
                    dve.tensor_copy(m_split[0:PAIRS, :], m_rows[:]).then_inc(S["m_hi_ready"], 1)
                    dve.wait_ge(S["m_hi_ready"], j + 1)
                    dve.tensor_tensor(m_split[32:32 + PAIRS, :], m_rows[:], m_split[0:PAIRS, :].bitcast(F32),
                                      ALU.subtract).then_inc(S["m_lo_ready"], 1)

            def largest_log(j):
                dve.wait_ge(S["mT_done"], j + 1)
                dve.tensor_tensor(max_log[:], small_bank[:, 0:PAIRS], cum_f[:], ALU.add)\
                    .then_inc(S["max_log_ready"], 1)

            def heads_a(j, e):
                if e < GS:
                    n = j * GS + e
                    dve.wait_ge(S["qk_done"], n + 1)
                    dve.wait_ge(S["decay_ready"], MH * (n + 1))
                    dve.wait_ge(S["av_done"], n)
                    for i in range(2):
                        dve.scalar_tensor_tensor(cmat[:, i::2, :],
                                                 pair_bank[i][:, 0:2 * P].rearrange("p (h t) -> p h t", h=2),
                                                 QK_SCALE, decay[:, i::2, :], ALU.mult, ALU.mult)\
                            .then_inc(S["cmat_ready"], 1)

            def heads_b(j, e):
                if e < GS:
                    s = e
                    n = j * GS + s
                    if s == 0:
                        dve.wait_ge(S["floor_exp"], j + 1)
                        dve.tensor_scalar(floor[:], floor[:], NORM_EPS, None, ALU.add).then_inc(S["floor_ready"], 1)
                        dve.wait_ge(S["floor_ready"], j + 1)
                    dve.wait_ge(S["abs_norm"], n + 1)
                    dve.scalar_tensor_tensor(norm_max[:], norm_abs[:], NORM_EPS, floor[:, s * MH:(s + 1) * MH],
                                             ALU.add, ALU.max).then_inc(S["norm_ready"], 1)
                    dve.wait_ge(S["norm_ready"], n + 1)
                    dve.reciprocal(norm_inv[:], norm_max[:]).then_inc(S["inv_ready"], 1)
                    dve.wait_ge(S["inv_ready"], n + 1)
                    if s == 0:
                        dve.wait_ge(S["acc_ready"], 2 * j)
                    dve.tensor_tensor(y2[:, s, :].rearrange("p (h d) -> p h d", h=MH), head_out[:, :, 0:MD],
                                      norm_inv[:].unsqueeze(2).to_broadcast([P, MH, MD]), ALU.mult)\
                        .then_inc(S["h_ready"], 1)
                    dve.wait_ge(S["h_ready"], n + 1)
                    for h in range(MH):
                        dve.bn_stats(h_stats[:, h, :], y2[:, s, h * MD:(h + 1) * MD]).then_inc(S["h_stats_ready"], 1)
                    dve.wait_ge(S["h_stats_ready"], MH * (n + 1))
                    stand_apart(dve, S["dve_passed"])
                    for h in range(MH):
                        dve.bn_aggr(h_mv[:, s * MH + h, :], h_stats[:, h, :]).then_inc(S["h_mv_ready"], 1)
                if e == GS - 1:
                    seed(h_var[:], h_hvar[:], h_mv[:, :, 1], h_half[:], h_rstd[:], "h", PAIRS * (j + 1), j)
                if e == GS + 1:
                    for s in range(GS):
                        dve.wait_ge(S["z_ready"], GS * j + s + 1)
                        dve.bn_stats(l_stats[:, s, :], y2[:, s, :]).then_inc(S["l_stats_ready"], 1)
                    dve.wait_ge(S["l_stats_ready"], GS * (j + 1))
                    stand_apart(dve, S["dve_passed"])
                    for s in range(GS):
                        dve.bn_aggr(l_mv[:, s, :], l_stats[:, s, :]).then_inc(S["l_mv_ready"], 1)
                    seed(l_var[:], l_hvar[:], l_mv[:, :, 1], l_half[:], l_rstd[:], "l", GS * (j + 1), j)

            def clip_gate(g, e, fb):
                n = (g * E + e) * FB + fb
                dve.wait_ge(S["gate_out"], n + 1)
                dve.tensor_scalar(gate[:, fb, :], gate[:, fb, :], LIMIT, None, ALU.min).then_inc(S["gate_ready"], 1)

            def clip_up(g, e, fb):
                n = (g * E + e) * FB + fb
                dve.wait_ge(S["up_ready"], n + 1)
                dve.tensor_scalar(up[:, fb, :], up[:, fb, :], LIMIT, -LIMIT, ALU.min, ALU.max)\
                    .then_inc(S["clip_ready"], 1)

            def activate(g, e, fb):
                n = (g * E + e) * FB + fb
                dve.wait_ge(S["tanh_ready"], n + 1)
                dve.scalar_tensor_tensor(tanh[:, fb, :], tanh[:, fb, :], 1.0, gate[:, fb, :], ALU.add, ALU.mult)\
                    .then_inc(S["tanh_gate"], 1)
                dve.wait_ge(S["clip_ready"], n + 1)
                dve.wait_ge(S["tanh_gate"], n + 1)
                dve.scalar_tensor_tensor(tanh[:, fb, :], up[:, fb, :], 1.0, tanh[:, fb, :], ALU.add, ALU.mult)\
                    .then_inc(S["act_ready"], 1)

            def add_expert(g, e):
                for i in range(2):
                    dve.wait_ge(S["down_done"], 2 * (g * E + e) + i + 1)
                    for s in (2 * i, 2 * i + 1):
                        if e == 0:
                            dve.wait_ge(S["acc_ready"], 2 * (g + 1))
                        else:
                            dve.wait_ge(S["added"], GS * (g * E + e - 1) + s + 1)
                        dve.scalar_tensor_tensor(acc[:, s, :], down_bank[i][:, (s % 2) * DM:(s % 2 + 1) * DM],
                                                 half_share[:, s, e:e + 1], acc[:, s, :], ALU.mult, ALU.add)\
                            .then_inc(S["added"], 1)

            def lower_shares(g):
                dve.wait_ge(S["shareT_hi"], 2 * (g + 1))
                dve.tensor_tensor(share_T[2 * GS * E:3 * GS * E, :], small_bank[0:GS * E, 0:P],
                                  share_T[0:GS * E, :].bitcast(F32), ALU.subtract).then_inc(S["shareT_out"], 1)

            def split_biases():
                dve.wait_ge(S["dbias_loaded"], 16 * GS)
                for k in (0, 2):
                    dve.tensor_copy(d_bias[k * GS * E:(k + 1) * GS * E], d_bias_raw).then_inc(S["dbias_split"], 1)
                dve.wait_ge(S["dbias_split"], 1)
                dve.tensor_tensor(d_bias[GS * E:2 * GS * E], d_bias_raw, d_bias[0:GS * E].bitcast(F32), ALU.subtract)\
                    .then_inc(S["dbias_split"], 1)

            def start_acc(g):
                dve.wait_ge(S["dbias_done"], g + 1)
                dve.wait_ge(S["y_done"], GS * g)
                for i in range(2):
                    dve.tensor_tensor(acc[:, 2 * i:2 * i + 2, :].rearrange("p s d -> p (s d)"), down_bank[i][:],
                                      y2[:, 2 * i:2 * i + 2, :].rearrange("p s d -> p (s d)"), ALU.add)\
                        .then_inc(S["acc_ready"], 1)

            def output_stats(g):
                for s in range(GS):
                    dve.wait_ge(S["added"], GS * (g * E + E - 1) + s + 1)
                    dve.bn_stats(e_stats[:, s, :], acc[:, s, :]).then_inc(S["e_stats_ready"], 1)
                dve.wait_ge(S["e_stats_ready"], GS * (g + 1))
                stand_apart(dve, S["dve_passed"])
                for s in range(GS):
                    dve.bn_aggr(e_mv[:, s, :], e_stats[:, s, :]).then_inc(S["e_mv_ready"], 1)
                seed(e_var[:], e_hvar[:], e_mv[:, :, 1], e_half[:], e_rstd[:], "e", GS * (g + 1), g)

            def lower_y2(j):
                for c in range(KC):
                    dve.wait_ge(S["yT_hi_ready"], KC * j + c + 1)
                    dve.tensor_tensor(yT_lo[:, c, :], pair_bank[c][:], yT_hi[:, c, :].bitcast(F32), ALU.subtract)\
                        .then_inc(S["yT_lo_ready"], 1)

            def route(j):
                dve.wait_ge(S["logits_done"], j + 1)
                dve.tensor_tensor(logits[:], logits_ps, row_all[:, 0:E].unsqueeze(1).to_broadcast([P, GS, E]), ALU.add)\
                    .then_inc(S["logits_ready"], 1)
                dve.wait_ge(S["logits_ready"], j + 1)
                dve.tensor_reduce(peak[:], logits[:], AX.X, ALU.max).then_inc(S["peak_ready"], 1)
                dve.wait_ge(S["peak_ready"], j + 1)
                dve.tensor_tensor(r_exp[:], logits[:], peak[:].unsqueeze(2).to_broadcast([P, GS, E]), ALU.subtract)\
                    .then_inc(S["shifted"], 1)
                this = logits[:].unsqueeze(3).to_broadcast([P, GS, E, E])
                other = logits[:].unsqueeze(2).to_broadcast([P, GS, E, E])
                grid = "p (s k) e -> p s k e"
                dve.tensor_tensor(beats[:].rearrange(grid, s=GS), other, this, ALU.is_gt).then_inc(S["beats_raw"], 1)
                dve.tensor_tensor(ties[:].rearrange(grid, s=GS), other, this, ALU.is_ge).then_inc(S["ties_raw"], 1)
                dve.wait_ge(S["beats_raw"], j + 1)
                dve.tensor_tensor(beats[:].rearrange(grid, s=GS), beats[:].rearrange(grid, s=GS),
                                  behind[:].unsqueeze(1).to_broadcast([P, GS, E, E]), ALU.mult)\
                    .then_inc(S["beats_cut"], 1)
                dve.wait_ge(S["ties_raw"], j + 1)
                dve.tensor_tensor(ties[:].rearrange(grid, s=GS), ties[:].rearrange(grid, s=GS),
                                  before[:].unsqueeze(1).to_broadcast([P, GS, E, E]), ALU.mult)\
                    .then_inc(S["ties_cut"], 1)
                dve.wait_ge(S["beats_cut"], j + 1)
                dve.wait_ge(S["ties_cut"], j + 1)
                dve.tensor_tensor(beats[:], beats[:], ties[:], ALU.add).then_inc(S["beats_sum"], 1)
                dve.wait_ge(S["beats_sum"], j + 1)
                dve.tensor_reduce(rank[:], beats[:], AX.X, ALU.add).then_inc(S["rank_ready"], 1)
                dve.wait_ge(S["rank_ready"], j + 1)
                dve.tensor_scalar(top[:], rank[:], 2.0, None, ALU.is_lt).then_inc(S["top_ready"], 1)
                dve.wait_ge(S["r_exp_ready"], j + 1)
                dve.tensor_reduce(r_sum[:], r_exp[:], AX.X, ALU.add).then_inc(S["r_sum_ready"], 1)
                dve.wait_ge(S["r_sum_ready"], j + 1)
                dve.reciprocal(r_inv[:], r_sum[:]).then_inc(S["r_inv_ready"], 1)
                dve.wait_ge(S["top_ready"], j + 1)
                dve.tensor_tensor(r_exp[:].rearrange("p s e -> p (s e)"), r_exp[:].rearrange("p s e -> p (s e)"), top[:],
                                  ALU.mult).then_inc(S["top_exp"], 1)
                dve.wait_ge(S["top_exp"], j + 1)
                dve.wait_ge(S["r_inv_ready"], j + 1)
                dve.tensor_tensor(share[:], r_exp[:], r_inv[:].unsqueeze(2).to_broadcast([P, GS, E]), ALU.mult)\
                    .then_inc(S["share_ready"], 1)
                dve.wait_ge(S["share_ready"], j + 1)
                dve.tensor_scalar(half_share[:], share[:], 0.5, None, ALU.mult).then_inc(S["half_share_ready"], 1)

            for e in range(T_SLOT, E):
                gates_mid(0, e)
                gates_end(0, e)
            largest_log(0)
            for e in range(GS):
                heads_a(0, e)
                heads_b(0, e)
            dve.wait_ge(S["row_ready"], 2)
            dve.wait_ge(S["consts"], 16)
            normalise_heads(dve, 0)
            gates_mid(1, T_SLOT + 1)
            gates_end(1, T_SLOT + 1)
            add_residual(dve, 0)
            gates_mid(1, T_SLOT + 2)
            gates_end(1, T_SLOT + 2)
            heads_b(0, GS + 1)
            gates_mid(1, T_SLOT + 3)
            gates_end(1, T_SLOT + 3)
            largest_log(1)
            split_biases()
            lower_y2(0)
            route(0)

            def body(g, heads=True, gates=True):
                for e in range(E):
                    if heads:
                        heads_a(g + 1, e)
                    if e == 0:
                        lower_shares(g)
                    clip_gate(g, e, 0)
                    clip_up(g, e, 0)
                    if gates:
                        gates_mid(g + 2, e)
                    clip_gate(g, e, 1)
                    activate(g, e, 0)
                    clip_up(g, e, 1)
                    activate(g, e, 1)
                    if e == 0:
                        dve.wait_ge(S["half_share_ready"], g + 1)
                        start_acc(g)
                    if heads and e < GS:
                        heads_b(g + 1, e)
                    if gates:
                        gates_end(g + 2, e)
                    if e:
                        add_expert(g, e - 1)
                    if heads and e >= GS:
                        heads_b(g + 1, e)
                if heads:
                    lower_y2(g + 1)
                if gates:
                    largest_log(g + 2)
                add_expert(g, E - 1)
                output_stats(g)
                if heads:
                    route(g + 1)

            body(0)
            with dve.Fori(1, GROUPS - 2) as g:
                body(g)
            body(GROUPS - 2, gates=False)
            body(GROUPS - 1, heads=False, gates=False)

        @block.tensor
        def _(pe):
            pe.wait_ge(S["consts"], 16)

            def setup():
                pe.wait_ge(S["gate_loaded"], 32)
                pe.wait_ge(S["gbias_loaded"], 16)
                pe.wait_ge(S["r_loaded"], 16)
                for c in range(3 * KC):
                    pe.transpose(small_bank[:, c * 2 * MH:(c + 1) * 2 * MH], gate_rows[:, c * P:(c + 1) * P],
                                 ident[0:2 * MH, 0:2 * MH])
                pe.transpose(small_bank[:, 64:64 + E * 2 * FB], gu_bias_rows, ident[0:E * 2 * FB, 0:E * 2 * FB])
                for c in range(KC):
                    last_mm = pe.transpose(small_bank[:, 128 + c * E:128 + (c + 1) * E], r_rows[:, c * P:(c + 1) * P],
                                           ident[0:E, 0:E])
                last_mm.then_inc(S["setup_T"], 1)
                pe.wait_ge(S["gate_w_ready"], 5)

            def transpose_inputs(j, sequences):
                for s in sequences:
                    if s >= 2:
                        pe.wait_ge(S["yc_out"], GS * j + s - 1)
                    for c in range(KC):
                        pe.transpose(pair_bank[s % 2][:, c * P:(c + 1) * P], y_in[:, s, c * P:(c + 1) * P], ident[:])
                    for c in range(KC):
                        last = pe.transpose(pair_bank[s % 2][:, (KC + c) * P:(KC + c + 1) * P],
                                            c_in[:, s, c * P:(c + 1) * P], ident[:])
                    last.then_inc(S["yc_done"], 1)

            def gates_mid(j, e):
                if e == T_SLOT:
                    pe.wait_ge(S["y_loaded"], 16 * (j + 1))
                    pe.wait_ge(S["cin_loaded"], 16 * (j + 1))
                    pe.wait_ge(S["cmat_ready"], 2 * GS * j)
                    transpose_inputs(j, range(GS // 2))
                if e == T_SLOT + 1:
                    pe.wait_ge(S["yc_out"], GS * (j + 1))
                    pe.wait_ge(S["decay_ready"], MH * GS * j)
                    for c in range(2 * KC):
                        last = pe.matmul(log_bank[0:2 * MH, :].rearrange("p (s t) -> p s t", s=GS), gate_w[:, c, :],
                                         ycT[:, :, c, :], start=(c == 0), stop=(c == 2 * KC - 1))
                    last.then_inc(S["rows_done"], 1)
                if e == T_SLOT + 3:
                    pe.wait_ge(S["log_f_ready"], j + 1)
                    pe.matmul(small_bank[:, 0:PAIRS], ones_to[:], log_f[:].rearrange("p s h -> p (s h)"),
                              start=True, stop=True).then_inc(S["cum_done"], 1)

            def gates_end(j, e):
                if e == T_SLOT:
                    transpose_inputs(j, range(GS // 2, GS))
                if e == T_SLOT + 1:
                    pe.wait_ge(S["rows_out"], j + 1)
                    pe.wait_ge(S["h_ready"], GS * j)
                    stand_apart(pe, S["pe_passed"])
                    for s in range(GS):
                        last = pe.transpose(gates_ps[:, s, :], by_row[:, s * P:(s + 1) * P],
                                            ident[0:2 * MH, 0:2 * MH])
                    last.then_inc(S["gates_done"], 1)
                if e == T_SLOT + 3:
                    pe.wait_ge(S["a_ready"], j + 1)
                    pe.transpose(small_bank[0:PAIRS, 0:P], a_tok[:], ident[:]).then_inc(S["aT_done"], 1)

            def transpose_maxima(j):
                pe.wait_ge(S["m_lo_ready"], j + 2)
                stand_apart(pe, S["pe_passed"])
                pe.transpose(small_bank[:, 0:PAIRS], m_rows[:], ident[0:PAIRS, 0:PAIRS]).then_inc(S["mT_done"], 1)

            def log_decays(j, s):
                n = j * GS + s
                if s == 0:
                    pe.wait_ge(S["m_lo_ready"], j + 2)
                    if isinstance(j, int) and j == 0:
                        pe.wait_ge(S["rows_out"], 1)
                    else:
                        pe.wait_ge(S["logit_rows_out"], j)
                pe.wait_ge(S["decay_ready"], MH * n)
                pe.matmul(log_bank[:], ident_b[:], after_b[:].rearrange("p h t -> p (h t)"), start=True,
                          stop=False, skip_group_check=True)
                for h in range(MH):
                    last = pe.matmul(log_bank[:, h * P:(h + 1) * P], neg_sel[:, s * MH + h, :], m_split[:],
                                     start=False, stop=(h == MH - 1), skip_group_check=True)
                last.then_inc(S["log_done"], 1)

            def keys_queries(j, s):
                n = j * GS + s
                if s == 0:
                    pe.wait_ge(S["yc_out"], GS * (j + 1))
                    pe.wait_ge(S["yT_lo_ready"], KC * j)
                pe.wait_ge(S["cmat_ready"], 2 * n)
                for h in range(MH):
                    rows = slice(MD * (h % 2), MD * (h % 2 + 1))
                    last = pe.matmul(pair_bank[h % 2][:, (h // 2) * P:(h // 2 + 1) * P],
                                     ycT[rows, s, KC + h // 2, :], ycT[rows, s, h // 2, :], start=True, stop=True)
                last.then_inc(S["qk_done"], 1)

            def heads_a(j, e):
                if e == 0:
                    keys_queries(j, 0)
                    transpose_logits(j - 1, True)
                    log_decays(j, 0)
                elif e < GS:
                    log_decays(j, e)
                    keys_queries(j, e)

            def heads_b(j, e):
                if e < GS:
                    s = e
                    n = j * GS + s
                    pe.wait_ge(S["cmat_ready"], 2 * (n + 1))
                    if s == 0:
                        pe.wait_ge(S["c_loaded"], 16 * GS * (j + 1))
                        if isinstance(j, int) and j == 0:
                            pe.wait_ge(S["max_log_ready"], 1)
                        else:
                            pe.wait_ge(S["shareT_out"], j)
                    pe.wait_ge(S["h_ready"], n)
                    for h in range(MH):
                        last = pe.matmul(head_out[:, h, :], cmat[:, h, :], c_one[:, s, h, :], start=True, stop=True)
                    last.then_inc(S["av_done"], 1)

            def transpose_y2(j, gates):
                pe.wait_ge(S["y2_ready"], GS * (j + 1))
                if gates:
                    pe.wait_ge(S["yc_out"], GS * (j + 2))
                for c in range(KC):
                    for s in range(GS):
                        last = pe.transpose(pair_bank[c][:, s * P:(s + 1) * P], y2[:, s, c * P:(c + 1) * P], ident[:])
                last.then_inc(S["yT_done"], 1)

            def route(j, gates):
                pe.wait_ge(S["yT_lo_ready"], KC * (j + 1))
                pe.wait_ge(S["decay_ready"], MH * GS * (j + 1))
                if gates:
                    pe.wait_ge(S["rows_out"], j + 2)
                k = 0
                for w, yT in ((r_hi, yT_hi), (r_lo, yT_hi), (r_hi, yT_lo)):
                    for c in range(KC):
                        last = pe.matmul(log_bank[0:E, :], w[:, c, :], yT[:, c, :], start=(k == 0),
                                         stop=(k == 3 * KC - 1))
                        k += 1
                last.then_inc(S["logit_rows_done"], 1)

            def transpose_logits(j, heads):
                pe.wait_ge(S["logit_rows_out"], j + 1)
                pe.wait_ge(S["max_log_ready"], j + (2 if heads else 1))
                stand_apart(pe, S["pe_passed"])
                for s in range(GS):
                    last = pe.transpose(logits_ps[:, s, :], by_row[:, s * P:(s + 1) * P], ident[0:E, 0:E])
                last.then_inc(S["logits_done"], 1)

            def up_projections(g, e, gates):
                for fb in range(FB):
                    if gates and fb == 1:
                        gates_mid(g + 2, e)
                    for i in range(2):
                        if e == 0 and fb == 1 and i == 1:
                            transpose_shares(g)
                        n = (g * E + e) * FB + fb
                        pe.wait_ge(S["gate_out" if i == 0 else "up_ready"], n)
                        col = i * FI + fb * P
                        k = 0
                        for w, yT in ((gu_hi, yT_hi), (gu_lo, yT_hi), (gu_hi, yT_lo)):
                            for c in range(KC):
                                last = pe.matmul(up_bank[i][:], w[:, e, c, col:col + P], yT[:, c, :],
                                                 start=(k == 0), stop=(k == 3 * KC - 1))
                                k += 1
                        last.then_inc(S["up_done"], 1)

            def down_projection(g, e):
                for i in range(2):
                    if i == 0:
                        pe.wait_ge(S["act_lo_ready"], FB * (g * E + e + 1))
                    if e == 0:
                        pe.wait_ge(S["acc_ready"], 2 * (g + 1))
                    else:
                        pe.wait_ge(S["added"], GS * (g * E + e - 1) + 2 * i + 2)
                    for s in (2 * i, 2 * i + 1):
                        toks = slice(s * P, (s + 1) * P)
                        k = 0
                        for a, w in ((act_hi, d_hi), (act_hi, d_lo), (act_lo, d_hi)):
                            for fb in range(FB):
                                last = pe.matmul(down_bank[i][:, (s % 2) * DM:(s % 2 + 1) * DM],
                                                 a[:, e % 2, fb, toks], w[:, e, fb, :], start=(k == 0),
                                                 stop=(k == 3 * FB - 1))
                                k += 1
                    last.then_inc(S["down_done"], 1)

            def transpose_shares(g):
                pe.wait_ge(S["share_ready"], g + 1)
                pe.wait_ge(S["logits_ready"], g + 1)
                pe.transpose(small_bank[0:GS * E, 0:P], share[:].rearrange("p s e -> p (s e)"), ident[:])\
                    .then_inc(S["shareT_done"], 1)

            def bias_shares(g):
                pe.wait_ge(S["shareT_out"], g + 1)
                pe.wait_ge(S["added"], GS * E * g)
                for s in range(GS):
                    last = pe.matmul(down_bank[s // 2][:, (s % 2) * DM:(s % 2 + 1) * DM], share_T[:], d_bias[:, s, :],
                                     start=True, stop=True)
                last.then_inc(S["dbias_done"], 1)

            gates_mid(0, T_SLOT)
            gates_end(0, T_SLOT)
            setup()
            for e in range(T_SLOT + 1, E):
                gates_mid(0, e)
                gates_end(0, e)
            transpose_maxima(0)
            log_decays(0, 0)
            for s in range(GS):
                keys_queries(0, s)
                if s + 1 < GS:
                    log_decays(0, s + 1)
                heads_b(0, s)
            for e in range(T_SLOT, E):
                gates_mid(1, e)
                gates_end(1, e)
            transpose_maxima(1)
            pe.wait_ge(S["dbias_split"], 3)
            transpose_y2(0, gates=True)
            route(0, gates=True)

            def body(g, heads=True, gates=True, split=False):
                if not heads:
                    transpose_logits(g, False)
                for e in range(E):
                    if heads:
                        heads_a(g + 1, e)
                    if split:
                        pe.wait_ge(S["gu_ready"], e + 1)
                        pe.wait_ge(S["d_ready"], e + 1)
                    up_projections(g, e, gates)
                    if e == 0:
                        bias_shares(g)
                    if heads:
                        heads_b(g + 1, e)
                    if gates:
                        gates_end(g + 2, e)
                    if e:
                        down_projection(g, e - 1)
                if heads:
                    transpose_y2(g + 1, gates)
                if gates:
                    transpose_maxima(g + 2)
                down_projection(g, E - 1)
                if heads:
                    route(g + 1, gates)

            body(0, split=True)
            with pe.Fori(1, GROUPS - 2) as g:
                body(g)
            body(GROUPS - 2, gates=False)
            body(GROUPS - 1, heads=False, gates=False)


def decoder(nc, ins, out):
    y1 = nc.dram_tensor("y1_dram", [NSEQ, P, DM], F32, kind="Internal").ap()
    attention(nc, y1, ins["x"], *(ins["L0_attn_" + n] for n in ("wq", "wkv", "wo", "bo")))
    mlstm_and_experts(nc, out, y1, ins["ctx_1024"],
                      *(ins["L0_xattn_" + n] for n in ("w_igate", "b_igate", "w_fgate", "b_fgate", "ln_weight")),
                      *(ins["L0_ffn_" + n] for n in ("router_weight", "router_bias", "gate_up_proj",
                                                     "gate_up_bias", "down_proj", "down_bias")))


_INS = ['x', 'ctx_1024', 'L0_attn_wq', 'L0_attn_wkv', 'L0_attn_wo', 'L0_attn_bo', 'L0_xattn_w_igate',
        'L0_xattn_b_igate', 'L0_xattn_w_fgate', 'L0_xattn_b_fgate', 'L0_xattn_ln_weight',
        'L0_ffn_router_weight', 'L0_ffn_router_bias', 'L0_ffn_gate_up_proj', 'L0_ffn_gate_up_bias',
        'L0_ffn_down_proj', 'L0_ffn_down_bias']
_OUTS = [((32, 128, 256), 'float32')]


def kernel(**inputs):
    import numpy as _np
    import concourse.bacc as _bacc
    from concourse import mybir as _mybir
    from concourse.bass_utils import run_bass_kernel_spmd as _run

    nc = _bacc.Bacc("TRN2", target_bir_lowering=False, num_devices=1)
    arrays, aps = {}, {}
    for name in _INS:
        a = _np.ascontiguousarray(inputs[name])
        arrays[f"in_{name}_dram"] = a
        aps[name] = nc.dram_tensor(f"in_{name}_dram", a.shape, _mybir.dt.from_np(a.dtype), kind="ExternalInput").ap()
    shape, dtype = _OUTS[0]
    out = nc.dram_tensor("out_0_dram", shape, _mybir.dt.from_np(_np.dtype(dtype)), kind="ExternalOutput").ap()
    decoder(nc, aps, out)
    r = _run(nc, [arrays], core_ids=[0])
    return r.results[0]["out_0_dram"]
```
